# Optimizing a Trainium2 kernel written in Bass

```python
import numpy as np
import jax
import jax.numpy as jnp

def _softmax(x, axis=-1):
    return jax.nn.softmax(x, axis=axis)

def _gelu(x):
    return jax.nn.gelu(x, approximate=True)

def _silu(x):
    return jax.nn.silu(x)

def _sigmoid(x):
    return jax.nn.sigmoid(x)

def _layernorm(x, axis=-1, eps=1e-05):
    m = jnp.mean(x, axis=axis, keepdims=True)
    v = jnp.var(x, axis=axis, keepdims=True)
    return (x - m) / jnp.sqrt(v + eps)

def _scatter_add(tgt, idx, src, axis=0):
    return tgt.at[idx].add(src)

def _segment_sum(src, seg, n):
    return jax.ops.segment_sum(src, seg, n)
kernel_name = 'mk_macaron_d2_jaxref_r8_fb8bf7'

def setup_inputs(seed: int=0):
    np.random.seed(seed)
    _w = jnp.asarray

    def _L0_attn_setup():
        import jax, jax.numpy as jnp
        import numpy as np
        B, S, D, H = (2, 256, 128, 16)
        HD = D // H
        key = jax.random.key(seed)
        ks = jax.random.split(key, 5)
        return {'x': jax.random.normal(ks[0], (B, S, D), dtype=jnp.float32), 'qkv_w': jax.random.normal(ks[1], (3 * D, D), dtype=jnp.float32) * (1.0 / np.sqrt(D)), 'qkv_b': jax.random.normal(ks[2], (3 * D,), dtype=jnp.float32) * 0.02, 'proj_w': jax.random.normal(ks[3], (D, D), dtype=jnp.float32) * (1.0 / np.sqrt(D)), 'proj_b': jax.random.normal(ks[4], (D,), dtype=jnp.float32) * 0.02}
    _L0_attn_in = _L0_attn_setup()

    def _L0_ffn_setup():
        import jax, jax.numpy as jnp
        import numpy as np
        D = 128
        H = 128
        E = 8
        K = 2
        I = 2 * 128
        ROUTE_SCALE = 1.0
        key = jax.random.key(seed)
        ks = jax.random.split(key, 12)
        s = lambda *sh: 1.0 / np.sqrt(sh[-1])
        return {'x': jax.random.normal(ks[0], (1, 256, D), jnp.float32), 'gate_w': jax.random.normal(ks[1], (E, D), jnp.float32) * s(E, D), 'w1': jax.random.normal(ks[2], (E, H, D), jnp.float32) * s(H, D), 'b1': jax.random.normal(ks[3], (E, H), jnp.float32) * 0.01, 'w2': jax.random.normal(ks[4], (E, D, H), jnp.float32) * s(D, H), 'b2': jax.random.normal(ks[5], (E, D), jnp.float32) * 0.01, 'w3': jax.random.normal(ks[6], (E, H, D), jnp.float32) * s(H, D), 'b3': jax.random.normal(ks[7], (E, H), jnp.float32) * 0.01, 'sw1': jax.random.normal(ks[8], (I, D), jnp.float32) * s(I, D), 'sw2': jax.random.normal(ks[9], (I, D), jnp.float32) * s(I, D), 'sw3': jax.random.normal(ks[10], (D, I), jnp.float32) * s(D, I)}
    _L0_ffn_in = _L0_ffn_setup()

    def _L1_attn_setup():
        import jax, jax.numpy as jnp
        import numpy as np
        B, T, D, H, FFN = (2, 256, 128, 16, 512)
        K = D // H
        EPS = 1e-06
        LN_EPS = 1e-05
        LAM_MIN = 1e-08

        def _ln(x, w, b):
            m = x.mean(-1, keepdims=True)
            v = ((x - m) ** 2).mean(-1, keepdims=True)
            return (x - m) * jax.lax.rsqrt(v + LN_EPS) * w + b

        def _lion(phi_q, phi_k, v, lam):
            b, h, t, kk = phi_q.shape
            kv = v.shape[-1]
            to_t = lambda a: a.transpose(2, 0, 1, 3)
            qt, kt, vt, lt = (to_t(phi_q), to_t(phi_k), to_t(v), to_t(lam))
            S0 = jnp.zeros((b, h, kk, kv), phi_q.dtype)

            def fwd(S, inp):
                q_t, k_t, v_t, l_t = inp
                S = S * l_t[..., None] + k_t[..., None] * v_t[..., None, :]
                return (S, jnp.einsum('bhk,bhkv->bhv', q_t, S))
            _, out_f = jax.lax.scan(fwd, S0, (qt, kt, vt, lt))
            q_shift = jnp.concatenate([qt[:1], qt[:-1]], axis=0)

            def bwd(R, inp):
                qs_t, k_t, v_t, l_t = inp
                R = l_t[..., None] * (k_t[..., None] * v_t[..., None, :] + R)
                return (R, jnp.einsum('bhk,bhkv->bhv', qs_t, R))
            _, out_b = jax.lax.scan(bwd, S0, (q_shift, kt, vt, lt), reverse=True)
            out_b = jnp.concatenate([out_b[1:], jnp.zeros_like(out_b[:1])], axis=0)
            return (out_f + out_b).transpose(1, 2, 0, 3)
        key = jax.random.key(seed)
        ks = jax.random.split(key, 12)
        s = 0.02
        w = lambda k, shp: jax.random.normal(k, shp, jnp.float32) * s
        return {'x': jax.random.normal(ks[0], (B, T, D), jnp.float32), 'q_w': w(ks[1], (D, D)), 'q_b': jnp.zeros((D,), jnp.float32), 'k_w': w(ks[2], (D, D)), 'k_b': jnp.zeros((D,), jnp.float32), 'v_w': w(ks[3], (D, D)), 'v_b': jnp.zeros((D,), jnp.float32), 'o_w': w(ks[4], (D, D)), 'o_b': jnp.zeros((D,), jnp.float32), 'ln1_w': jnp.ones((D,), jnp.float32), 'ln1_b': jnp.zeros((D,), jnp.float32), 'ln2_w': jnp.ones((D,), jnp.float32), 'ln2_b': jnp.zeros((D,), jnp.float32), 'dec_w': w(ks[5], (D, H)), 'dec_b': jnp.full((H,), 5.0, jnp.float32), 'f1_w': w(ks[6], (D, FFN)), 'f1_b': jnp.zeros((FFN,), jnp.float32), 'f2_w': w(ks[7], (FFN, D)), 'f2_b': jnp.zeros((D,), jnp.float32)}
    _L1_attn_in = _L1_attn_setup()

    def _L1_ffn_setup():
        import jax, jax.numpy as jnp
        import numpy as np
        D_MODEL = 128
        HIDDEN = 256
        N_EXPERTS = 8
        TOP_K = 2
        BATCH = 2
        SEQ = 256
        key = jax.random.key(seed)
        ks = jax.random.split(key, 9)
        s = 0.02
        return {'x': jax.random.normal(ks[0], (BATCH, SEQ, D_MODEL), dtype=jnp.float32), 'w_router': jax.random.normal(ks[1], (D_MODEL, N_EXPERTS), dtype=jnp.float32) * s, 'w1': jax.random.normal(ks[2], (N_EXPERTS, D_MODEL, HIDDEN), dtype=jnp.float32) * s, 'w3': jax.random.normal(ks[3], (N_EXPERTS, D_MODEL, HIDDEN), dtype=jnp.float32) * s, 'w2': jax.random.normal(ks[4], (N_EXPERTS, HIDDEN, D_MODEL), dtype=jnp.float32) * s, 'sw1': jax.random.normal(ks[5], (D_MODEL, HIDDEN), dtype=jnp.float32) * s, 'sw3': jax.random.normal(ks[6], (D_MODEL, HIDDEN), dtype=jnp.float32) * s, 'sw2': jax.random.normal(ks[7], (HIDDEN, D_MODEL), dtype=jnp.float32) * s}
    _L1_ffn_in = _L1_ffn_setup()
    _d = {'L0_attn_x': _L0_attn_in['x'], 'L0_attn_qkv_w': _L0_attn_in['qkv_w'], 'L0_attn_qkv_b': _L0_attn_in['qkv_b'], 'L0_attn_proj_w': _L0_attn_in['proj_w'], 'L0_attn_proj_b': _L0_attn_in['proj_b'], 'L0_ffn_gate_w': _L0_ffn_in['gate_w'], 'L0_ffn_w1': _L0_ffn_in['w1'], 'L0_ffn_b1': _L0_ffn_in['b1'], 'L0_ffn_w2': _L0_ffn_in['w2'], 'L0_ffn_b2': _L0_ffn_in['b2'], 'L0_ffn_w3': _L0_ffn_in['w3'], 'L0_ffn_b3': _L0_ffn_in['b3'], 'L0_ffn_sw1': _L0_ffn_in['sw1'], 'L0_ffn_sw2': _L0_ffn_in['sw2'], 'L0_ffn_sw3': _L0_ffn_in['sw3'], 'L1_attn_q_w': _L1_attn_in['q_w'], 'L1_attn_q_b': _L1_attn_in['q_b'], 'L1_attn_k_w': _L1_attn_in['k_w'], 'L1_attn_k_b': _L1_attn_in['k_b'], 'L1_attn_v_w': _L1_attn_in['v_w'], 'L1_attn_v_b': _L1_attn_in['v_b'], 'L1_attn_o_w': _L1_attn_in['o_w'], 'L1_attn_o_b': _L1_attn_in['o_b'], 'L1_attn_ln1_w': _L1_attn_in['ln1_w'], 'L1_attn_ln1_b': _L1_attn_in['ln1_b'], 'L1_attn_ln2_w': _L1_attn_in['ln2_w'], 'L1_attn_ln2_b': _L1_attn_in['ln2_b'], 'L1_attn_dec_w': _L1_attn_in['dec_w'], 'L1_attn_dec_b': _L1_attn_in['dec_b'], 'L1_attn_f1_w': _L1_attn_in['f1_w'], 'L1_attn_f1_b': _L1_attn_in['f1_b'], 'L1_attn_f2_w': _L1_attn_in['f2_w'], 'L1_attn_f2_b': _L1_attn_in['f2_b'], 'L1_ffn_w_router': _L1_ffn_in['w_router'], 'L1_ffn_w1': _L1_ffn_in['w1'], 'L1_ffn_w3': _L1_ffn_in['w3'], 'L1_ffn_w2': _L1_ffn_in['w2'], 'L1_ffn_sw1': _L1_ffn_in['sw1'], 'L1_ffn_sw3': _L1_ffn_in['sw3'], 'L1_ffn_sw2': _L1_ffn_in['sw2']}
    _x0 = _d['L0_attn_x']
    _d['L0_attn_x'] = jax.random.normal(jax.random.fold_in(jax.random.key(seed), 1), (1, 2048, 128), dtype=_x0.dtype)
    del _x0
    return _d

def reference(L0_attn_x, L0_attn_qkv_w, L0_attn_qkv_b, L0_attn_proj_w, L0_attn_proj_b, L0_ffn_gate_w, L0_ffn_w1, L0_ffn_b1, L0_ffn_w2, L0_ffn_b2, L0_ffn_w3, L0_ffn_b3, L0_ffn_sw1, L0_ffn_sw2, L0_ffn_sw3, L1_attn_q_w, L1_attn_q_b, L1_attn_k_w, L1_attn_k_b, L1_attn_v_w, L1_attn_v_b, L1_attn_o_w, L1_attn_o_b, L1_attn_ln1_w, L1_attn_ln1_b, L1_attn_ln2_w, L1_attn_ln2_b, L1_attn_dec_w, L1_attn_dec_b, L1_attn_f1_w, L1_attn_f1_b, L1_attn_f2_w, L1_attn_f2_b, L1_ffn_w_router, L1_ffn_w1, L1_ffn_w3, L1_ffn_w2, L1_ffn_sw1, L1_ffn_sw3, L1_ffn_sw2):

    def _L0_attn_ref(x, qkv_w, qkv_b, proj_w, proj_b):
        import jax, jax.numpy as jnp
        import numpy as np
        B, S, D, H = (2, 256, 128, 16)
        HD = D // H
        b, s, d = x.shape
        qkv = jnp.einsum('bsd,ed->bse', x, qkv_w) + qkv_b
        qkv = qkv.reshape(b, s, 3, H, HD)
        q = jnp.transpose(qkv[:, :, 0], (0, 2, 1, 3))
        k = jnp.transpose(qkv[:, :, 1], (0, 2, 1, 3))
        v = jnp.transpose(qkv[:, :, 2], (0, 2, 1, 3))
        scale = 1.0 / jnp.sqrt(jnp.asarray(HD, dtype=x.dtype))
        scores = jnp.einsum('bhqe,bhke->bhqk', q, k) * scale
        attn = jax.nn.softmax(scores, axis=-1)
        out = jnp.einsum('bhqk,bhke->bhqe', attn, v)
        out = jnp.transpose(out, (0, 2, 1, 3)).reshape(b, s, d)
        out = jnp.einsum('bsd,ed->bse', out, proj_w) + proj_b
        return out

    def _L0_ffn_ref(x, gate_w, w1, b1, w2, b2, w3, b3, sw1, sw2, sw3):
        import jax, jax.numpy as jnp
        import numpy as np
        D = 128
        H = 128
        E = 8
        K = 2
        I = 2 * 128
        ROUTE_SCALE = 1.0
        B, S, _ = x.shape
        xt = x.reshape(-1, D)
        logits = xt @ gate_w.T
        scores = jax.nn.softmax(logits.astype(jnp.float32), axis=-1)
        top_vals, idx = jax.lax.top_k(scores, K)
        weights = jnp.take_along_axis(scores, idx, axis=1).astype(x.dtype) * ROUTE_SCALE
        xs = xt[:, None, :] * weights[:, :, None]
        y = jnp.zeros_like(xt)
        for e in range(E):
            mask = (idx == e).astype(x.dtype)
            h = jax.nn.silu(jnp.einsum('tkd,hd->tkh', xs, w1[e]) + b1[e])
            x2 = jnp.einsum('tkh,dh->tkd', h, w2[e]) + b2[e]
            x3 = jnp.einsum('tkd,hd->tkh', xs, w3[e]) + b3[e]
            y = y + jnp.sum(x2 * x3 * mask[:, :, None], axis=1)
        z = jax.nn.silu(xt @ sw1.T) * (xt @ sw2.T) @ sw3.T
        return (y + z).reshape(B, S, D)

    def _L1_attn_ref(x, q_w, q_b, k_w, k_b, v_w, v_b, o_w, o_b, ln1_w, ln1_b, ln2_w, ln2_b, dec_w, dec_b, f1_w, f1_b, f2_w, f2_b):
        import jax, jax.numpy as jnp
        import numpy as np
        B, T, D, H, FFN = (2, 256, 128, 16, 512)
        K = D // H
        EPS = 1e-06
        LN_EPS = 1e-05
        LAM_MIN = 1e-08

        def _ln(x, w, b):
            m = x.mean(-1, keepdims=True)
            v = ((x - m) ** 2).mean(-1, keepdims=True)
            return (x - m) * jax.lax.rsqrt(v + LN_EPS) * w + b

        def _lion(phi_q, phi_k, v, lam):
            b, h, t, kk = phi_q.shape
            kv = v.shape[-1]
            to_t = lambda a: a.transpose(2, 0, 1, 3)
            qt, kt, vt, lt = (to_t(phi_q), to_t(phi_k), to_t(v), to_t(lam))
            S0 = jnp.zeros((b, h, kk, kv), phi_q.dtype)

            def fwd(S, inp):
                q_t, k_t, v_t, l_t = inp
                S = S * l_t[..., None] + k_t[..., None] * v_t[..., None, :]
                return (S, jnp.einsum('bhk,bhkv->bhv', q_t, S))
            _, out_f = jax.lax.scan(fwd, S0, (qt, kt, vt, lt))
            q_shift = jnp.concatenate([qt[:1], qt[:-1]], axis=0)

            def bwd(R, inp):
                qs_t, k_t, v_t, l_t = inp
                R = l_t[..., None] * (k_t[..., None] * v_t[..., None, :] + R)
                return (R, jnp.einsum('bhk,bhkv->bhv', qs_t, R))
            _, out_b = jax.lax.scan(bwd, S0, (q_shift, kt, vt, lt), reverse=True)
            out_b = jnp.concatenate([out_b[1:], jnp.zeros_like(out_b[:1])], axis=0)
            return (out_f + out_b).transpose(1, 2, 0, 3)
        bb, tt, dd = x.shape
        residual = x
        x_n = _ln(x, ln1_w, ln1_b)
        split = lambda y: y.reshape(bb, tt, H, K).transpose(0, 2, 1, 3)
        q = split(x_n @ q_w + q_b)
        k = split(x_n @ k_w + k_b)
        v = split(x_n @ v_w + v_b)
        phi_q = jax.nn.elu(q) + 1.0
        phi_k = jax.nn.elu(k) + 1.0
        lam = jax.nn.sigmoid(x_n @ dec_w + dec_b)
        lam = jnp.maximum(lam, LAM_MIN).transpose(0, 2, 1)
        lam = jnp.broadcast_to(lam[..., None], (bb, H, tt, K))
        v_ext = jnp.concatenate([v, jnp.ones((bb, H, tt, 1), v.dtype)], axis=-1)
        out = _lion(phi_q, phi_k, v_ext, lam)
        num, den = (out[..., :K], jnp.maximum(out[..., K:], EPS))
        attn = (num / den).transpose(0, 2, 1, 3).reshape(bb, tt, dd)
        x = residual + (attn @ o_w + o_b)
        x2 = _ln(x, ln2_w, ln2_b)
        h = jax.nn.gelu(x2 @ f1_w + f1_b, approximate=False)
        return x + (h @ f2_w + f2_b)

    def _L1_ffn_ref(x, w_router, w1, w3, w2, sw1, sw3, sw2):
        import jax, jax.numpy as jnp
        import numpy as np
        D_MODEL = 128
        HIDDEN = 256
        N_EXPERTS = 8
        TOP_K = 2
        BATCH = 2
        SEQ = 256
        b, s, d = x.shape
        xf = x.reshape(b * s, d)
        probs = jax.nn.softmax(xf @ w_router, axis=-1)
        top_vals, top_idx = jax.lax.top_k(probs, TOP_K)
        gates = top_vals / jnp.sum(top_vals, axis=-1, keepdims=True)
        onehot = jax.nn.one_hot(top_idx, N_EXPERTS, dtype=xf.dtype)
        cw = jnp.einsum('tk,tke->te', gates, onehot)
        h1 = jnp.einsum('td,edh->eth', xf, w1)
        h3 = jnp.einsum('td,edh->eth', xf, w3)
        y = jnp.einsum('eth,ehd->etd', jax.nn.silu(h1) * h3, w2)
        out = jnp.einsum('etd,te->td', y, cw)
        out = out + jax.nn.silu(xf @ sw1) * (xf @ sw3) @ sw2
        return out.reshape(b, s, d)
    x = L0_attn_x
    x = x + 0.5 * _L0_ffn_ref(_layernorm(x, axis=-1), L0_ffn_gate_w, L0_ffn_w1, L0_ffn_b1, L0_ffn_w2, L0_ffn_b2, L0_ffn_w3, L0_ffn_b3, L0_ffn_sw1, L0_ffn_sw2, L0_ffn_sw3)
    x = x + _L0_attn_ref(_layernorm(x, axis=-1), L0_attn_qkv_w, L0_attn_qkv_b, L0_attn_proj_w, L0_attn_proj_b)
    x = x + 0.5 * _L0_ffn_ref(_layernorm(x, axis=-1), L0_ffn_gate_w, L0_ffn_w1, L0_ffn_b1, L0_ffn_w2, L0_ffn_b2, L0_ffn_w3, L0_ffn_b3, L0_ffn_sw1, L0_ffn_sw2, L0_ffn_sw3)
    x = x + 0.5 * _L1_ffn_ref(_layernorm(x, axis=-1), L1_ffn_w_router, L1_ffn_w1, L1_ffn_w3, L1_ffn_w2, L1_ffn_sw1, L1_ffn_sw3, L1_ffn_sw2)
    x = x + _L1_attn_ref(_layernorm(x, axis=-1), L1_attn_q_w, L1_attn_q_b, L1_attn_k_w, L1_attn_k_b, L1_attn_v_w, L1_attn_v_b, L1_attn_o_w, L1_attn_o_b, L1_attn_ln1_w, L1_attn_ln1_b, L1_attn_ln2_w, L1_attn_ln2_b, L1_attn_dec_w, L1_attn_dec_b, L1_attn_f1_w, L1_attn_f1_b, L1_attn_f2_w, L1_attn_f2_b)
    x = x + 0.5 * _L1_ffn_ref(_layernorm(x, axis=-1), L1_ffn_w_router, L1_ffn_w1, L1_ffn_w3, L1_ffn_w2, L1_ffn_sw1, L1_ffn_sw3, L1_ffn_sw2)
    return x

_drawn_inputs = setup_inputs


def setup_inputs(seed=0):
    import zlib

    import numpy as np

    out = dict(_drawn_inputs(seed))
    spreads = {'L1_attn_q_b': (0.0, 0.8),
     'L1_attn_k_b': (0.0, 2.0),
     'L1_attn_v_b': (0.0, 0.695),
     'L1_attn_o_b': (0.0, 0.1),
     'L1_attn_ln1_w': (1.0, 0.6),
     'L1_attn_ln1_b': (0.0, 0.8),
     'L1_attn_ln2_w': (1.0, 0.6),
     'L1_attn_ln2_b': (0.0, 2.0),
     'L1_attn_dec_b': (5.0, 0.6),
     'L1_attn_f1_b': (0.0, 0.729),
     'L1_attn_f2_b': (0.0, 0.1)}
    factors = {'L0_attn_proj_b': 3.104,
     'L0_ffn_b1': 8.0,
     'L0_ffn_b2': 8.0,
     'L0_ffn_b3': 8.0,
     'L1_attn_q_w': 8.0,
     'L1_attn_k_w': 8.0,
     'L1_attn_v_w': 8.0,
     'L1_attn_o_w': 4.668,
     'L1_attn_dec_w': 8.0,
     'L1_ffn_w_router': 8.0,
     'L1_ffn_w1': 8.0,
     'L1_ffn_w3': 8.0,
     'L1_ffn_w2': 8.0,
     'L1_ffn_sw1': 8.0,
     'L1_ffn_sw3': 8.0,
     'L1_ffn_sw2': 8.0}
    for name, (base, spread) in spreads.items():
        noise = np.random.default_rng([zlib.crc32(name.encode()), seed]).standard_normal(out[name].shape)
        drawn = base * np.exp(spread * noise) if base else spread * noise
        out[name] = jnp.asarray(drawn.astype(out[name].dtype))
    for name, factor in factors.items():
        out[name] = (out[name] * factor).astype(out[name].dtype)
    return out
```

```python
import concourse.bass as bass
from concourse import mybir
from contextlib import ExitStack

F32 = mybir.dt.float32
BF16 = mybir.dt.bfloat16
ALU = mybir.AluOpType
ACT = mybir.ActivationFunctionType
AX = mybir.AxisListType

P = 128
D = 128
T = 2048
TILES = T // P
CHUNK = 512
CHUNKS = T // CHUNK
TPC = CHUNK // P
E = 8
TOPK = 2
HID0 = 128
SH0 = 256 // P
HID1 = 256 // P
H = 16
HD = D // H
FFN = 512 // P
LN_EPS = 1e-5
DEN_EPS = 1e-6
LAM_MIN = 1e-8

GH = 4
GROUPS = H // GH
PARTS = 3
ROWS = PARTS * PARTS * HD
ROWS_M = ROWS + PARTS
VC = HD + 1
S1_STEPS = 56
P_RING = 3


class Chain:

    def __init__(self, engine, sem):
        self.engine, self.sem, self.count = engine, sem, 0

    def __call__(self, instruction):
        self.count += 1
        instruction.then_inc(self.sem, 1)
        self.engine.wait_ge(self.sem, self.count)


class Machine:

    def __init__(self, nc, stack):
        self.nc, self.stack, self.calls = nc, stack, 0
        self.in_use, self.cleared, self.free = [], [], []

    def sb(self, name, shape, dt=F32, stack=None):
        return (stack or self.stack).enter_context(self.nc.sbuf_tensor(name, shape, dt))

    def sem(self, name):
        handle = self.free.pop() if self.free else self.stack.enter_context(self.nc.semaphore(f"{name}_{self.calls}"))
        self.in_use.append(handle)
        return handle

    def stage(self):
        self.calls += 1
        self.free += self.cleared
        for handle in self.in_use:
            self.nc.sync.sem_clear(handle)
        self.cleared, self.in_use = self.in_use, []
        return f"_{self.calls}"


def setup(m, w):
    nc = m.nc
    m.stage()
    loaded_x, loaded_t, loaded_w = m.sem("loaded_x"), m.sem("loaded_t"), m.sem("loaded_w")
    pool_steps, ident_ready = m.sem("pool_steps"), m.sem("ident_ready")
    turned, stored = m.sem("turned"), m.sem("stored")
    raw = [(w["L0_ffn_w1"].rearrange("e h d -> h e d"), E, m.w1T),
           (w["L0_ffn_w3"].rearrange("e h d -> h e d"), E, m.w3T),
           (w["L0_ffn_w2"].rearrange("e h d -> h e d"), E, m.w2T),
           (w["L0_ffn_sw1"].rearrange("(a p) d -> p a d", p=P), SH0, m.sw1T),
           (w["L0_ffn_sw2"].rearrange("(a p) d -> p a d", p=P), SH0, m.sw2T),
           (w["L0_ffn_sw3"].rearrange("d (a p) -> d a p", p=P), SH0, m.sw3T),
           (w["L0_attn_qkv_w"].rearrange("(a p) d -> p a d", p=P), 3, m.qkvT),
           (w["L0_attn_proj_w"].rearrange("(a p) d -> p a d", p=P), 1, m.projT)]
    n_raw = sum(n for _, n, _ in raw)
    with ExitStack() as stack:
        wraw = m.sb("wraw", [P, n_raw, D], stack=stack)
        graw = m.sb("graw", [E, D], stack=stack)
        braw = m.sb("braw", [m.bias_rows, D], stack=stack)
        block = stack.enter_context(nc.Block())

        @block.sync
        def _(sp):
            at = 0
            for src, n, _ in raw:
                sp.dma_start(wraw[:, at:at + n, :], src).then_inc(loaded_t, 16)
                at += n
            sp.dma_start(graw[:, :], w["L0_ffn_gate_w"]).then_inc(loaded_t, 16)
            at = 0
            for src, n in m.biases:
                sp.dma_start(braw[at:at + n, :], src).then_inc(loaded_t, 16)
                at += n
            sp.dma_start(m.X[:, :, :], w["L0_attn_x"][0].rearrange("(t p) d -> p t d", p=P)).then_inc(loaded_x, 16)
            sp.wait_ge(loaded_x, 16)

        @block.scalar
        def _(act):
            n = 0
            for dst, src in m.loads:
                act.dma_start(dst, src).then_inc(loaded_w, 16)
                n += 16
            act.wait_ge(loaded_w, n)

        @block.gpsimd
        def _(pool):
            step = Chain(pool, pool_steps)
            step(nc.gpsimd.memset(m.ident[:, :], 0.0))
            step(nc.gpsimd.affine_select(out=m.ident[:, :], in_=m.ident[:, :], compare_op=ALU.not_equal, fill=1.0,
                                         base=0, pattern=[[-1, P]], channel_multiplier=1))
            nc.gpsimd.tensor_copy(m.identb[:, :], m.ident[:, :]).then_inc(ident_ready, 1)
            nc.gpsimd.memset(m.neg_half[:, :], -0.5)
            nc.gpsimd.memset(m.gT[:, :], 0.0)
            step(nc.gpsimd.memset(m.below[:, :, :], 1.0))
            step(nc.gpsimd.affine_select(out=m.below[:, :, :], in_=m.below[:, :, :], compare_op=ALU.is_gt, fill=0.0,
                                         base=0, pattern=[[1, E], [-1, E]], channel_multiplier=0))
            rows = PARTS + 1
            step(nc.gpsimd.memset(m.sel_gate[:, :, :], 1.0))
            step(nc.gpsimd.memset(m.sel_mask[:, :, :], 1.0))
            step(nc.gpsimd.affine_select(out=m.sel_gate[:, :, :], in_=m.sel_gate[:, :, :], compare_op=ALU.is_ge,
                                         fill=0.0, base=0, pattern=[[-rows, E], [0, P]], channel_multiplier=1))
            step(nc.gpsimd.affine_select(out=m.sel_gate[:, :, :], in_=m.sel_gate[:, :, :], compare_op=ALU.is_ge,
                                         fill=0.0, base=PARTS - 1, pattern=[[rows, E], [0, P]], channel_multiplier=-1))
            step(nc.gpsimd.affine_select(out=m.sel_mask[:, :, :], in_=m.sel_mask[:, :, :], compare_op=ALU.is_equal,
                                         fill=0.0, base=-PARTS, pattern=[[-rows, E], [0, P]], channel_multiplier=1))
            step(nc.gpsimd.memset(m.pick[:, :, :], 1.0))
            pick = m.pick[:, :, :].rearrange("p c (g v) -> p c g v", v=HD)
            step(nc.gpsimd.affine_select(out=pick, in_=pick, compare_op=ALU.is_ge, fill=0.0, base=0,
                                         pattern=[[0, HD], [-HD, H], [0, HD]], channel_multiplier=1))
            step(nc.gpsimd.affine_select(out=pick, in_=pick, compare_op=ALU.is_ge, fill=0.0, base=HD - 1,
                                         pattern=[[0, HD], [HD, H], [0, HD]], channel_multiplier=-1))
            step(nc.gpsimd.tensor_copy(m.same_head[:, :], m.pick[:, 0, :]))
            step(nc.gpsimd.affine_select(out=pick, in_=pick, compare_op=ALU.is_equal, fill=0.0, base=0,
                                         pattern=[[1, HD], [0, H], [-1, HD]], channel_multiplier=0))

        @block.tensor
        def _(pe):
            pe.wait_ge(ident_ready, 1)
            pe.wait_ge(loaded_t, 16 * (len(raw) + 1 + len(m.biases)))
            for i in range(0, n_raw, 4):
                if i // 4 >= 4:
                    pe.wait_ge(stored, i // 4 - 3)
                for j in range(i, min(i + 4, n_raw)):
                    last = nc.tensor.transpose(m.ps[:, i // 4 % 4, (j - i) * P:(j - i + 1) * P], wraw[:, j, :], m.ident[:, :])
                last.then_inc(turned, 1)
            nc.tensor.transpose(m.ps[:, 4, 0:E], graw[:, :], m.ident[0:E, 0:E]).then_inc(turned, 1)
            nb = m.bias_rows
            nc.tensor.transpose(m.ps[:, 5, 0:nb], braw[:, :], m.ident[0:nb, 0:nb]).then_inc(turned, 1)

        @block.vector
        def _(dve):
            for i in range(0, n_raw, 4):
                n = min(4, n_raw - i)
                dve.wait_ge(turned, i // 4 + 1)
                nc.vector.tensor_copy(m.wT[:, i:i + n, :], m.ps[:, i // 4 % 4, 0:n * P]).then_inc(stored, 1)
            dve.wait_ge(turned, (n_raw + 3) // 4 + 2)
            nc.vector.tensor_copy(m.gateT[:, :], m.ps[:, 4, 0:E]).then_inc(stored, 1)
            nc.vector.tensor_copy(m.biasT[:, :], m.ps[:, 5, 0:m.bias_rows]).then_inc(stored, 1)
            dve.wait_ge(loaded_w, 16 * len(m.loads))
            nc.vector.tensor_copy(m.dec_rep[:, :].rearrange("p (h k) -> p h k", k=HD),
                                  m.dec_w[:, :].unsqueeze(2).to_broadcast([P, H, HD]))
            for v in range(HD):
                nc.vector.tensor_copy(m.v_rep[:, v, :].rearrange("p (h k) -> p h k", k=HD),
                                      m.v_w[:, :].rearrange("p (h v) -> p h v", v=HD)[:, :, v:v + 1].to_broadcast([P, H, HD]))


def layer_norm(m, src, dst, scale=None, bias=None):
    nc = m.nc
    tag = m.stage()
    centred_sem, squared, var_ready, rstd_ready = m.sem("centred"), m.sem("squared"), m.sem("var_ready"), m.sem("rstd_ready")
    normed, turned, steps, stored = m.sem("normed"), m.sem("turned"), m.sem("ln_steps"), m.sem("xT_stored")
    with ExitStack() as stack:
        centred = m.sb("centred" + tag, [P, TILES, D], stack=stack)
        square = m.sb("square" + tag, [P, TILES, D], stack=stack)
        dst = centred if dst is None else dst
        total = m.sb("total" + tag, [P, TILES], stack=stack)
        mean = m.sb("mean" + tag, [P, TILES], stack=stack)
        total2 = m.sb("total2" + tag, [P, TILES], stack=stack)
        var = m.sb("var" + tag, [P, TILES], stack=stack)
        rstd = m.sb("rstd" + tag, [P, TILES], stack=stack)
        block = stack.enter_context(nc.Block())

        def tiles(c):
            return slice(c * TPC, (c + 1) * TPC)

        @block.vector
        def _(dve):
            step = Chain(dve, steps)
            for c in range(CHUNKS):
                t = tiles(c)
                step(nc.vector.reduce_sum(total[:, t], src[:, t, :], AX.X))
                step(nc.vector.tensor_scalar(mean[:, t], total[:, t], 1.0 / D, None, ALU.mult))
                nc.vector.tensor_tensor(centred[:, t, :], src[:, t, :], mean[:, t].unsqueeze(2).to_broadcast([P, TPC, D]),
                                        ALU.subtract).then_inc(centred_sem, 1)
            for c in range(CHUNKS):
                t = tiles(c)
                dve.wait_ge(squared, c + 1)
                step(nc.vector.reduce_sum(total2[:, t], square[:, t, :], AX.X))
                nc.vector.tensor_scalar(var[:, t], total2[:, t], 1.0 / D, LN_EPS, ALU.mult, ALU.add).then_inc(var_ready, 1)
            for c in range(CHUNKS):
                t = tiles(c)
                dve.wait_ge(rstd_ready, c + 1)
                nc.vector.tensor_tensor(dst[:, t, :], centred[:, t, :], rstd[:, t].unsqueeze(2).to_broadcast([P, TPC, D]),
                                        ALU.mult).then_inc(normed, 1)

        @block.gpsimd
        def _(pool):
            for c in range(CHUNKS):
                pool.wait_ge(var_ready, c + 1)
                nc.gpsimd.tensor_tensor(rstd[:, tiles(c)], var[:, tiles(c)], m.neg_half[:, 0:TPC], ALU.pow).then_inc(rstd_ready, 1)

        @block.tensor
        def _(pe):
            for c in range(CHUNKS):
                pe.wait_ge(normed, c + 1)
                for j in range(TPC):
                    last = nc.tensor.transpose(m.ps[:, c, j * P:(j + 1) * P], dst[:, c * TPC + j, :], m.ident[:, :])
                last.then_inc(turned, 1)

        @block.scalar
        def _(act):
            for c in range(CHUNKS):
                act.wait_ge(centred_sem, c + 1)
                nc.scalar.activation(square[:, tiles(c), :], centred[:, tiles(c), :], ACT.Square).then_inc(squared, 1)
            for c in range(CHUNKS):
                act.wait_ge(turned, c + 1)
                out = m.xT[:, c * CHUNK:(c + 1) * CHUNK]
                if scale is None:
                    nc.scalar.activation(out, m.ps[:, c, :], ACT.Copy).then_inc(stored, 1)
                else:
                    nc.scalar.activation(out, m.ps[:, c, :], ACT.Identity, bias=bias, scale=scale).then_inc(stored, 1)
            act.wait_ge(stored, CHUNKS)


def route(m, gate, pair):
    nc = m.nc
    tag = m.stage()
    logits_ready, shifted, exped, steps = m.sem("logits_ready"), m.sem("shifted"), m.sem("exped"), m.sem("route_steps")
    parts_ready, turned, stored = m.sem("parts_ready"), m.sem("gates_turned"), m.sem("gates_stored")
    rows = PARTS + 1
    with ExitStack() as stack:
        top = m.sb("top" + tag, [P, TILES], stack=stack)
        total = m.sb("total" + tag, [P, TILES], stack=stack)
        inv = m.sb("inv" + tag, [P, TILES], stack=stack)
        z = m.sb("z" + tag, [P, TILES, E], stack=stack)
        ez = m.sb("ez" + tag, [P, TILES, E], stack=stack)
        score = m.sb("score" + tag, [P, TILES, E], stack=stack)
        higher = m.sb("higher" + tag, [P, TILES, E * E], stack=stack)
        equal = m.sb("equal" + tag, [P, TILES, E * E], stack=stack)
        rank = m.sb("rank" + tag, [P, TILES, E], stack=stack)
        mask = m.sb("mask" + tag, [P, TILES, E], stack=stack)
        gates = m.sb("gates" + tag, [P, TILES, E], stack=stack)
        rest = m.sb("rest" + tag, [P, TILES, E], stack=stack)
        rest2 = m.sb("rest2" + tag, [P, TILES, E], stack=stack)
        packed = m.sb("packed" + tag, [P, TILES, E, rows], BF16, stack=stack)
        logits = m.ps[:, 0, 0:TILES * E].rearrange("p (t e) -> p t e", e=E)
        block = stack.enter_context(nc.Block())

        def over_e(a):
            return a[:, :].unsqueeze(2).to_broadcast([P, TILES, E])

        @block.tensor
        def _(pe):
            for t in range(TILES):
                last = nc.tensor.matmul(m.ps[:, 0, t * E:(t + 1) * E], m.xT[:, t * P:(t + 1) * P], gate[:, :],
                                        start=True, stop=True)
            last.then_inc(logits_ready, 1)
            if pair:
                pe.wait_ge(parts_ready, 1)
                for t in range(TILES):
                    out = m.ps[0:E * rows, 1 + t // 8, :].bitcast(BF16)[:, t % 8 * P:(t % 8 + 1) * P]
                    last = nc.tensor.transpose(out, packed[:, t, :, :].rearrange("p e r -> p (e r)"), m.identb[:, :])
                last.then_inc(turned, 1)

        @block.scalar
        def _(act):
            act.wait_ge(shifted, 1)
            nc.scalar.activation(ez[:, :, :], z[:, :, :], ACT.Exp).then_inc(exped, 1)

        @block.vector
        def _(dve):
            step = Chain(dve, steps)
            dve.wait_ge(logits_ready, 1)
            step(nc.vector.reduce_max(top[:, :], logits, AX.X))
            nc.vector.tensor_tensor(z[:, :, :], logits, over_e(top), ALU.subtract).then_inc(shifted, 1)
            dve.wait_ge(exped, 1)
            step(nc.vector.reduce_sum(total[:, :], ez[:, :, :], AX.X))
            step(nc.vector.reciprocal(inv[:, :], total[:, :]))
            step(nc.vector.tensor_tensor(score[:, :, :], ez[:, :, :], over_e(inv), ALU.mult))
            f_side = score[:, :, :].unsqueeze(2).to_broadcast([P, TILES, E, E])
            e_side = score[:, :, :].unsqueeze(3).to_broadcast([P, TILES, E, E])
            hi4 = higher[:, :, :].rearrange("p t (e f) -> p t e f", f=E)
            step(nc.vector.tensor_tensor(hi4, f_side, e_side, ALU.is_gt))
            eq4 = equal[:, :, :].rearrange("p t (e f) -> p t e f", f=E)
            step(nc.vector.tensor_tensor(eq4, f_side, e_side, ALU.is_equal))
            below = m.below[:, :, :].rearrange("p e f -> p (e f)").unsqueeze(1).to_broadcast([P, TILES, E * E])
            step(nc.vector.tensor_tensor(equal[:, :, :], equal[:, :, :], below, ALU.mult))
            step(nc.vector.tensor_tensor(higher[:, :, :], higher[:, :, :], equal[:, :, :], ALU.add))
            step(nc.vector.reduce_sum(rank[:, :, :], hi4, AX.X))
            step(nc.vector.tensor_scalar(mask[:, :, :], rank[:, :, :], TOPK - 0.5, None, ALU.is_lt))
            step(nc.vector.tensor_tensor(gates[:, :, :], score[:, :, :], mask[:, :, :], ALU.mult))
            if pair:
                step(nc.vector.tensor_copy(packed[:, :, :, 0], gates[:, :, :]))
                step(nc.vector.tensor_tensor(rest[:, :, :], gates[:, :, :], packed[:, :, :, 0], ALU.subtract))
                step(nc.vector.tensor_copy(packed[:, :, :, 1], rest[:, :, :]))
                step(nc.vector.tensor_tensor(rest2[:, :, :], rest[:, :, :], packed[:, :, :, 1], ALU.subtract))
                step(nc.vector.tensor_copy(packed[:, :, :, 2], rest2[:, :, :]))
                nc.vector.tensor_copy(packed[:, :, :, 3], mask[:, :, :]).then_inc(parts_ready, 1)
                dve.wait_ge(turned, 1)
                for i in range(2):
                    nc.vector.tensor_copy(m.gT[0:E * rows, i * 1024:(i + 1) * 1024],
                                          m.ps[0:E * rows, 1 + i, :].bitcast(BF16)).then_inc(stored, 1)
                dve.wait_ge(stored, 2)
            else:
                step(nc.vector.reduce_sum(total[:, :], gates[:, :, :], AX.X))
                step(nc.vector.reciprocal(inv[:, :], total[:, :]))
                step(nc.vector.tensor_scalar(inv[:, :], inv[:, :], 0.5, None, ALU.mult))
                step(nc.vector.tensor_tensor(m.cw[:, :, 0:E], gates[:, :, :], over_e(inv), ALU.mult))
                step(nc.vector.memset(m.cw[:, :, E:E + 1], 0.5))


def moe0(m):
    nc = m.nc
    tag = m.stage()
    bc_ready, xg_ready, up_ready, x3_ready = m.sem("bc_ready"), m.sem("xg_ready"), m.sem("up_ready"), m.sem("x3_ready")
    hid_ready, x3b_ready, x3m_ready, y_ready = m.sem("hid_ready"), m.sem("x3b_ready"), m.sem("x3m_ready"), m.sem("y_ready")
    prod_ready, summed, sh_silu, sh_hid = m.sem("prod_ready"), m.sem("summed"), m.sem("sh_silu"), m.sem("sh_hid")
    sh_a, sh_b, sh_out, yT_ready = m.sem("sh_a"), m.sem("sh_b"), m.sem("sh_out"), m.sem("yT_ready")
    y_turned, x_updated = m.sem("y_turned"), m.sem("x_updated")
    GB, MB, HB, TB, YB, ZB = [0, 1], [2, 3], 4, 5, 6, 7
    with ExitStack() as stack:
        xg = m.sb("xg" + tag, [P, 2, CHUNK], stack=stack)
        hid = m.sb("hid" + tag, [P, 2, CHUNK], stack=stack)
        x3b = m.sb("x3b" + tag, [P, 2, CHUNK], stack=stack)
        x3m = m.sb("x3m" + tag, [P, 2, CHUNK], stack=stack)
        prod = m.sb("prod" + tag, [P, 2, CHUNK], stack=stack)
        acc = m.sb("acc" + tag, [P, 2, CHUNK], stack=stack)
        shs = m.sb("shs" + tag, [P, SH0, CHUNK], stack=stack)
        shh = m.sb("shh" + tag, [P, SH0, CHUNK], stack=stack)
        yT = m.sb("yT" + tag, [P, CHUNK], stack=stack)
        block = stack.enter_context(nc.Block())

        @block.tensor
        def _(pe):
            with pe.Fori(0, CHUNKS) as c:
                x_c = m.xT[:, bass.ts(c, CHUNK)]
                g_c = m.gT[:, bass.ts(c, CHUNK)]

                def broadcast(e):
                    if e >= 2:
                        pe.wait_ge(xg_ready, c * E + (e - 1))
                        pe.wait_ge(x3m_ready, c * E + (e - 1))
                    nc.tensor.matmul(m.ps[:, GB[e % 2], :], m.sel_gate[:, e, :], g_c, start=True, stop=True)
                    nc.tensor.matmul(m.ps[:, MB[e % 2], :], m.sel_mask[:, e, :], g_c, start=True, stop=True)\
                        .then_inc(bc_ready, 1)

                def down(e):
                    pe.wait_ge(hid_ready, c * E + (e + 1))
                    if e >= 1:
                        pe.wait_ge(prod_ready, c * E + e)
                    nc.tensor.matmul(m.ps[:, YB, :], m.w2T[:, e, :], hid[:, e % 2, :], start=True, stop=True)\
                        .then_inc(y_ready, 1)

                broadcast(0)
                for i in range(SH0):
                    if i >= 1:
                        pe.wait_ge(sh_silu, c * SH0 + i)
                    nc.tensor.matmul(m.ps[:, HB, :], m.sw1T[:, i, :], x_c, start=True, stop=True).then_inc(sh_a, 1)
                    if i >= 1:
                        pe.wait_ge(sh_hid, c * SH0 + i)
                    nc.tensor.matmul(m.ps[:, TB, :], m.sw2T[:, i, :], x_c, start=True, stop=True).then_inc(sh_b, 1)
                for e in range(E):
                    if e + 1 < E:
                        broadcast(e + 1)
                    if e == 0:
                        pe.wait_ge(sh_silu, c * SH0 + SH0)
                    else:
                        pe.wait_ge(hid_ready, c * E + e)
                    pe.wait_ge(xg_ready, c * E + (e + 1))
                    nc.tensor.matmul(m.ps[:, HB, :], m.w1T[:, e, :], xg[:, e % 2, :], start=True, stop=True)\
                        .then_inc(up_ready, 1)
                    if e == 0:
                        pe.wait_ge(sh_hid, c * SH0 + SH0)
                    else:
                        pe.wait_ge(x3b_ready, c * E + e)
                    nc.tensor.matmul(m.ps[:, TB, :], m.w3T[:, e, :], xg[:, e % 2, :], start=True, stop=True)\
                        .then_inc(x3_ready, 1)
                    if e == 0:
                        for i in range(SH0):
                            last = nc.tensor.matmul(m.ps[:, ZB, :], m.sw3T[:, i, :], shh[:, i, :],
                                                    start=(i == 0), stop=(i == SH0 - 1))
                        last.then_inc(sh_out, 1)
                    else:
                        down(e - 1)
                down(E - 1)
                pe.wait_ge(yT_ready, c + 1)
                for j in range(TPC):
                    last = nc.tensor.transpose(m.ps[:, HB, j * P:(j + 1) * P], yT[:, j * P:(j + 1) * P], m.ident[:, :])
                last.then_inc(y_turned, 1)
                pe.wait_ge(x_updated, c + 1)

        @block.scalar
        def _(act):
            with act.Fori(0, CHUNKS) as c:
                for i in range(SH0):
                    act.wait_ge(sh_a, c * SH0 + (i + 1))
                    nc.scalar.activation(shs[:, i, :], m.ps[:, HB, :], ACT.Silu).then_inc(sh_silu, 1)
                for e in range(E):
                    act.wait_ge(up_ready, c * E + (e + 1))
                    if e >= 2:
                        act.wait_ge(y_ready, c * E + (e - 1))
                    nc.scalar.activation(hid[:, e % 2, :], m.ps[:, HB, :], ACT.Silu, bias=m.b1[:, e:e + 1])\
                        .then_inc(hid_ready, 1)
                    act.wait_ge(x3_ready, c * E + (e + 1))
                    if e >= 2:
                        act.wait_ge(x3m_ready, c * E + (e - 1))
                    nc.scalar.activation(x3b[:, e % 2, :], m.ps[:, TB, :], ACT.Identity, bias=m.b3[:, e:e + 1])\
                        .then_inc(x3b_ready, 1)

        @block.vector
        def _(dve):
            with dve.Fori(0, CHUNKS) as c:
                x_c = m.xT[:, bass.ts(c, CHUNK)]

                def gate_x(e):
                    dve.wait_ge(bc_ready, c * E + (e + 1))
                    if e >= 2:
                        dve.wait_ge(x3_ready, c * E + (e - 1))
                    nc.vector.tensor_tensor(xg[:, e % 2, :], m.ps[:, GB[e % 2], :], x_c, ALU.mult).then_inc(xg_ready, 1)

                def mask_x3(e):
                    dve.wait_ge(x3b_ready, c * E + (e + 1))
                    if e >= 2:
                        dve.wait_ge(prod_ready, c * E + (e - 1))
                    nc.vector.tensor_tensor(x3m[:, e % 2, :], m.ps[:, MB[e % 2], :], x3b[:, e % 2, :], ALU.mult)\
                        .then_inc(x3m_ready, 1)

                def product(e):
                    dve.wait_ge(y_ready, c * E + (e + 1))
                    dve.wait_ge(x3m_ready, c * E + (e + 1))
                    if e >= 2:
                        dve.wait_ge(summed, c * (E - 1) + max(1, e - 2))
                    nc.vector.scalar_tensor_tensor(out=prod[:, e % 2, :], in0=m.ps[:, YB, :], scalar=m.b2[:, e:e + 1],
                                                   in1=x3m[:, e % 2, :], op0=ALU.add, op1=ALU.mult).then_inc(prod_ready, 1)

                gate_x(0)
                for i in range(SH0):
                    dve.wait_ge(sh_b, c * SH0 + (i + 1))
                    dve.wait_ge(sh_silu, c * SH0 + (i + 1))
                    nc.vector.tensor_tensor(shh[:, i, :], m.ps[:, TB, :], shs[:, i, :], ALU.mult).then_inc(sh_hid, 1)
                for e in range(E):
                    if e + 1 < E:
                        gate_x(e + 1)
                    mask_x3(e)
                    if e >= 1:
                        product(e - 1)
                product(E - 1)
                dve.wait_ge(summed, c * (E - 1) + (E - 1))
                dve.wait_ge(sh_out, c + 1)
                nc.vector.tensor_tensor(yT[:, :], m.ps[:, ZB, :], acc[:, (E - 1) % 2, :], ALU.add).then_inc(yT_ready, 1)
                dve.wait_ge(y_turned, c + 1)
                x_t = m.X[:, bass.ts(c, TPC), :].rearrange("p t d -> p (t d)")
                nc.vector.scalar_tensor_tensor(out=x_t, in0=m.ps[:, HB, :], scalar=0.5, in1=x_t,
                                               op0=ALU.mult, op1=ALU.add).then_inc(x_updated, 1)

        @block.gpsimd
        def _(pool):
            with pool.Fori(0, CHUNKS) as c:
                for e in range(1, E):
                    pool.wait_ge(prod_ready, c * E + (e + 1))
                    if e > 1:
                        pool.wait_ge(summed, c * (E - 1) + (e - 1))
                    before = prod[:, 0, :] if e == 1 else acc[:, (e - 1) % 2, :]
                    nc.gpsimd.tensor_tensor(acc[:, e % 2, :], before, prod[:, e % 2, :], ALU.add).then_inc(summed, 1)


def moe1(m):
    nc = m.nc
    tag = m.stage()
    NE = E + 1
    a_ready, b_ready, silu_done, hid_ready = m.sem("a_ready"), m.sem("b_ready"), m.sem("silu_done"), m.sem("hid_ready")
    y_ready, y_used = m.sem("y_ready"), m.sem("y_used")
    AB, BB, YB = [0, 1], [2, 3], [4, 5]
    with ExitStack() as stack:
        silu = m.sb("silu" + tag, [P, HID1, CHUNK], stack=stack)
        hid = m.sb("hid1" + tag, [P, 2, HID1, CHUNK], stack=stack)
        block = stack.enter_context(nc.Block())

        @block.tensor
        def _(pe):
            with pe.Fori(0, CHUNKS) as c:
                x_c = m.xT[:, bass.ts(c, CHUNK)]

                def down(e):
                    pe.wait_ge(hid_ready, c * (NE * HID1) + HID1 * (e + 1))
                    if e >= 2:
                        pe.wait_ge(y_used, c * NE + (e - 1))
                    for j in range(TPC):
                        for i in range(HID1):
                            last = nc.tensor.matmul(m.ps[:, YB[e % 2], j * P:(j + 1) * P],
                                                    hid[:, e % 2, i, j * P:(j + 1) * P], m.ew2[:, e, i, :],
                                                    start=(i == 0), stop=(i == HID1 - 1))
                    last.then_inc(y_ready, 1)

                for e in range(NE):
                    for i in range(HID1):
                        if e >= 1:
                            pe.wait_ge(silu_done, c * (NE * HID1) + ((e - 1) * HID1 + i + 1))
                        nc.tensor.matmul(m.ps[:, AB[i], :], m.ew1[:, e, i * P:(i + 1) * P], x_c, start=True, stop=True)\
                            .then_inc(a_ready, 1)
                        if e >= 1:
                            pe.wait_ge(hid_ready, c * (NE * HID1) + ((e - 1) * HID1 + i + 1))
                        nc.tensor.matmul(m.ps[:, BB[i], :], m.ew3[:, e, i * P:(i + 1) * P], x_c, start=True, stop=True)\
                            .then_inc(b_ready, 1)
                    if e >= 1:
                        down(e - 1)
                down(NE - 1)
                pe.wait_ge(y_used, c * NE + NE)

        @block.scalar
        def _(act):
            with act.Fori(0, CHUNKS) as c:
                for e in range(NE):
                    for i in range(HID1):
                        act.wait_ge(a_ready, c * (NE * HID1) + (e * HID1 + i + 1))
                        if e >= 1:
                            act.wait_ge(hid_ready, c * (NE * HID1) + ((e - 1) * HID1 + i + 1))
                        nc.scalar.activation(silu[:, i, :], m.ps[:, AB[i], :], ACT.Silu).then_inc(silu_done, 1)

        @block.vector
        def _(dve):
            with dve.Fori(0, CHUNKS) as c:
                x_t = m.X[:, bass.ts(c, TPC), :]
                cw = m.cw[:, bass.ts(c, TPC), :]

                def add(e):
                    dve.wait_ge(y_ready, c * NE + (e + 1))
                    if e >= 1:
                        dve.wait_ge(y_used, c * NE + e)
                    for j in range(TPC):
                        last = nc.vector.scalar_tensor_tensor(out=x_t[:, j, :], in0=m.ps[:, YB[e % 2], j * P:(j + 1) * P],
                                                              scalar=cw[:, j, e:e + 1], in1=x_t[:, j, :],
                                                              op0=ALU.mult, op1=ALU.add)
                    last.then_inc(y_used, 1)

                for e in range(NE):
                    for i in range(HID1):
                        dve.wait_ge(b_ready, c * (NE * HID1) + (e * HID1 + i + 1))
                        dve.wait_ge(silu_done, c * (NE * HID1) + (e * HID1 + i + 1))
                        if e >= 2:
                            dve.wait_ge(y_ready, c * NE + (e - 1))
                        nc.vector.tensor_tensor(hid[:, e % 2, i, :], m.ps[:, BB[i], :], silu[:, i, :], ALU.mult)\
                            .then_inc(hid_ready, 1)
                    if e >= 1:
                        add(e - 1)
                add(NE - 1)


def softmax_attention(m, w):
    nc = m.nc
    tag = m.stage()
    scale = float(HD) ** -0.5
    dram_q = nc.dram_tensor("q_parts", [PARTS, D, T], BF16, kind="Internal").ap()
    dram_k = nc.dram_tensor("k_parts", [PARTS, D, T], BF16, kind="Internal").ap()
    kv_stack = ExitStack()
    values = m.sb("values", [P, GROUPS, TILES, GH, VC], stack=kv_stack)

    proj, f32_ready, hi_ready, steps = m.sem("proj"), m.sem("f32_ready"), m.sem("hi_ready"), m.sem("part_steps")
    parts_ready, parts_out, v_ready, v_stored = m.sem("parts_ready"), [m.sem("parts_out0"), m.sem("parts_out1")], m.sem("v_ready"), m.sem("v_stored")
    ones_set = m.sem("ones_set")
    sides = [(0, scale, dram_q), (1, 1.0, dram_k)]
    jobs = [(s, c) for c in range(CHUNKS) for s in range(2)]
    with ExitStack() as stack:
        full = m.sb("full" + tag, [P, 2, CHUNK], stack=stack)
        rest = m.sb("rest" + tag, [P, CHUNK], stack=stack)
        part = m.sb("part" + tag, [P, 2, PARTS, CHUNK], BF16, stack=stack)
        block = stack.enter_context(nc.Block())

        @block.tensor
        def _(pe):
            for n, (s, c) in enumerate(jobs):
                if n >= 2:
                    pe.wait_ge(hi_ready, n - 1)
                nc.tensor.matmul(m.ps[:, n % 2, :], m.qkvT[:, s, :], m.xT[:, c * CHUNK:(c + 1) * CHUNK],
                                 start=True, stop=True).then_inc(proj, 1)
                if n % 2 == 1:
                    for j in range(TPC):
                        t = c * TPC + j
                        last = nc.tensor.matmul(m.ps[:, 2 + c, j * P:(j + 1) * P], m.xT[:, t * P:(t + 1) * P],
                                                m.qkvT[:, 2, :], start=True, stop=True)
                    last.then_inc(v_ready, 1)

        @block.scalar
        def _(act):
            for n, (s, c) in enumerate(jobs):
                act.wait_ge(proj, n + 1)
                if n >= 2:
                    act.wait_ge(parts_ready, n - 1)
                nc.scalar.activation(full[:, n % 2, :], m.ps[:, n % 2, :], ACT.Identity, bias=m.qk_bias[:, s:s + 1],
                                     scale=sides[s][1]).then_inc(f32_ready, 1)
                act.wait_ge(f32_ready, n + 1)
                if n >= 2:
                    act.wait_ge(parts_out[n % 2], 16 * (n // 2))
                nc.scalar.activation(part[:, n % 2, 0, :], full[:, n % 2, :], ACT.Copy).then_inc(hi_ready, 1)

        @block.vector
        def _(dve):
            step = Chain(dve, steps)
            nc.vector.memset(values[:, :, :, :, HD:VC], 1.0).then_inc(ones_set, 1)
            for n, (s, c) in enumerate(jobs):
                dve.wait_ge(hi_ready, n + 1)
                if n >= 2:
                    dve.wait_ge(parts_out[n % 2], 16 * (n // 2))
                step(nc.vector.tensor_tensor(rest[:, :], full[:, n % 2, :], part[:, n % 2, 0, :], ALU.subtract))
                step(nc.vector.tensor_copy(part[:, n % 2, 1, :], rest[:, :]))
                nc.vector.tensor_tensor(part[:, n % 2, 2, :], rest[:, :], part[:, n % 2, 1, :], ALU.subtract)\
                    .then_inc(parts_ready, 1)
                dve.wait_ge(parts_ready, n + 1)
                if n % 2 == 1:
                    dve.wait_ge(v_ready, c + 1)
                    for j in range(TPC):
                        nc.vector.tensor_tensor(
                            values[:, :, c * TPC + j, :, 0:HD],
                            m.ps[:, 2 + c, j * P:(j + 1) * P].rearrange("p (g h e) -> p g h e", h=GH, e=HD),
                            m.v_bias[:, :].rearrange("p (g h e) -> p g h e", h=GH, e=HD), ALU.add).then_inc(v_stored, 1)

        @block.sync
        def _(sp):
            for n, (s, c) in enumerate(jobs):
                sp.wait_ge(parts_ready, n + 1)
                sp.dma_start(sides[s][2][:, :, c * CHUNK:(c + 1) * CHUNK].rearrange("i p t -> p i t"),
                             part[:, n % 2, :, :]).then_inc(parts_out[n % 2], 16)
            for i in range(2):
                sp.wait_ge(parts_out[i], 16 * len(jobs) // 2)

    m.stage()
    UNITS = GROUPS * CHUNKS
    STEPS = TILES * GH
    PAIRS = STEPS // 2
    q_loaded = [m.sem(f"q_loaded{i}") for i in range(CHUNKS)]
    k1_loaded = [m.sem(f"k1_loaded{i}") for i in range(GH)]
    k2_loaded = [m.sem(f"k2_loaded{i}") for i in range(2)]
    v_loaded = [m.sem(f"v_loaded{i}") for i in range(2)]
    fixed, s1_ready, s1_used, neg_ready = m.sem("fixed"), m.sem("s1_ready"), m.sem("s1_used"), m.sem("neg_ready")
    max_turned, max_stored, max_loaded = m.sem("max_turned"), m.sem("max_stored"), m.sem("max_loaded")
    s2_ready, exped, av_done, out_ready, out_stored = (m.sem("s2_ready"), m.sem("exped"), m.sem("av_done"),
                                                       m.sem("out_ready"), m.sem("out_stored"))
    max_steps = m.sem("max_steps")
    att_stack = ExitStack()
    outs = m.sb("outs", [P, UNITS, CHUNK], stack=att_stack)
    with ExitStack() as stack:
        q = m.sb("q", [ROWS_M, CHUNKS, GH, CHUNK], BF16, stack=stack)
        k1 = m.sb("k1", [ROWS, GH, T], BF16, stack=stack)
        k2 = m.sb("k2", [ROWS_M, GH, T], BF16, stack=stack)
        v = m.sb("v", [P, TILES, GH, VC], stack=stack)
        ex = [m.sb("ex", [P, GH, CHUNK], stack=stack)[:, :, :], m.xT[:, :].rearrange("p (h t) -> p h t", t=CHUNK),
              m.xn[:, :, :].rearrange("p (h a) d -> p h (a d)", a=TPC)]
        mx = m.sb("mx", [P, GH, TPC, CHUNKS], stack=stack)
        neg = m.sb("neg", [P, GH, TPC], stack=stack)
        neg_rest = m.sb("neg_rest", [P, 2, GH, TPC], stack=stack)
        neg_part = m.sb("neg_part", [P, TPC, PARTS, GH], BF16, stack=stack)
        max_rows = m.sb("max_rows", [PARTS * GH, CHUNK], BF16, stack=stack)
        zeros = m.sb("zeros", [P, CHUNK], BF16, stack=stack)
        S2B, S1B, MXB, AVB = [0, 1, 2, 3], [4, 5], 6, 7
        block = stack.enter_context(nc.Block())
        key_rows = dram_k.rearrange("j (h e) t -> j e h t", e=HD)
        query_rows = dram_q.rearrange("i (h e) t -> i e h t", e=HD)

        DMAS_Q = 16 * PARTS * PARTS
        DMAS_K = 16 * PARTS * PARTS

        def load_q(eng, g, qc):
            for i in range(PARTS):
                for j in range(PARTS):
                    r = (i * PARTS + j) * HD
                    eng.dma_start(q[r:r + HD, qc, :, :],
                                  query_rows[i, :, bass.ts(g, GH), qc * CHUNK:(qc + 1) * CHUNK]).then_inc(q_loaded[qc], 16)

        def load_k1(eng, g, h):
            for i in range(PARTS):
                for j in range(PARTS):
                    r = (i * PARTS + j) * HD
                    eng.dma_start(k1[r:r + HD, h, :], key_rows[j, :, bass.ts(g * GH + h, 1), :])\
                        .then_inc(k1_loaded[h], 16)

        def load_k2(eng, g, half):
            t = slice(half * (T // 2), (half + 1) * (T // 2))
            for i in range(PARTS):
                for j in range(PARTS):
                    r = (i * PARTS + j) * HD
                    eng.dma_start(k2[r:r + HD, :, t], key_rows[j, :, bass.ts(g, GH), t]).then_inc(k2_loaded[half], 16)

        def load_v(eng, g, half):
            t = slice(half * (TILES // 2), (half + 1) * (TILES // 2))
            eng.dma_start(v[:, t, :, :], values[:, bass.ts(g, 1), t, :, :].rearrange("p g t h e -> p (g t) h e"))\
                .then_inc(v_loaded[half], 16)

        S1_AT = [i * S1_STEPS // STEPS for i in range(STEPS)]

        @block.sync
        def _(sp):
            load_q(sp, 0, 0)
            for h in range(GH):
                load_k1(sp, 0, h)
            load_q(sp, 0, 1)
            sp.wait_ge(fixed, 1)
            for half in range(2):
                load_k2(sp, 0, half)
                load_v(sp, 0, half)

            def load_maxima(u, qc):
                sp.wait_ge(max_stored, u + 1)
                for i in range(PARTS):
                    sp.dma_start(q[ROWS + i:ROWS + i + 1, qc, :, :], max_rows[i * GH:(i + 1) * GH, :])\
                        .then_inc(max_loaded, 16)

            def unit(g, qc, last):
                u = g * CHUNKS + qc
                if qc == CHUNKS - 2 and not last:
                    for h in range(GH):
                        sp.wait_ge(s1_ready, (u + 1) * STEPS + (h + 1) * STEPS // GH)
                        load_k1(sp, g + 1, h)
                if qc == CHUNKS - 1 and not last:
                    sp.wait_ge(s2_ready, u * PAIRS + PAIRS // 2)
                    load_k2(sp, g + 1, 0)
                    sp.wait_ge(av_done, u * TILES + TILES // 2)
                    load_v(sp, g + 1, 0)
                if not (last and qc == CHUNKS - 1):
                    load_maxima(u + 1, (qc + 1) % CHUNKS)
                if qc == CHUNKS - 1 and not last:
                    sp.wait_ge(s2_ready, u * PAIRS + PAIRS)
                    load_k2(sp, g + 1, 1)
                    sp.wait_ge(av_done, u * TILES + TILES)
                    load_v(sp, g + 1, 1)
                if not (last and qc >= CHUNKS - 2):
                    if qc < 2:
                        load_q(sp, g, qc + 2)
                    else:
                        load_q(sp, g + 1, qc - 2)

            load_maxima(0, 0)
            with sp.Fori(0, GROUPS - 1) as g:
                for qc in range(CHUNKS):
                    unit(g, qc, False)
            for qc in range(CHUNKS):
                unit(GROUPS - 1, qc, True)

        @block.gpsimd
        def _(pool):
            nc.gpsimd.memset(k2[64:ROWS_M, :, :], 1.0).then_inc(fixed, 1)
            pool.wait_ge(fixed, 1)
            nc.gpsimd.memset(zeros[:, :], 0.0).then_inc(fixed, 1)

        @block.tensor
        def _(pe):
            def first_pass(g, qc, i):
                h, qt, kc = i // (TPC * CHUNKS), i // CHUNKS % TPC, i % CHUNKS
                if i == 0:
                    pe.wait_ge(q_loaded[qc], DMAS_Q * (g + 1))
                if qc == 0 and i % (TPC * CHUNKS) == 0:
                    pe.wait_ge(k1_loaded[h], DMAS_K * (g + 1))
                n = (g * CHUNKS + qc) * STEPS + i
                if not (isinstance(g, int) and g == 0 and qc == 0 and i < 2):
                    pe.wait_ge(s1_used, n - 1)
                nc.tensor.matmul(m.ps[:, S1B[i % 2], :], q[0:ROWS, qc, h, qt * P:(qt + 1) * P],
                                 k1[:, h, kc * CHUNK:(kc + 1) * CHUNK], start=True, stop=True).then_inc(s1_ready, 1)

            def turn_maxima(g, qc):
                pe.wait_ge(neg_ready, g * CHUNKS + (qc + 1))
                for qt in range(TPC):
                    out = m.ps[0:PARTS * GH, MXB, :].bitcast(BF16)[:, qt * P:(qt + 1) * P]
                    last = nc.tensor.transpose(out, neg_part[:, qt, :, :].rearrange("p i h -> p (i h)"), m.identb[:, :])
                last.then_inc(max_turned, 1)

            def weigh(g, qc, kt, first):
                u = g * CHUNKS + qc
                if qc == 0 and kt % (TILES // 2) == 0:
                    pe.wait_ge(v_loaded[kt // (TILES // 2)], 16 * (g + 1))
                if kt == 0 and not first:
                    pe.wait_ge(out_stored, u + 0)
                pe.wait_ge(exped, u * PAIRS + (2 * kt + 2))
                for h in range(GH):
                    last = nc.tensor.matmul(m.ps[32 * h:32 * h + VC, AVB, :], v[:, kt, h, :],
                                            ex[kt % P_RING][:, h, :], start=(kt == 0), stop=(kt == TILES - 1),
                                            skip_group_check=True)
                last.then_inc(av_done, 1)
                if kt == TILES - 1:
                    pass

            def unit(g, qc, last, first=False):
                u = g * CHUNKS + qc
                nxt = (g, qc + 1) if qc + 1 < CHUNKS else (g + 1, 0)
                has_next = not (last and qc == CHUNKS - 1)
                pe.wait_ge(max_loaded, 16 * PARTS * (u + 1))
                step1 = 0
                for kt in range(TILES):
                    if qc == 0 and kt % (TILES // 2) == 0:
                        pe.wait_ge(k2_loaded[kt // (TILES // 2)], DMAS_K * (g + 1))
                    for h in range(GH):
                        s = kt * GH + h
                        if h % 2 == 0 and not (first and s < GH):
                            pe.wait_ge(exped, u * PAIRS + (s // 2 - 1))
                        mm = nc.tensor.matmul(m.ps[:, S2B[h], :], k2[:, h, kt * P:(kt + 1) * P], q[:, qc, h, :],
                                              start=True, stop=True)
                        if h % 2 == 1:
                            mm.then_inc(s2_ready, 1)
                        while has_next and step1 < STEPS and S1_AT[step1] == s:
                            first_pass(nxt[0], nxt[1], step1)
                            step1 += 1
                    if kt >= 1:
                        weigh(g, qc, kt - 1, first)
                if has_next:
                    turn_maxima(*nxt)
                weigh(g, qc, TILES - 1, first)

            pe.wait_ge(fixed, 2)
            nc.tensor.matmul(m.ps[:, AVB, :], zeros[:, 0:P], zeros[:, :], start=True, stop=True)
            for i in range(STEPS):
                first_pass(0, 0, i)
            turn_maxima(0, 0)
            unit(0, 0, False, True)
            for qc in range(1, CHUNKS):
                unit(0, qc, False)
            with pe.Fori(1, GROUPS - 1) as g:
                for qc in range(CHUNKS):
                    unit(g, qc, False)
            for qc in range(CHUNKS):
                unit(GROUPS - 1, qc, True)

        @block.scalar
        def _(act):
            def unit(g, qc, last, first=False):
                u = g * CHUNKS + qc
                for kt in range(TILES):
                    for pair in range(2):
                        act.wait_ge(s2_ready, u * PAIRS + (2 * kt + pair + 1))
                        if pair == 0 and not (first and kt < P_RING):
                            act.wait_ge(av_done, u * TILES + (kt - P_RING + 1))
                        nc.scalar.activation(ex[kt % P_RING][:, 2 * pair:2 * pair + 2, :],
                                             m.ps[:, 2 * pair:2 * pair + 2, :], ACT.Exp).then_inc(exped, 1)
                if not (last and qc == CHUNKS - 1):
                    store_maxima(u + 1, False)
                act.wait_ge(av_done, (u + 1) * TILES)
                nc.scalar.activation(outs[:, bass.ts(u, 1), :].rearrange("p u t -> p (u t)"), m.ps[:, AVB, :],
                                     ACT.Copy).then_inc(out_stored, 1)

            def store_maxima(u, first):
                act.wait_ge(max_turned, u + 1)
                if not first:
                    act.wait_ge(max_loaded, 16 * PARTS * u)
                nc.scalar.activation(max_rows[:, :], m.ps[0:PARTS * GH, MXB, :].bitcast(BF16)[:, 0:CHUNK],
                                     ACT.Copy).then_inc(max_stored, 1)

            store_maxima(0, True)
            unit(0, 0, False, True)
            for qc in range(1, CHUNKS):
                unit(0, qc, False)
            with act.Fori(1, GROUPS - 1) as g:
                for qc in range(CHUNKS):
                    unit(g, qc, False)
            for qc in range(CHUNKS):
                unit(GROUPS - 1, qc, True)

        @block.vector
        def _(dve):
            def maxima(u, first=False):
                for i in range(STEPS):
                    dve.wait_ge(s1_ready, u * STEPS + (i + 1))
                    h, qt, kc = i // (TPC * CHUNKS), i // CHUNKS % TPC, i % CHUNKS
                    nc.vector.reduce_max(mx[:, h, qt, kc:kc + 1], m.ps[:, S1B[i % 2], :], AX.X).then_inc(s1_used, 1)
                dve.wait_ge(s1_used, (u + 1) * STEPS)
                nc.vector.tensor_reduce(neg[:, :, :], mx[:, :, :, :], axis=AX.X, op=ALU.max, negate=True)\
                    .then_inc(max_steps, 1)
                dve.wait_ge(max_steps, u * 5 + 1)
                if not first:
                    dve.wait_ge(max_turned, u + 0)
                out = neg_part[:, :, :, :].rearrange("p t i h -> p h t i")
                nc.vector.tensor_copy(out[:, :, :, 0], neg[:, :, :]).then_inc(max_steps, 1)
                dve.wait_ge(max_steps, u * 5 + 2)
                nc.vector.tensor_tensor(neg_rest[:, 0, :, :], neg[:, :, :], out[:, :, :, 0], ALU.subtract).then_inc(max_steps, 1)
                dve.wait_ge(max_steps, u * 5 + 3)
                nc.vector.tensor_copy(out[:, :, :, 1], neg_rest[:, 0, :, :]).then_inc(max_steps, 1)
                dve.wait_ge(max_steps, u * 5 + 4)
                nc.vector.tensor_tensor(neg_rest[:, 1, :, :], neg_rest[:, 0, :, :], out[:, :, :, 1], ALU.subtract)\
                    .then_inc(max_steps, 1)
                dve.wait_ge(max_steps, u * 5 + 5)
                nc.vector.tensor_copy(out[:, :, :, 2], neg_rest[:, 1, :, :]).then_inc(neg_ready, 1)

            maxima(0, True)
            with dve.Fori(1, UNITS) as u:
                maxima(u)

    m.stage()
    out_turned, inv_ready, att_ready, att_turned = m.sem("out_turned"), m.sem("inv_ready"), m.sem("att_ready"), m.sem("att_turned")
    attT_ready, projected, bias_added, x_updated = m.sem("attT_ready"), m.sem("projected"), m.sem("bias_added"), m.sem("x_updated")
    with ExitStack() as stack:
        inv = m.sb("inv_den", [P, TPC, GH], stack=stack)
        att = m.sb("att", [P, TILES, D], stack=stack)
        attT = m.sb("attT", [P, T], stack=stack)
        xb = m.sb("xb", [P, 2, TPC, D], stack=stack)
        block = stack.enter_context(nc.Block())

        @block.tensor
        def _(pe):
            for qc in range(CHUNKS):
                for g in range(GROUPS):
                    n = qc * GROUPS + g
                    if n >= 2:
                        pe.wait_ge(att_ready, n - 1)
                    for j in range(TPC):
                        last = nc.tensor.transpose(m.ps[:, n % 2, j * P:(j + 1) * P],
                                                   outs[:, g * CHUNKS + qc, j * P:(j + 1) * P], m.ident[:, :])
                    last.then_inc(out_turned, 1)
                pe.wait_ge(att_ready, (qc + 1) * GROUPS)
                for j in range(TPC):
                    last = nc.tensor.transpose(m.ps[:, 2 + qc % 2, j * P:(j + 1) * P], att[:, qc * TPC + j, :], m.ident[:, :])
                last.then_inc(att_turned, 1)
                pe.wait_ge(attT_ready, qc + 1)
                if qc >= 2:
                    pe.wait_ge(bias_added, qc - 1)
                for j in range(TPC):
                    t = qc * TPC + j
                    last = nc.tensor.matmul(m.ps[:, 4 + qc % 2, j * P:(j + 1) * P], attT[:, t * P:(t + 1) * P],
                                            m.projT[:, 0, :], start=True, stop=True)
                last.then_inc(projected, 1)

        @block.scalar
        def _(act):
            for qc in range(CHUNKS):
                act.wait_ge(att_turned, qc + 1)
                nc.scalar.activation(attT[:, qc * CHUNK:(qc + 1) * CHUNK], m.ps[:, 2 + qc % 2, :], ACT.Copy)\
                    .then_inc(attT_ready, 1)

        @block.vector
        def _(dve):
            for qc in range(CHUNKS):
                for g in range(GROUPS):
                    n = qc * GROUPS + g
                    dve.wait_ge(out_turned, n + 1)
                    turned = m.ps[:, n % 2, :].rearrange("p (t h r) -> p t h r", h=GH, r=32)
                    if n >= 1:
                        dve.wait_ge(att_ready, n)
                    nc.vector.reciprocal(inv[:, :, :], turned[:, :, :, HD]).then_inc(inv_ready, 1)
                    dve.wait_ge(inv_ready, n + 1)
                    dst = att[:, qc * TPC:(qc + 1) * TPC, g * GH * HD:(g + 1) * GH * HD].rearrange("p t (h e) -> p t h e", e=HD)
                    nc.vector.tensor_tensor(dst, turned[:, :, :, 0:HD],
                                            inv[:, :, :].unsqueeze(3).to_broadcast([P, TPC, GH, HD]), ALU.mult)\
                        .then_inc(att_ready, 1)
                dve.wait_ge(projected, qc + 1)
                x_t = m.X[:, qc * TPC:(qc + 1) * TPC, :]
                nc.vector.tensor_tensor(xb[:, qc % 2, :, :], m.ps[:, 4 + qc % 2, :].rearrange("p (t d) -> p t d", d=D),
                                        m.proj_bias[:, :].unsqueeze(1).to_broadcast([P, TPC, D]), ALU.add).then_inc(bias_added, 1)
                dve.wait_ge(bias_added, qc + 1)
                nc.vector.tensor_tensor(x_t, x_t, xb[:, qc % 2, :, :], ALU.add).then_inc(x_updated, 1)
    att_stack.close()
    kv_stack.close()


def decay_attention(m):
    nc = m.nc
    tag = m.stage()
    proj, clipped, exped = m.sem("proj"), m.sem("clipped"), m.sem("exped")
    steps, feat_ready = m.sem("feat_steps"), m.sem("feat_ready")
    with ExitStack() as outer:
        phi = m.sb("phi" + tag, [P, 2, T], stack=outer)
        lam = m.sb("lam" + tag, [P, T], stack=outer)
        with ExitStack() as stack:
            low = m.sb("low" + tag, [P, 2, CHUNK], stack=stack)
            high = m.sb("high" + tag, [P, 2, CHUNK], stack=stack)
            elow = m.sb("elow" + tag, [P, 2, CHUNK], stack=stack)
            one_plus = m.sb("one_plus" + tag, [P, CHUNK], stack=stack)
            sig = m.sb("sig" + tag, [P, CHUNK], stack=stack)
            jobs = [(s, c) for c in range(CHUNKS) for s in range(3)]
            weights = [m.q_w, m.k_w, m.dec_rep]
            block = stack.enter_context(nc.Block())

            @block.tensor
            def _(pe):
                for n, (s, c) in enumerate(jobs):
                    if n >= 4:
                        pe.wait_ge(feat_ready, n - 3)
                    nc.tensor.matmul(m.ps[:, n % 4, :], weights[s][:, :], m.xT[:, c * CHUNK:(c + 1) * CHUNK],
                                     start=True, stop=True).then_inc(proj, 1)

            @block.scalar
            def _(act):
                for n, (s, c) in enumerate(jobs):
                    if s < 2:
                        act.wait_ge(clipped, 2 * c + s + 1)
                        if n >= 2:
                            act.wait_ge(feat_ready, n - 1)
                        nc.scalar.activation(elow[:, n % 2, :], low[:, n % 2, :], ACT.Exp).then_inc(exped, 1)
                    else:
                        act.wait_ge(proj, n + 1)
                        if n >= 2:
                            act.wait_ge(feat_ready, n - 1)
                        nc.scalar.activation(elow[:, n % 2, :], m.ps[:, n % 4, :], ACT.Exp, bias=m.neg_dec_b[:, 0:1],
                                             scale=-1.0).then_inc(exped, 1)

            @block.vector
            def _(dve):
                step = Chain(dve, steps)
                for n, (s, c) in enumerate(jobs):
                    t = slice(c * CHUNK, (c + 1) * CHUNK)
                    bank = m.ps[:, n % 4, :]
                    if s < 2:
                        dve.wait_ge(proj, n + 1)
                        nc.vector.tensor_scalar(low[:, n % 2, :], bank, m.qk1_bias[:, s:s + 1], 0.0, ALU.add, ALU.min)\
                            .then_inc(clipped, 1)
                        step(nc.vector.tensor_scalar(high[:, n % 2, :], bank, m.qk1_bias[:, s:s + 1], 0.0, ALU.add, ALU.max))
                        dve.wait_ge(exped, n + 1)
                        nc.vector.tensor_tensor(phi[:, s, t], high[:, n % 2, :], elow[:, n % 2, :], ALU.add)\
                            .then_inc(feat_ready, 1)
                        dve.wait_ge(feat_ready, n + 1)
                    else:
                        dve.wait_ge(exped, n + 1)
                        step(nc.vector.tensor_scalar(one_plus[:, :], elow[:, n % 2, :], 1.0, None, ALU.add))
                        step(nc.vector.reciprocal(sig[:, :], one_plus[:, :]))
                        nc.vector.tensor_scalar(lam[:, t], sig[:, :], LAM_MIN, None, ALU.max).then_inc(feat_ready, 1)
                        dve.wait_ge(feat_ready, n + 1)

        m.stage()
        v_ready, kv_ready, fwd_ready, bwd_ready = m.sem("v_ready"), m.sem("kv_ready"), m.sem("fwd_ready"), m.sem("bwd_ready")
        both_ready, qs_ready, summed, num_done = m.sem("both_ready"), m.sem("qs_ready"), m.sem("summed"), m.sem("num_done")
        edge, steps2, attT_ready, o_ready, ob_ready, x_ready = (m.sem("edge"), m.sem("steps"), m.sem("attT_ready"),
                                                                 m.sem("o_ready"), m.sem("ob_ready"), m.sem("x_ready"))
        with ExitStack() as stack:
            kv = m.sb("kv" + tag, [P, 2, T], stack=stack)
            fwd = m.sb("fwd" + tag, [P, 2, T], stack=stack)
            bwd = m.sb("bwd" + tag, [P, 2, T], stack=stack)
            both = fwd
            qs = m.sb("qs" + tag, [P, 2, T], stack=stack)
            den = m.sb("den" + tag, [P, 2, CHUNK], stack=stack)
            attT = m.sb("attT" + tag, [P, T], stack=stack)
            ob = m.sb("ob" + tag, [P, 2, TPC, D], stack=stack)
            block = stack.enter_context(nc.Block())

            def weigh(dve, v):
                dve.wait_ge(both_ready, v + 1)
                if v >= 2:
                    dve.wait_ge(summed, v - 1)
                nc.vector.tensor_tensor(qs[:, v % 2, :], phi[:, 0, :], both[:, v % 2, :], ALU.mult).then_inc(qs_ready, 1)

            @block.tensor
            def _(pe):
                def values_of(v):
                    for c in range(CHUNKS):
                        if v >= 1:
                            pe.wait_ge(kv_ready, (v - 1) * CHUNKS + c + 1)
                        nc.tensor.matmul(m.ps[:, 4 + c, :], m.v_rep[:, v, :], m.xT[:, c * CHUNK:(c + 1) * CHUNK],
                                         start=True, stop=True).then_inc(v_ready, 1)

                values_of(0)
                for v in range(VC):
                    if v + 1 < HD:
                        values_of(v + 1)
                    pe.wait_ge(qs_ready, v + 1)
                    if v == HD:
                        pe.wait_ge(kv_ready, HD * CHUNKS)
                    for c in range(CHUNKS):
                        if v < HD:
                            last = nc.tensor.matmul(m.ps[:, c, :], m.pick[:, v, :], qs[:, v % 2, c * CHUNK:(c + 1) * CHUNK],
                                                    start=(v == 0), stop=(v == HD - 1))
                        else:
                            last = nc.tensor.matmul(m.ps[:, 4 + c, :], m.same_head[:, :], qs[:, v % 2, c * CHUNK:(c + 1) * CHUNK],
                                                    start=True, stop=True)
                    last.then_inc(summed, 1)
                for c in range(CHUNKS):
                    pe.wait_ge(attT_ready, c + 1)
                    for j in range(TPC):
                        t = c * TPC + j
                        last = nc.tensor.matmul(m.ps[:, c, j * P:(j + 1) * P], attT[:, t * P:(t + 1) * P], m.o_w[:, :],
                                                start=True, stop=True)
                    last.then_inc(o_ready, 1)

            @block.vector
            def _(dve):
                step = Chain(dve, steps2)
                nc.vector.memset(bwd[:, 0, T - 1:T], 0.0).then_inc(edge, 1)
                nc.vector.memset(bwd[:, 1, T - 1:T], 0.0).then_inc(edge, 1)
                for v in range(VC):
                    if v < HD:
                        for c in range(CHUNKS):
                            t = slice(c * CHUNK, (c + 1) * CHUNK)
                            dve.wait_ge(v_ready, v * CHUNKS + c + 1)
                            nc.vector.scalar_tensor_tensor(out=kv[:, v % 2, t], in0=m.ps[:, 4 + c, :], scalar=m.v1_bias[:, v:v + 1],
                                                           in1=phi[:, 1, t], op0=ALU.add, op1=ALU.mult).then_inc(kv_ready, 1)
                        dve.wait_ge(kv_ready, (v + 1) * CHUNKS)
                        src = kv[:, v % 2, :]
                    else:
                        src = phi[:, 1, :]
                    if v >= 2:
                        dve.wait_ge(qs_ready, v - 1)
                    nc.vector.tensor_tensor_scan(fwd[:, v % 2, :], lam[:, :], src, 0.0, ALU.mult, ALU.add).then_inc(fwd_ready, 1)
                    nc.vector.tensor_tensor_scan(bwd[:, v % 2, 0:T - 1][:, ::-1], src[:, 1:T][:, ::-1], lam[:, 1:T][:, ::-1],
                                                 0.0, ALU.add, ALU.mult).then_inc(bwd_ready, 1)
                    if v >= 1:
                        weigh(dve, v - 1)
                weigh(dve, VC - 1)
                for c in range(CHUNKS):
                    t = slice(c * CHUNK, (c + 1) * CHUNK)
                    dve.wait_ge(summed, VC)
                    step(nc.vector.tensor_scalar(den[:, 0, :], m.ps[:, 4 + c, :], DEN_EPS, None, ALU.max))
                    step(nc.vector.reciprocal(den[:, 1, :], den[:, 0, :]))
                    nc.vector.tensor_tensor(attT[:, t], m.ps[:, c, :], den[:, 1, :], ALU.mult).then_inc(attT_ready, 1)
                    dve.wait_ge(attT_ready, c + 1)
                for c in range(CHUNKS):
                    dve.wait_ge(o_ready, c + 1)
                    if c >= 2:
                        dve.wait_ge(x_ready, c - 1)
                    nc.vector.tensor_tensor(ob[:, c % 2, :, :], m.ps[:, c, :].rearrange("p (t d) -> p t d", d=D),
                                            m.o_bias[:, :].unsqueeze(1).to_broadcast([P, TPC, D]), ALU.add).then_inc(ob_ready, 1)
                    dve.wait_ge(ob_ready, c + 1)
                    x_t = m.xn[:, c * TPC:(c + 1) * TPC, :]
                    nc.vector.tensor_tensor(x_t, x_t, ob[:, c % 2, :, :], ALU.add).then_inc(x_ready, 1)

            @block.gpsimd
            def _(pool):
                pool.wait_ge(edge, 2)
                for v in range(VC):
                    pool.wait_ge(fwd_ready, v + 1)
                    pool.wait_ge(bwd_ready, v + 1)
                    nc.gpsimd.tensor_tensor(both[:, v % 2, :], fwd[:, v % 2, :], bwd[:, v % 2, :], ALU.add).then_inc(both_ready, 1)


def gelu_ffn(m):
    nc = m.nc
    tag = m.stage()
    a_ready, hid_ready, y_ready, res_ready, yb_ready, x_ready = (m.sem("a_ready"), m.sem("hid_ready"), m.sem("y_ready"),
                                                                 m.sem("res_ready"), m.sem("yb_ready"), m.sem("x_ready"))
    with ExitStack() as stack:
        hid = m.sb("fhid" + tag, [P, 2, FFN, CHUNK], stack=stack)
        res = m.sb("fres" + tag, [P, 2, TPC, D], stack=stack)
        yb = m.sb("fyb" + tag, [P, 2, TPC, D], stack=stack)
        block = stack.enter_context(nc.Block())

        @block.tensor
        def _(pe):
            def up(c):
                for i in range(FFN):
                    if c >= 1:
                        pe.wait_ge(hid_ready, (c - 1) * FFN + i + 1)
                    nc.tensor.matmul(m.ps[:, i, :], m.f1_w[:, i * P:(i + 1) * P], m.xT[:, c * CHUNK:(c + 1) * CHUNK],
                                     start=True, stop=True).then_inc(a_ready, 1)

            up(0)
            for c in range(CHUNKS):
                if c + 1 < CHUNKS:
                    up(c + 1)
                pe.wait_ge(hid_ready, (c + 1) * FFN)
                if c >= 2:
                    pe.wait_ge(yb_ready, c - 1)
                for j in range(TPC):
                    for i in range(FFN):
                        last = nc.tensor.matmul(m.ps[:, 4 + c % 2, j * P:(j + 1) * P], hid[:, c % 2, i, j * P:(j + 1) * P],
                                                m.f2_w[:, i, :], start=(i == 0), stop=(i == FFN - 1))
                last.then_inc(y_ready, 1)

        @block.scalar
        def _(act):
            for c in range(CHUNKS):
                for i in range(FFN):
                    act.wait_ge(a_ready, c * FFN + i + 1)
                    if c >= 2:
                        act.wait_ge(y_ready, c - 1)
                    nc.scalar.activation(hid[:, c % 2, i, :], m.ps[:, i, :], ACT.Gelu, bias=m.f1_b[:, i:i + 1]).then_inc(hid_ready, 1)

        @block.vector
        def _(dve):
            for c in range(CHUNKS):
                t = slice(c * TPC, (c + 1) * TPC)
                if c >= 2:
                    dve.wait_ge(x_ready, c - 1)
                nc.vector.tensor_tensor(res[:, c % 2, :, :], m.X[:, t, :], m.xn[:, t, :], ALU.add).then_inc(res_ready, 1)
                dve.wait_ge(y_ready, c + 1)
                nc.vector.tensor_tensor(yb[:, c % 2, :, :], m.ps[:, 4 + c % 2, :].rearrange("p (t d) -> p t d", d=D),
                                        m.f2_bias[:, :].unsqueeze(1).to_broadcast([P, TPC, D]), ALU.add).then_inc(yb_ready, 1)
                dve.wait_ge(yb_ready, c + 1)
                dve.wait_ge(res_ready, c + 1)
                nc.vector.tensor_tensor(m.X[:, t, :], res[:, c % 2, :, :], yb[:, c % 2, :, :], ALU.add).then_inc(x_ready, 1)


def store(m, out):
    nc = m.nc
    m.stage()
    stored = m.sem("stored")
    with nc.Block() as block:

        @block.sync
        def _(sp):
            sp.dma_start(out[0].rearrange("(t p) d -> p t d", p=P), m.X[:, :, :]).then_inc(stored, 16)
            sp.wait_ge(stored, 16)


def macaron(nc: bass.Bass, w, out):
    with ExitStack() as stack:
        m = Machine(nc, stack)
        m.ps = stack.enter_context(nc.psum_tensor("ps", [P, 8, CHUNK], F32))
        m.X = m.sb("X", [P, TILES, D])
        m.xn = m.sb("xn", [P, TILES, D])
        m.xT = m.sb("xT", [P, T])
        m.ident = m.sb("ident", [P, P])
        m.identb = m.sb("identb", [P, P], BF16)
        m.neg_half = m.sb("neg_half", [P, TPC])
        m.below = m.sb("below", [P, E, E])
        m.sel_gate = m.sb("sel_gate", [P, E, P], BF16)
        m.sel_mask = m.sb("sel_mask", [P, E, P], BF16)
        m.gT = m.sb("gT", [P, T], BF16)
        m.pick = m.sb("pick", [P, HD, P])
        m.same_head = m.sb("same_head", [P, P])
        m.cw = m.sb("cw", [P, TILES, E + 1])
        counts = [E, E, E, SH0, SH0, SH0, 3, 1]
        m.wT = m.sb("wT", [P, sum(counts), D])
        at = [sum(counts[:i]) for i in range(len(counts) + 1)]
        m.w1T, m.w3T, m.w2T, m.sw1T, m.sw2T, m.sw3T, m.qkvT, m.projT = (
            m.wT[:, at[i]:at[i + 1], :] for i in range(len(counts)))
        m.gateT = m.sb("gateT", [P, E])
        m.biases = [(w["L0_ffn_b1"], E), (w["L0_ffn_b2"], E), (w["L0_ffn_b3"], E),
                    (w["L0_attn_qkv_b"][0:2 * D].rearrange("(s p) -> s p", p=P), 2),
                    (w["L1_attn_f1_b"].rearrange("(i p) -> i p", p=P), FFN)]
        m.biases += [(w[n].unsqueeze(0), 1) for n in ("L1_attn_q_b", "L1_attn_k_b", "L1_attn_ln1_w", "L1_attn_ln1_b",
                                                      "L1_attn_ln2_w", "L1_attn_ln2_b")]
        m.bias_rows = sum(n for _, n in m.biases)
        m.biasT = m.sb("biasT", [P, m.bias_rows])
        ends = [sum(n for _, n in m.biases[:i + 1]) for i in range(len(m.biases))]
        m.b1, m.b2, m.b3, m.qk_bias_raw, m.f1_b = (m.biasT[:, e - n:e] for e, (_, n) in zip(ends, m.biases[:5]))
        m.qk1_bias = m.biasT[:, ends[4]:ends[4] + 2]
        m.ln = m.biasT[:, ends[4] + 2:ends[4] + 6]
        m.qk_bias = m.sb("qk_bias", [P, 2])
        m.v_bias = m.sb("v_bias", [P, D])
        m.proj_bias = m.sb("proj_bias", [P, D])
        m.router = m.sb("router", [P, E])
        m.ew1 = m.sb("ew1", [P, E + 1, HID1 * P])
        m.ew3 = m.sb("ew3", [P, E + 1, HID1 * P])
        m.ew2 = m.sb("ew2", [P, E + 1, HID1, D])
        m.q_w, m.k_w, m.v_w, m.o_w = (m.sb(n, [P, D]) for n in ("q_w", "k_w", "v_w", "o_w"))
        m.dec_w = m.sb("dec_w", [P, H])
        m.dec_rep = m.sb("dec_rep", [P, D])
        m.v_rep = m.sb("v_rep", [P, HD, D])
        m.f1_w = m.sb("f1_w", [P, FFN * P])
        m.f2_w = m.sb("f2_w", [P, FFN, D])
        m.dec_b_all = m.sb("dec_b_all", [P, H])
        m.v_b_all = m.sb("v_b_all", [P, D])
        m.neg_dec_b = m.sb("neg_dec_b", [P, 1])
        m.v1_bias = m.sb("v1_bias", [P, HD])
        m.o_bias, m.f2_bias = m.sb("o_bias", [P, D]), m.sb("f2_bias", [P, D])

        def on_all(v):
            return v.unsqueeze(0).to_broadcast([P, v.shape[0]])

        m.loads = [
            (m.v_bias[:, :], on_all(w["L0_attn_qkv_b"][2 * D:3 * D])),
            (m.proj_bias[:, :], on_all(w["L0_attn_proj_b"])),
            (m.router[:, :], w["L1_ffn_w_router"]),
            (m.ew1[:, 0:E, :], w["L1_ffn_w1"].rearrange("e d h -> d e h")),
            (m.ew1[:, E, :], w["L1_ffn_sw1"]),
            (m.ew3[:, 0:E, :], w["L1_ffn_w3"].rearrange("e d h -> d e h")),
            (m.ew3[:, E, :], w["L1_ffn_sw3"]),
            (m.ew2[:, 0:E, :, :].rearrange("p e i d -> p (e i) d"), w["L1_ffn_w2"].rearrange("e (i p) d -> p (e i) d", p=P)),
            (m.ew2[:, E, :, :], w["L1_ffn_sw2"].rearrange("(i p) d -> p i d", p=P)),
            (m.q_w[:, :], w["L1_attn_q_w"]), (m.k_w[:, :], w["L1_attn_k_w"]),
            (m.v_w[:, :], w["L1_attn_v_w"]), (m.o_w[:, :], w["L1_attn_o_w"]),
            (m.dec_w[:, :], w["L1_attn_dec_w"]),
            (m.f1_w[:, :], w["L1_attn_f1_w"]),
            (m.f2_w[:, :, :], w["L1_attn_f2_w"].rearrange("(i p) d -> p i d", p=P)),
            (m.o_bias[:, :], on_all(w["L1_attn_o_b"])), (m.f2_bias[:, :], on_all(w["L1_attn_f2_b"])),
            (m.dec_b_all[:, :], on_all(w["L1_attn_dec_b"])), (m.v_b_all[:, :], on_all(w["L1_attn_v_b"])),
        ]

        setup(m, w)
        derive_biases(m)
        layer_norm(m, m.X, m.xn)
        route(m, m.gateT, True)
        moe0(m)
        layer_norm(m, m.X, m.xn)
        softmax_attention(m, w)
        layer_norm(m, m.X, m.xn)
        route(m, m.gateT, True)
        moe0(m)
        layer_norm(m, m.X, m.xn)
        route(m, m.router, False)
        moe1(m)
        layer_norm(m, m.X, m.xn)
        layer_norm(m, m.xn, None, m.ln[:, 0:1], m.ln[:, 1:2])
        decay_attention(m)
        layer_norm(m, m.xn, None, m.ln[:, 2:3], m.ln[:, 3:4])
        gelu_ffn(m)
        layer_norm(m, m.X, m.xn)
        route(m, m.router, False)
        moe1(m)
        store(m, out)


def derive_biases(m):
    nc = m.nc
    tag = m.stage()
    steps = m.sem("bias_steps")
    with ExitStack() as stack:
        own = m.sb("own" + tag, [P, D], stack=stack)
        own_dec = m.sb("own_dec" + tag, [P, H], stack=stack)
        block = stack.enter_context(nc.Block())

        @block.vector
        def _(dve):
            step = Chain(dve, steps)
            nc.vector.tensor_scalar(m.qk_bias[:, 0:1], m.qk_bias_raw[:, 0:1], float(HD) ** -0.5, None, ALU.mult)
            nc.vector.tensor_copy(m.qk_bias[:, 1:2], m.qk_bias_raw[:, 1:2])
            step(nc.vector.tensor_tensor(own[:, :], m.v_b_all[:, :], m.same_head[:, :], ALU.mult))
            step(nc.vector.reduce_sum(m.v1_bias[:, :], own[:, :].rearrange("p (h v) -> p v h", v=HD), AX.X))
            head = m.same_head[:, :].rearrange("p (h v) -> p h v", v=HD)[:, :, 0]
            step(nc.vector.tensor_tensor(own_dec[:, :], m.dec_b_all[:, :], head, ALU.mult))
            step(nc.vector.tensor_reduce(m.neg_dec_b[:, :], own_dec[:, :], axis=AX.X, op=ALU.add, negate=True))


_INS = ['L0_attn_x', 'L0_attn_qkv_w', 'L0_attn_qkv_b', 'L0_attn_proj_w', 'L0_attn_proj_b', 'L0_ffn_gate_w', 'L0_ffn_w1',
        'L0_ffn_b1', 'L0_ffn_w2', 'L0_ffn_b2', 'L0_ffn_w3', 'L0_ffn_b3', 'L0_ffn_sw1', 'L0_ffn_sw2', 'L0_ffn_sw3',
        'L1_attn_q_w', 'L1_attn_q_b', 'L1_attn_k_w', 'L1_attn_k_b', 'L1_attn_v_w', 'L1_attn_v_b', 'L1_attn_o_w',
        'L1_attn_o_b', 'L1_attn_ln1_w', 'L1_attn_ln1_b', 'L1_attn_ln2_w', 'L1_attn_ln2_b', 'L1_attn_dec_w',
        'L1_attn_dec_b', 'L1_attn_f1_w', 'L1_attn_f1_b', 'L1_attn_f2_w', 'L1_attn_f2_b', 'L1_ffn_w_router', 'L1_ffn_w1',
        'L1_ffn_w3', 'L1_ffn_w2', 'L1_ffn_sw1', 'L1_ffn_sw3', 'L1_ffn_sw2']
_OUTS = [((1, T, D), 'float32')]


def kernel(**inputs):
    import numpy as _np
    import concourse.bacc as _bacc
    from concourse import mybir as _mybir
    from concourse.bass_utils import run_bass_kernel_spmd as _run

    nc = _bacc.Bacc("TRN2", target_bir_lowering=False, num_devices=1)
    arrays, args = {}, {}
    for name in _INS:
        a = _np.ascontiguousarray(inputs[name])
        arrays[f"in_{name}_dram"] = a
        args[name] = nc.dram_tensor(f"in_{name}_dram", a.shape, _mybir.dt.from_np(a.dtype), kind="ExternalInput").ap()
    shape, dtype = _OUTS[0]
    out = nc.dram_tensor("out_0_dram", shape, _mybir.dt.from_np(_np.dtype(dtype)), kind="ExternalOutput").ap()
    macaron(nc, args, out)
    r = _run(nc, [arrays], core_ids=[0])
    return r.results[0]["out_0_dram"]
```

```python
import concourse.bass as bass
from concourse import mybir
from contextlib import ExitStack

F32 = mybir.dt.float32
BF16 = mybir.dt.bfloat16
ALU = mybir.AluOpType
ACT = mybir.ActivationFunctionType
AX = mybir.AxisListType

P = 128
D = 128
T = 2048
TILES = T // P
CHUNK = 512
CHUNKS = T // CHUNK
TPC = CHUNK // P
E = 8
TOPK = 2
HID0 = 128
SH0 = 256 // P
HID1 = 256 // P
H = 16
HD = D // H
FFN = 512 // P
LN_EPS = 1e-5
DEN_EPS = 1e-6
LAM_MIN = 1e-8

GH = 4
GROUPS = H // GH
PARTS = 3
ROWS = PARTS * PARTS * HD
ROWS_M = ROWS + PARTS * GH
VC = HD + 1
LEAD = 12
HOLE = 3
P_RING = 2


class Chain:

    def __init__(self, engine, sem, before=0):
        self.engine, self.sem, self.before, self.count = engine, sem, before, 0

    def __call__(self, instruction):
        self.count += 1
        instruction.then_inc(self.sem, 1)
        self.engine.wait_ge(self.sem, self.before + self.count)


class Machine:

    def __init__(self, nc, stack):
        self.nc, self.stack, self.calls = nc, stack, 0
        self.in_use, self.cleared, self.free = [], [], []

    def sb(self, name, shape, dt=F32, stack=None):
        return (stack or self.stack).enter_context(self.nc.sbuf_tensor(name, shape, dt))

    def sem(self, name):
        handle = self.free.pop() if self.free else self.stack.enter_context(self.nc.semaphore(f"{name}_{self.calls}"))
        self.in_use.append(handle)
        return handle

    def stage(self):
        self.calls += 1
        self.free += self.cleared
        for handle in self.in_use:
            self.nc.sync.sem_clear(handle)
        self.cleared, self.in_use = self.in_use, []
        return f"_{self.calls}"


def setup(m, w):
    nc = m.nc
    m.stage()
    loaded_x, loaded_t, loaded_w = m.sem("loaded_x"), m.sem("loaded_t"), m.sem("loaded_w")
    pool_steps, ident_ready = m.sem("pool_steps"), m.sem("ident_ready")
    turned, stored = m.sem("turned"), m.sem("stored")
    raw = [(w["L0_ffn_w1"].rearrange("e h d -> h e d"), E, m.w1T),
           (w["L0_ffn_w3"].rearrange("e h d -> h e d"), E, m.w3T),
           (w["L0_ffn_w2"].rearrange("e h d -> h e d"), E, m.w2T),
           (w["L0_ffn_sw1"].rearrange("(a p) d -> p a d", p=P), SH0, m.sw1T),
           (w["L0_ffn_sw2"].rearrange("(a p) d -> p a d", p=P), SH0, m.sw2T),
           (w["L0_ffn_sw3"].rearrange("d (a p) -> d a p", p=P), SH0, m.sw3T),
           (w["L0_attn_qkv_w"].rearrange("(a p) d -> p a d", p=P), 3, m.qkvT),
           (w["L0_attn_proj_w"].rearrange("(a p) d -> p a d", p=P), 1, m.projT)]
    n_raw = sum(n for _, n, _ in raw)
    with ExitStack() as stack:
        wraw = m.sb("wraw", [P, n_raw, D], stack=stack)
        graw = m.sb("graw", [E, D], stack=stack)
        braw = m.sb("braw", [m.bias_rows, D], stack=stack)
        block = stack.enter_context(nc.Block())

        @block.sync
        def _(sp):
            at = 0
            for src, n, _ in raw:
                sp.dma_start(wraw[:, at:at + n, :], src).then_inc(loaded_t, 16)
                at += n
            sp.dma_start(graw[:, :], w["L0_ffn_gate_w"]).then_inc(loaded_t, 16)
            at = 0
            for src, n in m.biases:
                sp.dma_start(braw[at:at + n, :], src).then_inc(loaded_t, 16)
                at += n
            sp.dma_start(m.X[:, :, :], w["L0_attn_x"][0].rearrange("(t p) d -> p t d", p=P)).then_inc(loaded_x, 16)
            sp.wait_ge(loaded_x, 16)

        @block.scalar
        def _(act):
            n = 0
            for dst, src in m.loads:
                act.dma_start(dst, src).then_inc(loaded_w, 16)
                n += 16
            act.wait_ge(loaded_w, n)

        @block.gpsimd
        def _(pool):
            step = Chain(pool, pool_steps)
            step(nc.gpsimd.memset(m.ident[:, :], 0.0))
            step(nc.gpsimd.affine_select(out=m.ident[:, :], in_=m.ident[:, :], compare_op=ALU.not_equal, fill=1.0,
                                         base=0, pattern=[[-1, P]], channel_multiplier=1))
            nc.gpsimd.tensor_copy(m.identb[:, :], m.ident[:, :]).then_inc(ident_ready, 1)
            nc.gpsimd.memset(m.neg_half[:, :], -0.5)
            nc.gpsimd.memset(m.euler[:, :], 2.718281828459045)
            nc.gpsimd.memset(m.cw[:, :, E:E + 1], 0.5)
            nc.gpsimd.memset(m.gT[:, :], 0.0)
            step(nc.gpsimd.memset(m.below[:, :, :], 1.0))
            step(nc.gpsimd.affine_select(out=m.below[:, :, :], in_=m.below[:, :, :], compare_op=ALU.is_gt, fill=0.0,
                                         base=0, pattern=[[1, E], [-1, E]], channel_multiplier=0))
            rows = PARTS + 1
            step(nc.gpsimd.memset(m.sel_gate[:, :, :], 1.0))
            step(nc.gpsimd.memset(m.sel_mask[:, :, :], 1.0))
            step(nc.gpsimd.affine_select(out=m.sel_gate[:, :, :], in_=m.sel_gate[:, :, :], compare_op=ALU.is_ge,
                                         fill=0.0, base=0, pattern=[[-rows, E], [0, P]], channel_multiplier=1))
            step(nc.gpsimd.affine_select(out=m.sel_gate[:, :, :], in_=m.sel_gate[:, :, :], compare_op=ALU.is_ge,
                                         fill=0.0, base=PARTS - 1, pattern=[[rows, E], [0, P]], channel_multiplier=-1))
            step(nc.gpsimd.affine_select(out=m.sel_mask[:, :, :], in_=m.sel_mask[:, :, :], compare_op=ALU.is_equal,
                                         fill=0.0, base=-PARTS, pattern=[[-rows, E], [0, P]], channel_multiplier=1))
            step(nc.gpsimd.memset(m.pick[:, :, :], 1.0))
            pick = m.pick[:, :, :].rearrange("p c (g v) -> p c g v", v=HD)
            step(nc.gpsimd.affine_select(out=pick, in_=pick, compare_op=ALU.is_ge, fill=0.0, base=0,
                                         pattern=[[0, HD], [-HD, H], [0, HD]], channel_multiplier=1))
            step(nc.gpsimd.affine_select(out=pick, in_=pick, compare_op=ALU.is_ge, fill=0.0, base=HD - 1,
                                         pattern=[[0, HD], [HD, H], [0, HD]], channel_multiplier=-1))
            step(nc.gpsimd.tensor_copy(m.same_head[:, :], m.pick[:, 0, :]))
            step(nc.gpsimd.affine_select(out=pick, in_=pick, compare_op=ALU.is_equal, fill=0.0, base=0,
                                         pattern=[[1, HD], [0, H], [-1, HD]], channel_multiplier=0))

        @block.tensor
        def _(pe):
            pe.wait_ge(ident_ready, 1)
            pe.wait_ge(loaded_t, 16 * (len(raw) + 1 + len(m.biases)))
            for i in range(0, n_raw, 4):
                if i // 4 >= 4:
                    pe.wait_ge(stored, i // 4 - 3)
                for j in range(i, min(i + 4, n_raw)):
                    last = nc.tensor.transpose(m.ps[:, i // 4 % 4, (j - i) * P:(j - i + 1) * P], wraw[:, j, :], m.ident[:, :])
                last.then_inc(turned, 1)
            nc.tensor.transpose(m.ps[:, 4, 0:E], graw[:, :], m.ident[0:E, 0:E]).then_inc(turned, 1)
            nb = m.bias_rows
            nc.tensor.transpose(m.ps[:, 5, 0:nb], braw[:, :], m.ident[0:nb, 0:nb]).then_inc(turned, 1)

        @block.vector
        def _(dve):
            for i in range(0, n_raw, 4):
                n = min(4, n_raw - i)
                dve.wait_ge(turned, i // 4 + 1)
                nc.vector.tensor_copy(m.wT[:, i:i + n, :], m.ps[:, i // 4 % 4, 0:n * P]).then_inc(stored, 1)
            dve.wait_ge(turned, (n_raw + 3) // 4 + 2)
            nc.vector.tensor_copy(m.gateT[:, :], m.ps[:, 4, 0:E]).then_inc(stored, 1)
            nc.vector.tensor_copy(m.biasT[:, :], m.ps[:, 5, 0:m.bias_rows]).then_inc(stored, 1)
            dve.wait_ge(loaded_w, 16 * len(m.loads))
            nc.vector.tensor_copy(m.dec_rep[:, :].rearrange("p (h k) -> p h k", k=HD),
                                  m.dec_w[:, :].unsqueeze(2).to_broadcast([P, H, HD]))
            for v in range(HD):
                nc.vector.tensor_copy(m.v_rep[:, v, :].rearrange("p (h k) -> p h k", k=HD),
                                      m.v_w[:, :].rearrange("p (h v) -> p h v", v=HD)[:, :, v:v + 1].to_broadcast([P, H, HD]))


def layer_norm(m, src, dst, scale=None, bias=None):
    nc = m.nc
    tag = m.stage()
    centred_sem, squared, var_ready, rstd_ready = m.sem("centred"), m.sem("squared"), m.sem("var_ready"), m.sem("rstd_ready")
    normed, turned, steps, stored = m.sem("normed"), m.sem("turned"), m.sem("ln_steps"), m.sem("xT_stored")
    with ExitStack() as stack:
        centred = m.sb("centred" + tag, [P, TILES, D], stack=stack)
        square = m.sb("square" + tag, [P, TILES, D], stack=stack)
        dst = centred if dst is None else dst
        total = m.sb("total" + tag, [P, TILES], stack=stack)
        mean = m.sb("mean" + tag, [P, TILES], stack=stack)
        total2 = m.sb("total2" + tag, [P, TILES], stack=stack)
        var = m.sb("var" + tag, [P, TILES], stack=stack)
        rstd = m.sb("rstd" + tag, [P, TILES], stack=stack)
        block = stack.enter_context(nc.Block())

        def tiles(c):
            return slice(c * TPC, (c + 1) * TPC)

        @block.vector
        def _(dve):
            step = Chain(dve, steps)
            for c in range(CHUNKS):
                t = tiles(c)
                step(nc.vector.reduce_sum(total[:, t], src[:, t, :], AX.X))
                step(nc.vector.tensor_scalar(mean[:, t], total[:, t], 1.0 / D, None, ALU.mult))
                nc.vector.tensor_tensor(centred[:, t, :], src[:, t, :], mean[:, t].unsqueeze(2).to_broadcast([P, TPC, D]),
                                        ALU.subtract).then_inc(centred_sem, 1)
            for c in range(CHUNKS):
                t = tiles(c)
                dve.wait_ge(squared, c + 1)
                step(nc.vector.reduce_sum(total2[:, t], square[:, t, :], AX.X))
                nc.vector.tensor_scalar(var[:, t], total2[:, t], 1.0 / D, LN_EPS, ALU.mult, ALU.add).then_inc(var_ready, 1)
            for c in range(CHUNKS):
                t = tiles(c)
                dve.wait_ge(rstd_ready, c + 1)
                nc.vector.tensor_tensor(dst[:, t, :], centred[:, t, :], rstd[:, t].unsqueeze(2).to_broadcast([P, TPC, D]),
                                        ALU.mult).then_inc(normed, 1)

        @block.gpsimd
        def _(pool):
            for c in range(CHUNKS):
                pool.wait_ge(var_ready, c + 1)
                nc.gpsimd.tensor_tensor(rstd[:, tiles(c)], var[:, tiles(c)], m.neg_half[:, 0:TPC], ALU.pow).then_inc(rstd_ready, 1)

        @block.tensor
        def _(pe):
            for c in range(CHUNKS):
                pe.wait_ge(normed, c + 1)
                for j in range(TPC):
                    last = nc.tensor.transpose(m.ps[:, c, j * P:(j + 1) * P], dst[:, c * TPC + j, :], m.ident[:, :])
                last.then_inc(turned, 1)

        @block.scalar
        def _(act):
            for c in range(CHUNKS):
                act.wait_ge(centred_sem, c + 1)
                nc.scalar.activation(square[:, tiles(c), :], centred[:, tiles(c), :], ACT.Square).then_inc(squared, 1)
            for c in range(CHUNKS):
                act.wait_ge(turned, c + 1)
                out = m.xT[:, c * CHUNK:(c + 1) * CHUNK]
                if scale is None:
                    nc.scalar.activation(out, m.ps[:, c, :], ACT.Copy).then_inc(stored, 1)
                else:
                    nc.scalar.activation(out, m.ps[:, c, :], ACT.Identity, bias=bias, scale=scale).then_inc(stored, 1)
            act.wait_ge(stored, CHUNKS)


class Prepare:

    STEPS_NORM = 3
    STEPS_ROUTE = (11, 5, 5)

    def __init__(self, m, stack, gate, pair, bank_turn, bank_route):
        self.m, self.gate, self.pair = m, gate, pair
        self.turn, self.route = bank_turn, bank_route
        tag = f"_{m.calls}"
        self.s_centred = m.sem("centred")
        self.s_squared = m.sem("squared")
        self.s_var_ready = m.sem("var_ready")
        self.s_rstd_ready = m.sem("rstd_ready")
        self.s_normed = m.sem("normed")
        self.s_turned = m.sem("turned")
        self.s_xT_ready = m.sem("xT_ready")
        self.s_logits_ready = m.sem("logits_ready")
        self.s_shifted = m.sem("shifted")
        self.s_exped = m.sem("exped")
        self.s_packed_ready = m.sem("packed_ready")
        self.s_gates_turned = m.sem("gates_turned")
        self.s_gates_ready = m.sem("gates_ready")
        self.s_norm_steps = m.sem("norm_steps")
        self.s_route_steps = m.sem("route_steps")
        self.total = m.sb("total" + tag, [P, TPC], stack=stack)
        self.mean = m.sb("mean" + tag, [P, TPC], stack=stack)
        self.centred = m.sb("centred" + tag, [P, TPC, D], stack=stack)
        self.square = m.sb("square" + tag, [P, TPC, D], stack=stack)
        self.total2 = m.sb("total2" + tag, [P, TPC], stack=stack)
        self.var = m.sb("var" + tag, [P, TPC], stack=stack)
        self.rstd = m.sb("rstd" + tag, [P, TPC], stack=stack)
        self.norm = m.sb("norm" + tag, [P, TPC, D], stack=stack)
        self.xs = m.sb("xs" + tag, [P, CHUNK], stack=stack)
        self.top = m.sb("top" + tag, [P, TPC], stack=stack)
        self.z = m.sb("z" + tag, [P, TPC * E], stack=stack)
        self.ez = m.sb("ez" + tag, [P, TPC * E], stack=stack)
        self.sum = m.sb("sum" + tag, [P, TPC], stack=stack)
        self.inv = m.sb("inv" + tag, [P, TPC], stack=stack)
        self.inv2 = m.sb("inv2" + tag, [P, TPC], stack=stack)
        self.score = m.sb("score" + tag, [P, TPC, E], stack=stack)
        self.higher = m.sb("higher" + tag, [P, TPC, E, E], stack=stack)
        self.equal = m.sb("equal" + tag, [P, TPC, E, E], stack=stack)
        self.tied = m.sb("tied" + tag, [P, TPC, E, E], stack=stack)
        self.outranked = m.sb("outranked" + tag, [P, TPC, E, E], stack=stack)
        self.rank = m.sb("rank" + tag, [P, TPC, E], stack=stack)
        self.mask = m.sb("mask" + tag, [P, TPC, E], stack=stack)
        self.gates = m.sb("gates" + tag, [P, TPC, E], stack=stack)
        self.rest = m.sb("rest" + tag, [P, TPC, E], stack=stack)
        self.rest2 = m.sb("rest2" + tag, [P, TPC, E], stack=stack)
        self.packed = m.sb("packed" + tag, [P, TPC, E, PARTS + 1], BF16, stack=stack)


    def sums(self, dve, c):
        nc, m = self.m.nc, self.m
        step = Chain(dve, self.s_norm_steps, c * self.STEPS_NORM)
        x = m.X[:, bass.ts(c, TPC), :]
        step(nc.vector.reduce_sum(self.total[:, :], x, AX.X))
        step(nc.vector.tensor_scalar(self.mean[:, :], self.total[:, :], 1.0 / D, None, ALU.mult))
        nc.vector.tensor_tensor(self.centred[:, :, :], x, self.mean[:, :].unsqueeze(2).to_broadcast([P, TPC, D]),
                                ALU.subtract).then_inc(self.s_centred, 1)

    def variances(self, dve, c):
        nc = self.m.nc
        step = Chain(dve, self.s_norm_steps, c * self.STEPS_NORM + 2)
        dve.wait_ge(self.s_squared, c + 1)
        step(nc.vector.reduce_sum(self.total2[:, :], self.square[:, :, :], AX.X))
        nc.vector.tensor_scalar(self.var[:, :], self.total2[:, :], 1.0 / D, LN_EPS, ALU.mult, ALU.add)\
            .then_inc(self.s_var_ready, 1)

    def normalise(self, dve, c):
        nc = self.m.nc
        dve.wait_ge(self.s_rstd_ready, c + 1)
        nc.vector.tensor_tensor(self.norm[:, :, :], self.centred[:, :, :],
                                self.rstd[:, :].unsqueeze(2).to_broadcast([P, TPC, D]), ALU.mult).then_inc(self.s_normed, 1)

    def over_e(self, a):
        return a[:, :].unsqueeze(2).to_broadcast([P, TPC, E])

    def shift(self, dve, c):
        nc, m = self.m.nc, self.m
        step = Chain(dve, self.s_route_steps, c * self.route_steps())
        logits = m.ps[:, self.route, 0:TPC * E].rearrange("p (t e) -> p t e", e=E)
        dve.wait_ge(self.s_logits_ready, c + 1)
        step(nc.vector.reduce_max(self.top[:, :], logits, AX.X))
        nc.vector.tensor_tensor(self.z[:, :].rearrange("p (t e) -> p t e", e=E), logits, self.over_e(self.top),
                                ALU.subtract).then_inc(self.s_shifted, 1)

    def route_steps(self):
        return self.STEPS_ROUTE[0] + self.STEPS_ROUTE[1 if self.pair else 2]

    def compare(self, dve, c):
        nc, m = self.m.nc, self.m
        step = Chain(dve, self.s_route_steps, c * self.route_steps() + 1)
        dve.wait_ge(self.s_exped, c + 1)
        ez = self.ez[:, :].rearrange("p (t e) -> p t e", e=E)
        step(nc.vector.reduce_sum(self.sum[:, :], ez, AX.X))
        step(nc.vector.reciprocal(self.inv[:, :], self.sum[:, :]))
        step(nc.vector.tensor_tensor(self.score[:, :, :], ez, self.over_e(self.inv), ALU.mult))
        f_side = self.score[:, :, :].unsqueeze(2).to_broadcast([P, TPC, E, E])
        e_side = self.score[:, :, :].unsqueeze(3).to_broadcast([P, TPC, E, E])
        step(nc.vector.tensor_tensor(self.higher[:, :, :, :], f_side, e_side, ALU.is_gt))
        step(nc.vector.tensor_tensor(self.equal[:, :, :, :], f_side, e_side, ALU.is_equal))

    def rank_gates(self, dve, c):
        nc, m = self.m.nc, self.m
        step = Chain(dve, self.s_route_steps, c * self.route_steps() + 6)
        below = m.below[:, :, :].rearrange("p e f -> p (e f)").unsqueeze(1).to_broadcast([P, TPC, E * E])
        flat = "p t e f -> p t (e f)"
        step(nc.vector.tensor_tensor(self.tied[:, :, :, :].rearrange(flat), self.equal[:, :, :, :].rearrange(flat), below,
                                     ALU.mult))
        step(nc.vector.tensor_tensor(self.outranked[:, :, :, :], self.higher[:, :, :, :], self.tied[:, :, :, :], ALU.add))
        step(nc.vector.reduce_sum(self.rank[:, :, :], self.outranked[:, :, :, :], AX.X))
        step(nc.vector.tensor_scalar(self.mask[:, :, :], self.rank[:, :, :], TOPK - 0.5, None, ALU.is_lt))
        step(nc.vector.tensor_tensor(self.gates[:, :, :], self.score[:, :, :], self.mask[:, :, :], ALU.mult))

    def pack(self, dve, c):
        nc, m = self.m.nc, self.m
        step = Chain(dve, self.s_route_steps, c * self.route_steps() + 11)
        if self.pair:
            if not isinstance(c, int):
                dve.wait_ge(self.s_gates_turned, c)
            step(nc.vector.tensor_copy(self.packed[:, :, :, 0], self.gates[:, :, :]))
            step(nc.vector.tensor_tensor(self.rest[:, :, :], self.gates[:, :, :], self.packed[:, :, :, 0], ALU.subtract))
            step(nc.vector.tensor_copy(self.packed[:, :, :, 1], self.rest[:, :, :]))
            step(nc.vector.tensor_tensor(self.rest2[:, :, :], self.rest[:, :, :], self.packed[:, :, :, 1], ALU.subtract))
            step(nc.vector.tensor_copy(self.packed[:, :, :, 2], self.rest2[:, :, :]))
            nc.vector.tensor_copy(self.packed[:, :, :, 3], self.mask[:, :, :]).then_inc(self.s_packed_ready, 1)
        else:
            step(nc.vector.reduce_sum(self.sum[:, :], self.gates[:, :, :], AX.X))
            step(nc.vector.reciprocal(self.inv[:, :], self.sum[:, :]))
            step(nc.vector.tensor_scalar(self.inv2[:, :], self.inv[:, :], 0.5, None, ALU.mult))
            step(nc.vector.tensor_tensor(self.rest[:, :, :], self.gates[:, :, :], self.over_e(self.inv2), ALU.mult))
            step(nc.vector.tensor_copy(m.cw[:, bass.ts(c, TPC), 0:E], self.rest[:, :, :]))

    def store_gates(self, dve, c):
        nc, m = self.m.nc, self.m
        rows = E * (PARTS + 1)
        dve.wait_ge(self.s_gates_turned, c + 1)
        nc.vector.tensor_copy(m.gT[0:rows, bass.ts(c, CHUNK)], m.ps[0:rows, self.route, :].bitcast(BF16)[:, 0:CHUNK])\
            .then_inc(self.s_gates_ready, 1)


    def squares(self, act, c):
        act.wait_ge(self.s_centred, c + 1)
        self.m.nc.scalar.activation(self.square[:, :, :], self.centred[:, :, :], ACT.Square).then_inc(self.s_squared, 1)

    def store_xT(self, act, c):
        nc, m = self.m.nc, self.m
        act.wait_ge(self.s_turned, c + 1)
        if not isinstance(c, int):
            act.wait_ge(self.s_logits_ready, c)
        nc.scalar.activation(self.xs[:, :], m.ps[:, self.turn, :], ACT.Copy).then_inc(self.s_xT_ready, 1)
        nc.scalar.activation(m.xT[:, bass.ts(c, CHUNK)], m.ps[:, self.turn, :], ACT.Copy).then_inc(self.s_xT_ready, 1)

    def first_exps(self, act):
        act.wait_ge(self.s_shifted, 1)
        self.m.nc.scalar.activation(self.ez[:, :], self.z[:, :], ACT.Exp).then_inc(self.s_exped, 1)


    def rstds(self, pool, c):
        pool.wait_ge(self.s_var_ready, c + 1)
        self.m.nc.gpsimd.tensor_tensor(self.rstd[:, :], self.var[:, :], self.m.neg_half[:, 0:TPC], ALU.pow)\
            .then_inc(self.s_rstd_ready, 1)

    def exps(self, pool, c):
        pool.wait_ge(self.s_shifted, c + 1)
        self.m.nc.gpsimd.tensor_tensor(self.ez[:, :], self.m.euler[:, :], self.z[:, :], ALU.pow).then_inc(self.s_exped, 1)


    def transpose(self, pe, c):
        nc, m = self.m.nc, self.m
        pe.wait_ge(self.s_normed, c + 1)
        if not isinstance(c, int):
            pe.wait_ge(self.s_xT_ready, c * 2)
        for j in range(TPC):
            last = nc.tensor.transpose(m.ps[:, self.turn, j * P:(j + 1) * P], self.norm[:, j, :], m.ident[:, :])
        last.then_inc(self.s_turned, 1)

    def logits(self, pe, c):
        nc, m = self.m.nc, self.m
        pe.wait_ge(self.s_xT_ready, c * 2 + 1)
        for j in range(TPC):
            last = nc.tensor.matmul(m.ps[:, self.route, j * E:(j + 1) * E], self.xs[:, j * P:(j + 1) * P], self.gate[:, :],
                                    start=True, stop=True)
        last.then_inc(self.s_logits_ready, 1)

    def transpose_gates(self, pe, c):
        nc, m = self.m.nc, self.m
        rows = E * (PARTS + 1)
        pe.wait_ge(self.s_packed_ready, c + 1)
        for j in range(TPC):
            last = nc.tensor.transpose(m.ps[0:rows, self.route, :].bitcast(BF16)[:, j * P:(j + 1) * P],
                                       self.packed[:, j, :, :].rearrange("p e r -> p (e r)"), m.identb[:, :])
        last.then_inc(self.s_gates_turned, 1)


def moe0(m):
    nc = m.nc
    tag = m.stage()
    bc_ready, xg_ready, up_ready, x3_ready = m.sem("bc_ready"), m.sem("xg_ready"), m.sem("up_ready"), m.sem("x3_ready")
    mask_bc = m.sem("mask_bc")
    hid_ready, x3b_ready, x3m_ready, y_ready = m.sem("hid_ready"), m.sem("x3b_ready"), m.sem("x3m_ready"), m.sem("y_ready")
    prod_ready, summed, sh_silu, sh_hid = m.sem("prod_ready"), m.sem("summed"), m.sem("sh_silu"), m.sem("sh_hid")
    sh_a, sh_b, sh_out, first_sum = m.sem("sh_a"), m.sem("sh_b"), m.sem("sh_out"), m.sem("first_sum")
    y_turned, x_updated = m.sem("y_turned"), m.sem("x_updated")
    GB, MB, HB, TB, YB, ZB, NB = [0, 1], 2, 3, 4, 5, 6, 7
    with ExitStack() as stack:
        xg = m.sb("xg" + tag, [P, 2, CHUNK], stack=stack)
        hid = m.sb("hid" + tag, [P, 2, CHUNK], stack=stack)
        x3b = m.sb("x3b" + tag, [P, 2, CHUNK], stack=stack)
        x3m = m.sb("x3m" + tag, [P, 2, CHUNK], stack=stack)
        prod = m.sb("prod" + tag, [P, 2, CHUNK], stack=stack)
        acc = m.sb("acc" + tag, [P, 2, CHUNK], stack=stack)
        shs = m.sb("shs" + tag, [P, SH0, CHUNK], stack=stack)
        shh = m.sb("shh" + tag, [P, SH0, CHUNK], stack=stack)
        prep = Prepare(m, stack, m.gateT, True, NB, ZB)
        block = stack.enter_context(nc.Block())

        @block.tensor
        def _(pe):
            def broadcast_gate(c, e):
                if e >= 2:
                    pe.wait_ge(xg_ready, c * E + (e - 1))
                nc.tensor.matmul(m.ps[:, GB[e % 2], :], m.sel_gate[:, e, :], m.gT[:, bass.ts(c, CHUNK)],
                                 start=True, stop=True).then_inc(bc_ready, 1)

            def broadcast_mask(c, e):
                if e >= 1:
                    pe.wait_ge(x3m_ready, c * E + e)
                elif not isinstance(c, int) or c > 0:
                    pe.wait_ge(x_updated, c)
                nc.tensor.matmul(m.ps[:, MB, :], m.sel_mask[:, e, :], m.gT[:, bass.ts(c, CHUNK)],
                                 start=True, stop=True).then_inc(mask_bc, 1)

            def down(c, e):
                pe.wait_ge(hid_ready, c * E + (e + 1))
                if e >= 1:
                    pe.wait_ge(prod_ready, c * E + e)
                nc.tensor.matmul(m.ps[:, YB, :], m.w2T[:, e, :], hid[:, e % 2, :], start=True, stop=True)\
                    .then_inc(y_ready, 1)

            def head(c, first=False):
                x_c = m.xT[:, bass.ts(c, CHUNK)]
                pe.wait_ge(prep.s_xT_ready, c * 2 + 2)
                for i in range(SH0):
                    if i >= 1:
                        pe.wait_ge(sh_silu, c * SH0 + i)
                    elif not first:
                        pe.wait_ge(hid_ready, c * E)
                    nc.tensor.matmul(m.ps[:, HB, :], m.sw1T[:, i, :], x_c, start=True, stop=True).then_inc(sh_a, 1)
                    if first and i == 0:
                        prep.logits(pe, c)
                    if i >= 1:
                        prep.transpose_gates(pe, c)
                        pe.wait_ge(sh_hid, c * SH0 + i)
                    elif not first:
                        pe.wait_ge(x3b_ready, c * E)
                    nc.tensor.matmul(m.ps[:, TB, :], m.sw2T[:, i, :], x_c, start=True, stop=True).then_inc(sh_b, 1)
                pe.wait_ge(prep.s_gates_ready, c + 1)
                if not first:
                    pe.wait_ge(xg_ready, c * E)
                broadcast_gate(c, 0)

            def turn_back(c):
                pe.wait_ge(summed, c * (E - 1) + (E - 1))
                pe.wait_ge(x3m_ready, c * E + E)
                for j in range(TPC):
                    last = nc.tensor.transpose(m.ps[:, MB, j * P:(j + 1) * P], acc[:, (E - 1) % 2, j * P:(j + 1) * P],
                                               m.ident[:, :])
                last.then_inc(y_turned, 1)

            def chunk(c, more):
                for e in range(E):
                    if e + 1 < E:
                        broadcast_gate(c, e + 1)
                    if e == 0:
                        pe.wait_ge(sh_silu, c * SH0 + SH0)
                    else:
                        pe.wait_ge(hid_ready, c * E + e)
                    pe.wait_ge(xg_ready, c * E + (e + 1))
                    nc.tensor.matmul(m.ps[:, HB, :], m.w1T[:, e, :], xg[:, e % 2, :], start=True, stop=True)\
                        .then_inc(up_ready, 1)
                    if e == 0:
                        pe.wait_ge(sh_hid, c * SH0 + SH0)
                    else:
                        pe.wait_ge(x3b_ready, c * E + e)
                    nc.tensor.matmul(m.ps[:, TB, :], m.w3T[:, e, :], xg[:, e % 2, :], start=True, stop=True)\
                        .then_inc(x3_ready, 1)
                    broadcast_mask(c, e)
                    if e == 0:
                        for i in range(SH0):
                            last = nc.tensor.matmul(m.ps[:, ZB, :], m.sw3T[:, i, :], shh[:, i, :],
                                                    start=(i == 0), stop=(i == SH0 - 1))
                        last.then_inc(sh_out, 1)
                    else:
                        down(c, e - 1)
                    if more and e == 3:
                        prep.transpose(pe, c + 1)
                    if more and e == 4:
                        pe.wait_ge(first_sum, c + 1)
                        prep.logits(pe, c + 1)
                down(c, E - 1)
                if more:
                    head(c + 1)
                turn_back(c)

            prep.transpose(pe, 0)
            head(0, True)
            with pe.Fori(0, CHUNKS - 1) as c:
                chunk(c, True)
            chunk(CHUNKS - 1, False)

        @block.scalar
        def _(act):
            def head(c):
                for i in range(SH0):
                    act.wait_ge(sh_a, c * SH0 + (i + 1))
                    nc.scalar.activation(shs[:, i, :], m.ps[:, HB, :], ACT.Silu).then_inc(sh_silu, 1)

            def chunk(c, more):
                for e in range(E):
                    act.wait_ge(up_ready, c * E + (e + 1))
                    if e >= 2:
                        act.wait_ge(y_ready, c * E + (e - 1))
                    nc.scalar.activation(hid[:, e % 2, :], m.ps[:, HB, :], ACT.Silu, bias=m.b1[:, e:e + 1])\
                        .then_inc(hid_ready, 1)
                    act.wait_ge(x3_ready, c * E + (e + 1))
                    if e >= 2:
                        act.wait_ge(x3m_ready, c * E + (e - 1))
                    nc.scalar.activation(x3b[:, e % 2, :], m.ps[:, TB, :], ACT.Identity, bias=m.b3[:, e:e + 1])\
                        .then_inc(x3b_ready, 1)
                    if more and e == 0:
                        prep.squares(act, c + 1)
                    if more and e == 3:
                        prep.store_xT(act, c + 1)
                if more:
                    head(c + 1)

            prep.squares(act, 0)
            prep.store_xT(act, 0)
            prep.first_exps(act)
            head(0)
            with act.Fori(0, CHUNKS - 1) as c:
                chunk(c, True)
            chunk(CHUNKS - 1, False)

        @block.vector
        def _(dve):
            def gate_x(c, e):
                dve.wait_ge(bc_ready, c * E + (e + 1))
                if e >= 2:
                    dve.wait_ge(x3_ready, c * E + (e - 1))
                nc.vector.tensor_tensor(xg[:, e % 2, :], m.ps[:, GB[e % 2], :], m.xT[:, bass.ts(c, CHUNK)], ALU.mult)\
                    .then_inc(xg_ready, 1)

            def mask_x3(c, e):
                dve.wait_ge(x3b_ready, c * E + (e + 1))
                dve.wait_ge(mask_bc, c * E + (e + 1))
                if e >= 2:
                    dve.wait_ge(prod_ready, c * E + (e - 1))
                nc.vector.tensor_tensor(x3m[:, e % 2, :], m.ps[:, MB, :], x3b[:, e % 2, :], ALU.mult)\
                    .then_inc(x3m_ready, 1)

            def product(c, e):
                dve.wait_ge(y_ready, c * E + (e + 1))
                dve.wait_ge(x3m_ready, c * E + (e + 1))
                if e >= 2:
                    dve.wait_ge(summed, c * (E - 1) + max(1, e - 2))
                nc.vector.scalar_tensor_tensor(out=prod[:, e % 2, :], in0=m.ps[:, YB, :], scalar=m.b2[:, e:e + 1],
                                               in1=x3m[:, e % 2, :], op0=ALU.add, op1=ALU.mult).then_inc(prod_ready, 1)

            def head(c):
                for i in range(SH0):
                    dve.wait_ge(sh_b, c * SH0 + (i + 1))
                    dve.wait_ge(sh_silu, c * SH0 + (i + 1))
                    nc.vector.tensor_tensor(shh[:, i, :], m.ps[:, TB, :], shs[:, i, :], ALU.mult).then_inc(sh_hid, 1)
                    if i == 0:
                        prep.store_gates(dve, c)
                gate_x(c, 0)

            def update(c):
                dve.wait_ge(y_turned, c + 1)
                x_t = m.X[:, bass.ts(c, TPC), :].rearrange("p t d -> p (t d)")
                nc.vector.scalar_tensor_tensor(out=x_t, in0=m.ps[:, MB, :], scalar=0.5, in1=x_t,
                                               op0=ALU.mult, op1=ALU.add).then_inc(x_updated, 1)

            def chunk(c, more):
                for e in range(E):
                    if e + 1 < E:
                        gate_x(c, e + 1)
                    mask_x3(c, e)
                    if e >= 1:
                        product(c, e - 1)
                    if e == 1:
                        dve.wait_ge(prod_ready, c * E + 1)
                        dve.wait_ge(sh_out, c + 1)
                        nc.vector.tensor_tensor(acc[:, 0, :], m.ps[:, ZB, :], prod[:, 0, :], ALU.add).then_inc(first_sum, 1)
                    if more:
                        if e == 0:
                            prep.sums(dve, c + 1)
                        if e == 1:
                            prep.variances(dve, c + 1)
                        if e == 2:
                            prep.normalise(dve, c + 1)
                        if e == 4:
                            prep.shift(dve, c + 1)
                        if e == 6:
                            prep.compare(dve, c + 1)
                        if e == 7:
                            prep.rank_gates(dve, c + 1)
                            prep.pack(dve, c + 1)
                product(c, E - 1)
                if more:
                    head(c + 1)
                update(c)

            prep.sums(dve, 0)
            prep.variances(dve, 0)
            prep.normalise(dve, 0)
            prep.shift(dve, 0)
            prep.compare(dve, 0)
            prep.rank_gates(dve, 0)
            prep.pack(dve, 0)
            head(0)
            with dve.Fori(0, CHUNKS - 1) as c:
                chunk(c, True)
            chunk(CHUNKS - 1, False)

        @block.gpsimd
        def _(pool):
            def chunk(c, more):
                for e in range(1, E):
                    pool.wait_ge(prod_ready, c * E + (e + 1))
                    if e == 1:
                        pool.wait_ge(first_sum, c + 1)
                    else:
                        pool.wait_ge(summed, c * (E - 1) + (e - 1))
                    nc.gpsimd.tensor_tensor(acc[:, e % 2, :], acc[:, (e - 1) % 2, :], prod[:, e % 2, :], ALU.add)\
                        .then_inc(summed, 1)
                    if more and e == 1:
                        prep.rstds(pool, c + 1)
                    if more and e == 3:
                        prep.exps(pool, c + 1)

            prep.rstds(pool, 0)
            with pool.Fori(0, CHUNKS - 1) as c:
                chunk(c, True)
            chunk(CHUNKS - 1, False)


def moe1(m):
    nc = m.nc
    tag = m.stage()
    NE = E + 1
    a_ready, b_ready, silu_done, hid_ready = m.sem("a_ready"), m.sem("b_ready"), m.sem("silu_done"), m.sem("hid_ready")
    y_ready, y_used = m.sem("y_ready"), m.sem("y_used")
    AB, BB, YB, NB, RB = [0, 1], [2, 3], [4, 5], 6, 7
    with ExitStack() as stack:
        silu = m.sb("silu" + tag, [P, HID1, CHUNK], stack=stack)
        hid = m.sb("hid1" + tag, [P, 2, HID1, CHUNK], stack=stack)
        prep = Prepare(m, stack, m.router, False, NB, RB)
        block = stack.enter_context(nc.Block())

        @block.tensor
        def _(pe):
            prep.transpose(pe, 0)
            prep.logits(pe, 0)

            def chunk(c, more):
                x_c = m.xT[:, bass.ts(c, CHUNK)]

                def down(e):
                    pe.wait_ge(hid_ready, c * (NE * HID1) + HID1 * (e + 1))
                    if e >= 2:
                        pe.wait_ge(y_used, c * NE + (e - 1))
                    for j in range(TPC):
                        for i in range(HID1):
                            last = nc.tensor.matmul(m.ps[:, YB[e % 2], j * P:(j + 1) * P],
                                                    hid[:, e % 2, i, j * P:(j + 1) * P], m.ew2[:, e, i, :],
                                                    start=(i == 0), stop=(i == HID1 - 1))
                    last.then_inc(y_ready, 1)

                pe.wait_ge(prep.s_xT_ready, c * 2 + 2)
                for e in range(NE):
                    for i in range(HID1):
                        if e >= 1:
                            pe.wait_ge(silu_done, c * (NE * HID1) + ((e - 1) * HID1 + i + 1))
                        nc.tensor.matmul(m.ps[:, AB[i], :], m.ew1[:, e, i * P:(i + 1) * P], x_c, start=True, stop=True)\
                            .then_inc(a_ready, 1)
                        if e >= 1:
                            pe.wait_ge(hid_ready, c * (NE * HID1) + ((e - 1) * HID1 + i + 1))
                        nc.tensor.matmul(m.ps[:, BB[i], :], m.ew3[:, e, i * P:(i + 1) * P], x_c, start=True, stop=True)\
                            .then_inc(b_ready, 1)
                    if e >= 1:
                        down(e - 1)
                    if more and e == 3:
                        prep.transpose(pe, c + 1)
                    if more and e == 4:
                        prep.logits(pe, c + 1)
                down(NE - 1)
                pe.wait_ge(y_used, c * NE + (NE - 1))

            with pe.Fori(0, CHUNKS - 1) as c:
                chunk(c, True)
            chunk(CHUNKS - 1, False)

        @block.scalar
        def _(act):
            prep.squares(act, 0)
            prep.store_xT(act, 0)
            prep.first_exps(act)

            def chunk(c, more):
                for e in range(NE):
                    for i in range(HID1):
                        act.wait_ge(a_ready, c * (NE * HID1) + (e * HID1 + i + 1))
                        if e >= 1:
                            act.wait_ge(hid_ready, c * (NE * HID1) + ((e - 1) * HID1 + i + 1))
                        nc.scalar.activation(silu[:, i, :], m.ps[:, AB[i], :], ACT.Silu).then_inc(silu_done, 1)
                    if more and e == 0:
                        prep.squares(act, c + 1)
                    if more and e == 3:
                        prep.store_xT(act, c + 1)

            with act.Fori(0, CHUNKS - 1) as c:
                chunk(c, True)
            chunk(CHUNKS - 1, False)

        @block.vector
        def _(dve):
            prep.sums(dve, 0)
            prep.variances(dve, 0)
            prep.normalise(dve, 0)
            prep.shift(dve, 0)
            prep.compare(dve, 0)
            prep.rank_gates(dve, 0)
            prep.pack(dve, 0)

            def chunk(c, more):
                x_t = m.X[:, bass.ts(c, TPC), :]
                cw = m.cw[:, bass.ts(c, TPC), :]

                def add(e):
                    dve.wait_ge(y_ready, c * NE + (e + 1))
                    if e >= 1:
                        dve.wait_ge(y_used, c * NE + e)
                    for j in range(TPC):
                        last = nc.vector.scalar_tensor_tensor(out=x_t[:, j, :], in0=m.ps[:, YB[e % 2], j * P:(j + 1) * P],
                                                              scalar=cw[:, j, e:e + 1], in1=x_t[:, j, :],
                                                              op0=ALU.mult, op1=ALU.add)
                    last.then_inc(y_used, 1)

                for e in range(NE):
                    for i in range(HID1):
                        dve.wait_ge(b_ready, c * (NE * HID1) + (e * HID1 + i + 1))
                        dve.wait_ge(silu_done, c * (NE * HID1) + (e * HID1 + i + 1))
                        if e >= 2:
                            dve.wait_ge(y_ready, c * NE + (e - 1))
                        nc.vector.tensor_tensor(hid[:, e % 2, i, :], m.ps[:, BB[i], :], silu[:, i, :], ALU.mult)\
                            .then_inc(hid_ready, 1)
                    if e >= 1:
                        add(e - 1)
                    if more:
                        if e == 0:
                            prep.sums(dve, c + 1)
                        if e == 1:
                            prep.variances(dve, c + 1)
                        if e == 2:
                            prep.normalise(dve, c + 1)
                        if e == 5:
                            prep.shift(dve, c + 1)
                        if e == 6:
                            prep.compare(dve, c + 1)
                        if e == 7:
                            prep.rank_gates(dve, c + 1)
                        if e == 8:
                            prep.pack(dve, c + 1)
                add(NE - 1)

            with dve.Fori(0, CHUNKS - 1) as c:
                chunk(c, True)
            chunk(CHUNKS - 1, False)

        @block.gpsimd
        def _(pool):
            prep.rstds(pool, 0)
            for c in range(1, CHUNKS):
                prep.rstds(pool, c)
                prep.exps(pool, c)


def softmax_attention(m, w):
    nc = m.nc
    tag = m.stage()
    scale = float(HD) ** -0.5
    dram_q = nc.dram_tensor("q_parts", [PARTS, D, T], BF16, kind="Internal").ap()
    dram_k = nc.dram_tensor("k_parts", [PARTS, D, T], BF16, kind="Internal").ap()
    kv_stack = ExitStack()
    values = m.sb("values", [P, GROUPS, TILES, GH, VC], stack=kv_stack)

    proj, f32_ready, hi_ready, steps = m.sem("proj"), m.sem("f32_ready"), m.sem("hi_ready"), m.sem("part_steps")
    parts_ready, parts_out, v_ready, v_stored = m.sem("parts_ready"), [m.sem("parts_out0"), m.sem("parts_out1")], m.sem("v_ready"), m.sem("v_stored")
    ones_set = m.sem("ones_set")
    sides = [(0, scale, dram_q), (1, 1.0, dram_k)]
    jobs = [(s, c) for c in range(CHUNKS) for s in range(2)]
    with ExitStack() as stack:
        full = m.sb("full" + tag, [P, 2, CHUNK], stack=stack)
        rest = m.sb("rest" + tag, [P, CHUNK], stack=stack)
        part = m.sb("part" + tag, [P, 2, PARTS, CHUNK], BF16, stack=stack)
        block = stack.enter_context(nc.Block())

        @block.tensor
        def _(pe):
            for n, (s, c) in enumerate(jobs):
                if n >= 2:
                    pe.wait_ge(hi_ready, n - 1)
                nc.tensor.matmul(m.ps[:, n % 2, :], m.qkvT[:, s, :], m.xT[:, c * CHUNK:(c + 1) * CHUNK],
                                 start=True, stop=True).then_inc(proj, 1)
                if n % 2 == 1:
                    for j in range(TPC):
                        t = c * TPC + j
                        last = nc.tensor.matmul(m.ps[:, 2 + c, j * P:(j + 1) * P], m.xT[:, t * P:(t + 1) * P],
                                                m.qkvT[:, 2, :], start=True, stop=True)
                    last.then_inc(v_ready, 1)

        @block.scalar
        def _(act):
            for n, (s, c) in enumerate(jobs):
                act.wait_ge(proj, n + 1)
                if n >= 2:
                    act.wait_ge(parts_ready, n - 1)
                nc.scalar.activation(full[:, n % 2, :], m.ps[:, n % 2, :], ACT.Identity, bias=m.qk_bias[:, s:s + 1],
                                     scale=sides[s][1]).then_inc(f32_ready, 1)
                act.wait_ge(f32_ready, n + 1)
                if n >= 2:
                    act.wait_ge(parts_out[n % 2], 16 * (n // 2))
                nc.scalar.activation(part[:, n % 2, 0, :], full[:, n % 2, :], ACT.Copy).then_inc(hi_ready, 1)

        @block.vector
        def _(dve):
            step = Chain(dve, steps)
            nc.vector.memset(values[:, :, :, :, HD:VC], 1.0).then_inc(ones_set, 1)
            for n, (s, c) in enumerate(jobs):
                dve.wait_ge(hi_ready, n + 1)
                if n >= 2:
                    dve.wait_ge(parts_out[n % 2], 16 * (n // 2))
                step(nc.vector.tensor_tensor(rest[:, :], full[:, n % 2, :], part[:, n % 2, 0, :], ALU.subtract))
                step(nc.vector.tensor_copy(part[:, n % 2, 1, :], rest[:, :]))
                nc.vector.tensor_tensor(part[:, n % 2, 2, :], rest[:, :], part[:, n % 2, 1, :], ALU.subtract)\
                    .then_inc(parts_ready, 1)
                dve.wait_ge(parts_ready, n + 1)
                if n % 2 == 1:
                    dve.wait_ge(v_ready, c + 1)
                    for j in range(TPC):
                        nc.vector.tensor_tensor(
                            values[:, :, c * TPC + j, :, 0:HD],
                            m.ps[:, 2 + c, j * P:(j + 1) * P].rearrange("p (g h e) -> p g h e", h=GH, e=HD),
                            m.v_bias[:, :].rearrange("p (g h e) -> p g h e", h=GH, e=HD), ALU.add).then_inc(v_stored, 1)

        @block.sync
        def _(sp):
            for n, (s, c) in enumerate(jobs):
                sp.wait_ge(parts_ready, n + 1)
                sp.dma_start(sides[s][2][:, :, c * CHUNK:(c + 1) * CHUNK].rearrange("i p t -> p i t"),
                             part[:, n % 2, :, :]).then_inc(parts_out[n % 2], 16)
            for i in range(2):
                sp.wait_ge(parts_out[i], 16 * len(jobs) // 2)

    m.stage()
    UNITS = GROUPS * CHUNKS
    STEPS = TILES * GH
    PAIRS = STEPS // 2
    q_loaded = [m.sem(f"q_loaded{i}") for i in range(CHUNKS)]
    k1_loaded = [m.sem(f"k1_loaded{i}") for i in range(GH)]
    k2_loaded = [m.sem(f"k2_loaded{i}") for i in range(2)]
    v_loaded = [m.sem(f"v_loaded{i}") for i in range(2)]
    fixed, s1_ready, s1_used = m.sem("fixed"), m.sem("s1_ready"), m.sem("s1_used")
    own_ready, ones_stored, pool_steps = m.sem("own_ready"), m.sem("ones_stored"), m.sem("pool_steps")
    max_turned, max_loaded = m.sem("max_turned"), m.sem("max_loaded")
    s2_ready, exped, av_done, out_ready, out_stored = (m.sem("s2_ready"), m.sem("exped"), m.sem("av_done"),
                                                       m.sem("out_ready"), m.sem("out_stored"))
    max_steps = m.sem("max_steps")
    att_stack = ExitStack()
    outs = m.sb("outs", [P, UNITS, CHUNK], stack=att_stack)
    with ExitStack() as stack:
        q = m.sb("q", [ROWS_M, CHUNKS, GH, CHUNK], BF16, stack=stack)
        k1 = m.sb("k1", [ROWS, GH, T], BF16, stack=stack)
        k2 = m.sb("k2", [ROWS_M, GH, T], BF16, stack=stack)
        v = m.sb("v", [P, TILES, GH, VC], stack=stack)
        ex = [m.xT[:, :].rearrange("p (h t) -> p h t", t=CHUNK),
              m.xn[:, :, :].rearrange("p (h a) d -> p h (a d)", a=TPC)]
        mx = m.sb("mx", [P, GH, TPC, CHUNKS // 2], stack=stack)
        neg = m.sb("neg", [P, GH, TPC], stack=stack)
        neg_rest = m.sb("neg_rest", [P, 2, GH, TPC], stack=stack)
        neg_part = m.sb("neg_part", [P, TPC, 32], BF16, stack=stack)
        neg_turned = m.sb("neg_turned", [P, 32, TPC], BF16, stack=stack)
        zeros = m.sb("zeros", [P, CHUNK], BF16, stack=stack)
        own_row = m.sb("own_row", [P, GH], BF16, stack=stack)
        S1B, S2B, AVB = [0, 1, 2, 3], [4, 5, 6], 7
        S2_BANK = [S2B[s % 3] for s in range(STEPS - 1)] + [S2B[1]]
        S2_SINCE = [next(d for d in range(1, STEPS) if S2_BANK[s - d] == S2_BANK[s]) for s in range(STEPS)]
        done = [max(0, (k + 1 - HOLE) * STEPS // (STEPS - HOLE)) for k in range(-1, STEPS)]
        S1_IN = [range(done[k], done[k + 1]) for k in range(STEPS)]
        block = stack.enter_context(nc.Block())
        key_rows = dram_k.rearrange("j (h e) t -> j e h t", e=HD)
        query_rows = dram_q.rearrange("i (h e) t -> i e h t", e=HD)

        DMAS_M = 16 * (P // 32)
        DMAS_Q = 16 * PARTS * PARTS
        DMAS_K = 16 * PARTS * PARTS

        def load_q(eng, g, qc):
            for i in range(PARTS):
                for j in range(PARTS):
                    r = (i * PARTS + j) * HD
                    eng.dma_start(q[r:r + HD, qc, :, :],
                                  query_rows[i, :, bass.ts(g, GH), qc * CHUNK:(qc + 1) * CHUNK]).then_inc(q_loaded[qc], 16)

        def load_k1(eng, g, h):
            for i in range(PARTS):
                for j in range(PARTS):
                    r = (i * PARTS + j) * HD
                    eng.dma_start(k1[r:r + HD, h, :], key_rows[j, :, bass.ts(g * GH + h, 1), :])\
                        .then_inc(k1_loaded[h], 16)

        def load_k2(eng, g, half):
            t = slice(half * (T // 2), (half + 1) * (T // 2))
            for i in range(PARTS):
                for j in range(PARTS):
                    r = (i * PARTS + j) * HD
                    eng.dma_start(k2[r:r + HD, :, t], key_rows[j, :, bass.ts(g, GH), t]).then_inc(k2_loaded[half], 16)

        def load_v(eng, g, half):
            t = slice(half * (TILES // 2), (half + 1) * (TILES // 2))
            eng.dma_start(v[:, t, :, :], values[:, bass.ts(g, 1), t, :, :].rearrange("p g t h e -> p (g t) h e"))\
                .then_inc(v_loaded[half], 16)

        @block.sync
        def _(sp):
            load_q(sp, 0, 0)
            for h in range(GH):
                load_k1(sp, 0, h)
            load_q(sp, 0, 1)
            sp.wait_ge(ones_stored, 1)
            for half in range(2):
                load_k2(sp, 0, half)
                load_v(sp, 0, half)
            load_q(sp, 0, 2)

            def load_maxima(u, qc):
                sp.wait_ge(max_turned, u + 1)
                for b in range(P // 32):
                    rows = neg_turned[b * 32:b * 32 + PARTS * GH, :, :].rearrange("r j t -> r (j t)").unsqueeze(1)\
                        .to_broadcast([PARTS * GH, GH, P])
                    sp.dma_start(q[ROWS:ROWS_M, qc, :, b * P:(b + 1) * P], rows).then_inc(max_loaded, 16)

            def unit(g, qc, last):
                u = g * CHUNKS + qc
                load_next_q(g, qc, last)
                if qc == CHUNKS - 2 and not last:
                    for h in range(GH):
                        if h == GH - 1:
                            load_maxima(u + 1, CHUNKS - 1)
                        sp.wait_ge(s1_ready, (u + 1) * PAIRS + (h + 1) * PAIRS // GH)
                        load_k1(sp, g + 1, h)
                elif qc == CHUNKS - 1 and not last:
                    for half in range(2):
                        if half == 1:
                            load_maxima(u + 1, 0)
                        sp.wait_ge(s2_ready, u * STEPS + (half + 1) * STEPS // 2)
                        load_k2(sp, g + 1, half)
                        sp.wait_ge(av_done, u * TILES + (half + 1) * TILES // 2)
                        load_v(sp, g + 1, half)
                elif qc < CHUNKS - 1:
                    load_maxima(u + 1, qc + 1)

            def load_next_q(g, qc, last):
                if last and qc >= 1:
                    return
                u = g * CHUNKS + qc
                if qc == 0:
                    if not isinstance(g, int) or g > 0:
                        sp.wait_ge(s2_ready, u * STEPS)
                    load_q(sp, g, 3)
                else:
                    sp.wait_ge(s2_ready, u * STEPS)
                    load_q(sp, g + 1, qc - 1)

            load_maxima(0, 0)
            for qc in range(CHUNKS):
                unit(0, qc, False)
            with sp.Fori(1, GROUPS - 1) as g:
                for qc in range(CHUNKS):
                    unit(g, qc, False)
            for qc in range(CHUNKS):
                unit(GROUPS - 1, qc, True)

        @block.gpsimd
        def _(pool):
            step = Chain(pool, pool_steps)
            step(nc.gpsimd.memset(own_row[:, :], 0.0))
            for i in range(PARTS):
                step(nc.gpsimd.affine_select(out=own_row[:, :], in_=own_row[:, :], compare_op=ALU.not_equal, fill=1.0,
                                             base=-(ROWS + i * GH), pattern=[[-1, GH]], channel_multiplier=1))
            pool.sem_inc(own_ready, 1)
            step(nc.gpsimd.memset(zeros[:, :], 0.0))
            step(nc.gpsimd.memset(neg_part[:, :, :], 0.0))
            pool.sem_inc(fixed, 1)

        @block.tensor
        def _(pe):
            def first_pass(g, qc, i):
                h, qt, kc = i // (TPC * CHUNKS), i // CHUNKS % TPC, i % CHUNKS
                if i == 0:
                    pe.wait_ge(q_loaded[qc], DMAS_Q * (g + 1))
                if qc == 0 and i % (TPC * CHUNKS) == 0:
                    pe.wait_ge(k1_loaded[h], DMAS_K * (g + 1))
                if i % 2 == 0 and not (isinstance(g, int) and g == 0 and qc == 0 and i < len(S1B)):
                    pe.wait_ge(s1_used, (g * CHUNKS + qc) * PAIRS + (i // 2 - 1))
                queries = q[0:ROWS, qc, h, :].rearrange("r (p t) -> r t p", t=TPC)[:, qt, :]
                mm = nc.tensor.matmul(m.ps[:, S1B[i % 4], :], queries,
                                      k1[:, h, kc * CHUNK:(kc + 1) * CHUNK], start=True, stop=True)
                if i % 2 == 1:
                    mm.then_inc(s1_ready, 1)

            def weigh(g, qc, kt, first=False):
                u = g * CHUNKS + qc
                if qc == 0 and kt % (TILES // 2) == 0:
                    pe.wait_ge(v_loaded[kt // (TILES // 2)], 16 * (g + 1))
                if kt == 0 and not first:
                    pe.wait_ge(out_stored, u)
                pe.wait_ge(exped, u * STEPS + (kt + 1) * GH)
                for h in range(GH):
                    last = nc.tensor.matmul(m.ps[32 * h:32 * h + VC, AVB, :], v[:, kt, h, :],
                                            ex[kt % P_RING][:, h, :], start=(kt == 0), stop=(kt == TILES - 1),
                                            skip_group_check=True)
                last.then_inc(av_done, 1)

            def unit(g, qc, last, first=False):
                u = g * CHUNKS + qc
                after = [(g, qc + 1), (g, qc + 2)]
                after = [(a, b) if b < CHUNKS else (a + 1, b - CHUNKS) for a, b in after]

                def ahead(s):
                    if last and (qc == CHUNKS - 1 or (qc == CHUNKS - 2 and s + LEAD >= STEPS)):
                        return
                    for i in S1_IN[(s + LEAD) % STEPS]:
                        first_pass(*after[(s + LEAD) // STEPS], i)

                def score(s):
                    kt, h = s // GH, s % GH
                    if not (first and s < len(S2B)):
                        pe.wait_ge(exped, u * STEPS + (s - S2_SINCE[s] + 1))
                    nc.tensor.matmul(m.ps[:, S2_BANK[s], :], k2[:, h, kt * P:(kt + 1) * P], q[:, qc, h, :],
                                     start=True, stop=True).then_inc(s2_ready, 1)

                pe.wait_ge(max_loaded, DMAS_M * (u + 1))
                for kt in range(TILES):
                    if qc == 0 and kt % (TILES // 2) == 0:
                        pe.wait_ge(k2_loaded[kt // (TILES // 2)], DMAS_K * (g + 1))
                    s = kt * GH
                    score(s)
                    score(s + 1)
                    ahead(s)
                    score(s + 2)
                    ahead(s + 1)
                    score(s + 3)
                    ahead(s + 2)
                    if kt >= 1:
                        weigh(g, qc, kt - 1, first)
                    elif qc >= 1:
                        weigh(g, qc - 1, TILES - 1)
                    elif not first:
                        weigh(g - 1, CHUNKS - 1, TILES - 1)
                    ahead(s + 3)

            pe.wait_ge(fixed, 1)
            nc.tensor.matmul(m.ps[:, AVB, :], zeros[:, 0:P], zeros[:, :], start=True, stop=True)
            for i in range(STEPS):
                first_pass(0, 0, i)
            for i in range(S1_IN[LEAD].start):
                first_pass(0, 1, i)
            unit(0, 0, False, True)
            for qc in range(1, CHUNKS):
                unit(0, qc, False)
            with pe.Fori(1, GROUPS - 1) as g:
                for qc in range(CHUNKS):
                    unit(g, qc, False)
            for qc in range(CHUNKS):
                unit(GROUPS - 1, qc, True)
            weigh(GROUPS - 1, CHUNKS - 1, TILES - 1)

        @block.scalar
        def _(act):
            def store_out(u):
                act.wait_ge(av_done, (u + 1) * TILES)
                nc.scalar.activation(outs[:, bass.ts(u, 1), :].rearrange("p u t -> p (u t)"), m.ps[:, AVB, :],
                                     ACT.Copy).then_inc(out_stored, 1)

            def unit(g, qc, last, first=False):
                u = g * CHUNKS + qc
                for kt in range(TILES):
                    for h in range(GH):
                        s = kt * GH + h
                        act.wait_ge(s2_ready, u * STEPS + (s + 1))
                        if h == 0 and not (first and kt < P_RING):
                            act.wait_ge(av_done, u * TILES + (kt - P_RING + 1))
                        nc.scalar.activation(ex[kt % P_RING][:, h, :], m.ps[:, S2_BANK[s], :], ACT.Exp).then_inc(exped, 1)
                    if kt == 0 and not first:
                        store_out(u - 1)

            act.wait_ge(own_ready, 1)
            low = 64
            nc.scalar.activation(k2[low:ROWS_M, :, :], own_row[low:ROWS_M, :].unsqueeze(2).to_broadcast([ROWS_M - low, GH, T]),
                                 ACT.Copy).then_inc(ones_stored, 1)
            unit(0, 0, False, True)
            for qc in range(1, CHUNKS):
                unit(0, qc, False)
            with act.Fori(1, GROUPS - 1) as g:
                for qc in range(CHUNKS):
                    unit(g, qc, False)
            for qc in range(CHUNKS):
                unit(GROUPS - 1, qc, True)
            store_out(UNITS - 1)

        @block.vector
        def _(dve):
            def maxima(u, first=False):
                for i in range(PAIRS):
                    dve.wait_ge(s1_ready, u * PAIRS + (i + 1))
                    h, qt, kc = 2 * i // (TPC * CHUNKS), 2 * i // CHUNKS % TPC, i % (CHUNKS // 2)
                    nc.vector.reduce_max(mx[:, h, qt, kc:kc + 1], m.ps[:, 2 * (i % 2):2 * (i % 2) + 2, :], AX.XY)\
                        .then_inc(s1_used, 1)
                dve.wait_ge(s1_used, (u + 1) * PAIRS)
                nc.vector.tensor_reduce(neg[:, :, :], mx[:, :, :, :], axis=AX.X, op=ALU.max, negate=True)\
                    .then_inc(max_steps, 1)
                dve.wait_ge(max_steps, u * 6 + 1)
                out = neg_part[:, :, 0:PARTS * GH].rearrange("p t (i h) -> p h t i", h=GH)
                nc.vector.tensor_copy(out[:, :, :, 0], neg[:, :, :]).then_inc(max_steps, 1)
                dve.wait_ge(max_steps, u * 6 + 2)
                nc.vector.tensor_tensor(neg_rest[:, 0, :, :], neg[:, :, :], out[:, :, :, 0], ALU.subtract).then_inc(max_steps, 1)
                dve.wait_ge(max_steps, u * 6 + 3)
                nc.vector.tensor_copy(out[:, :, :, 1], neg_rest[:, 0, :, :]).then_inc(max_steps, 1)
                dve.wait_ge(max_steps, u * 6 + 4)
                nc.vector.tensor_tensor(neg_rest[:, 1, :, :], neg_rest[:, 0, :, :], out[:, :, :, 1], ALU.subtract)\
                    .then_inc(max_steps, 1)
                dve.wait_ge(max_steps, u * 6 + 5)
                nc.vector.tensor_copy(out[:, :, :, 2], neg_rest[:, 1, :, :]).then_inc(max_steps, 1)
                dve.wait_ge(max_steps, u * 6 + 6)
                if not first:
                    dve.wait_ge(max_loaded, DMAS_M * u)
                nc.vector.transpose(neg_turned[:, :, :].rearrange("p j t -> p t j"), neg_part[:, :, :]).then_inc(max_turned, 1)
                dve.wait_ge(max_turned, u + 1)

            dve.wait_ge(fixed, 1)
            maxima(0, True)
            with dve.Fori(1, UNITS) as u:
                maxima(u)

    m.stage()
    out_turned, inv_ready, att_ready, att_turned = m.sem("out_turned"), m.sem("inv_ready"), m.sem("att_ready"), m.sem("att_turned")
    attT_ready, projected, bias_added, x_updated = m.sem("attT_ready"), m.sem("projected"), m.sem("bias_added"), m.sem("x_updated")
    with ExitStack() as stack:
        inv = m.sb("inv_den", [P, TPC, GH], stack=stack)
        att = m.sb("att", [P, TILES, D], stack=stack)
        attT = m.sb("attT", [P, T], stack=stack)
        xb = m.sb("xb", [P, 2, TPC, D], stack=stack)
        block = stack.enter_context(nc.Block())

        @block.tensor
        def _(pe):
            for qc in range(CHUNKS):
                for g in range(GROUPS):
                    n = qc * GROUPS + g
                    if n >= 2:
                        pe.wait_ge(att_ready, n - 1)
                    for j in range(TPC):
                        last = nc.tensor.transpose(m.ps[:, n % 2, j * P:(j + 1) * P],
                                                   outs[:, g * CHUNKS + qc, j * P:(j + 1) * P], m.ident[:, :])
                    last.then_inc(out_turned, 1)
                pe.wait_ge(att_ready, (qc + 1) * GROUPS)
                for j in range(TPC):
                    last = nc.tensor.transpose(m.ps[:, 2 + qc % 2, j * P:(j + 1) * P], att[:, qc * TPC + j, :], m.ident[:, :])
                last.then_inc(att_turned, 1)
                pe.wait_ge(attT_ready, qc + 1)
                if qc >= 2:
                    pe.wait_ge(bias_added, qc - 1)
                for j in range(TPC):
                    t = qc * TPC + j
                    last = nc.tensor.matmul(m.ps[:, 4 + qc % 2, j * P:(j + 1) * P], attT[:, t * P:(t + 1) * P],
                                            m.projT[:, 0, :], start=True, stop=True)
                last.then_inc(projected, 1)

        @block.scalar
        def _(act):
            for qc in range(CHUNKS):
                act.wait_ge(att_turned, qc + 1)
                nc.scalar.activation(attT[:, qc * CHUNK:(qc + 1) * CHUNK], m.ps[:, 2 + qc % 2, :], ACT.Copy)\
                    .then_inc(attT_ready, 1)

        @block.vector
        def _(dve):
            for qc in range(CHUNKS):
                for g in range(GROUPS):
                    n = qc * GROUPS + g
                    dve.wait_ge(out_turned, n + 1)
                    turned = m.ps[:, n % 2, :].rearrange("p (t h r) -> p t h r", h=GH, r=32)
                    if n >= 1:
                        dve.wait_ge(att_ready, n)
                    nc.vector.reciprocal(inv[:, :, :], turned[:, :, :, HD]).then_inc(inv_ready, 1)
                    dve.wait_ge(inv_ready, n + 1)
                    dst = att[:, qc * TPC:(qc + 1) * TPC, g * GH * HD:(g + 1) * GH * HD].rearrange("p t (h e) -> p t h e", e=HD)
                    nc.vector.tensor_tensor(dst, turned[:, :, :, 0:HD],
                                            inv[:, :, :].unsqueeze(3).to_broadcast([P, TPC, GH, HD]), ALU.mult)\
                        .then_inc(att_ready, 1)
                dve.wait_ge(projected, qc + 1)
                x_t = m.X[:, qc * TPC:(qc + 1) * TPC, :]
                nc.vector.tensor_tensor(xb[:, qc % 2, :, :], m.ps[:, 4 + qc % 2, :].rearrange("p (t d) -> p t d", d=D),
                                        m.proj_bias[:, :].unsqueeze(1).to_broadcast([P, TPC, D]), ALU.add).then_inc(bias_added, 1)
                dve.wait_ge(bias_added, qc + 1)
                nc.vector.tensor_tensor(x_t, x_t, xb[:, qc % 2, :, :], ALU.add).then_inc(x_updated, 1)
    att_stack.close()
    kv_stack.close()


def decay_attention(m):
    nc = m.nc
    tag = m.stage()
    proj, clipped, exped = m.sem("proj"), m.sem("clipped"), m.sem("exped")
    steps, feat_ready = m.sem("feat_steps"), m.sem("feat_ready")
    with ExitStack() as outer:
        phi = m.sb("phi" + tag, [P, 2, T], stack=outer)
        lam = m.sb("lam" + tag, [P, T], stack=outer)
        with ExitStack() as stack:
            z = m.sb("z" + tag, [P, 2, CHUNK], stack=stack)
            low = m.sb("low" + tag, [P, 2, CHUNK], stack=stack)
            z_ready = m.sem("z_ready")
            elow = m.sb("elow" + tag, [P, 2, CHUNK], stack=stack)
            one_plus = m.sb("one_plus" + tag, [P, CHUNK], stack=stack)
            sig = m.sb("sig" + tag, [P, CHUNK], stack=stack)
            jobs = [(s, c) for c in range(CHUNKS) for s in range(3)]
            weights = [m.q_w, m.k_w, m.dec_rep]
            block = stack.enter_context(nc.Block())

            @block.tensor
            def _(pe):
                for n, (s, c) in enumerate(jobs):
                    if n >= 4:
                        pe.wait_ge(feat_ready, n - 3)
                    nc.tensor.matmul(m.ps[:, n % 4, :], weights[s][:, :], m.xT[:, c * CHUNK:(c + 1) * CHUNK],
                                     start=True, stop=True).then_inc(proj, 1)

            @block.scalar
            def _(act):
                for n, (s, c) in enumerate(jobs):
                    if s < 2:
                        act.wait_ge(proj, n + 1)
                        if n >= 2:
                            act.wait_ge(feat_ready, n - 1)
                        nc.scalar.activation(z[:, n % 2, :], m.ps[:, n % 4, :], ACT.Identity, bias=m.qk1_bias[:, s:s + 1])\
                            .then_inc(z_ready, 1)
                        act.wait_ge(clipped, 2 * c + s + 1)
                        nc.scalar.activation(elow[:, n % 2, :], low[:, n % 2, :], ACT.Exp).then_inc(exped, 1)
                    else:
                        act.wait_ge(proj, n + 1)
                        if n >= 2:
                            act.wait_ge(feat_ready, n - 1)
                        nc.scalar.activation(elow[:, n % 2, :], m.ps[:, n % 4, :], ACT.Exp, bias=m.neg_dec_b[:, 0:1],
                                             scale=-1.0).then_inc(exped, 1)

            @block.vector
            def _(dve):
                step = Chain(dve, steps)
                for n, (s, c) in enumerate(jobs):
                    t = slice(c * CHUNK, (c + 1) * CHUNK)
                    if s < 2:
                        dve.wait_ge(z_ready, 2 * c + s + 1)
                        nc.vector.tensor_scalar(low[:, n % 2, :], z[:, n % 2, :], 0.0, None, ALU.min).then_inc(clipped, 1)
                        dve.wait_ge(exped, n + 1)
                        nc.vector.scalar_tensor_tensor(out=phi[:, s, t], in0=z[:, n % 2, :], scalar=0.0,
                                                       in1=elow[:, n % 2, :], op0=ALU.max, op1=ALU.add)\
                            .then_inc(feat_ready, 1)
                        dve.wait_ge(feat_ready, n + 1)
                    else:
                        dve.wait_ge(exped, n + 1)
                        step(nc.vector.tensor_scalar(one_plus[:, :], elow[:, n % 2, :], 1.0, None, ALU.add))
                        step(nc.vector.reciprocal(sig[:, :], one_plus[:, :]))
                        nc.vector.tensor_scalar(lam[:, t], sig[:, :], LAM_MIN, None, ALU.max).then_inc(feat_ready, 1)
                        dve.wait_ge(feat_ready, n + 1)

        m.stage()
        v_ready, kv_ready, fwd_ready, bwd_ready = m.sem("v_ready"), m.sem("kv_ready"), m.sem("fwd_ready"), m.sem("bwd_ready")
        both_ready, qs_ready, summed, num_done = m.sem("both_ready"), m.sem("qs_ready"), m.sem("summed"), m.sem("num_done")
        edge, steps2, attT_ready, o_ready, ob_ready, x_ready = (m.sem("edge"), m.sem("steps"), m.sem("attT_ready"),
                                                                 m.sem("o_ready"), m.sem("ob_ready"), m.sem("x_ready"))
        with ExitStack() as stack:
            kv = m.sb("kv" + tag, [P, 2, T], stack=stack)
            fwd = m.sb("fwd" + tag, [P, 2, T], stack=stack)
            bwd = m.sb("bwd" + tag, [P, 2, T], stack=stack)
            both = fwd
            qs = m.sb("qs" + tag, [P, 2, T], stack=stack)
            den = m.sb("den" + tag, [P, 2, CHUNK], stack=stack)
            attT = m.sb("attT" + tag, [P, T], stack=stack)
            ob = m.sb("ob" + tag, [P, 2, TPC, D], stack=stack)
            block = stack.enter_context(nc.Block())

            def weigh(dve, v):
                dve.wait_ge(both_ready, v + 1)
                if v >= 2:
                    dve.wait_ge(summed, v - 1)
                nc.vector.tensor_tensor(qs[:, v % 2, :], phi[:, 0, :], both[:, v % 2, :], ALU.mult).then_inc(qs_ready, 1)

            @block.tensor
            def _(pe):
                def values_of(v):
                    for c in range(CHUNKS):
                        if v >= 1:
                            pe.wait_ge(kv_ready, (v - 1) * CHUNKS + c + 1)
                        nc.tensor.matmul(m.ps[:, 4 + c, :], m.v_rep[:, v, :], m.xT[:, c * CHUNK:(c + 1) * CHUNK],
                                         start=True, stop=True).then_inc(v_ready, 1)

                values_of(0)
                values_of(1)
                for v in range(VC):
                    if v + 2 < HD:
                        values_of(v + 2)
                    pe.wait_ge(qs_ready, v + 1)
                    if v == HD:
                        pe.wait_ge(kv_ready, HD * CHUNKS)
                    for c in range(CHUNKS):
                        if v < HD:
                            last = nc.tensor.matmul(m.ps[:, c, :], m.pick[:, v, :], qs[:, v % 2, c * CHUNK:(c + 1) * CHUNK],
                                                    start=(v == 0), stop=(v == HD - 1))
                        else:
                            last = nc.tensor.matmul(m.ps[:, 4 + c, :], m.same_head[:, :], qs[:, v % 2, c * CHUNK:(c + 1) * CHUNK],
                                                    start=True, stop=True)
                    last.then_inc(summed, 1)
                for c in range(CHUNKS):
                    pe.wait_ge(attT_ready, c + 1)
                    for j in range(TPC):
                        t = c * TPC + j
                        last = nc.tensor.matmul(m.ps[:, c, j * P:(j + 1) * P], attT[:, t * P:(t + 1) * P], m.o_w[:, :],
                                                start=True, stop=True)
                    last.then_inc(o_ready, 1)

            @block.vector
            def _(dve):
                step = Chain(dve, steps2)
                nc.vector.memset(bwd[:, 0, T - 1:T], 0.0).then_inc(edge, 1)
                nc.vector.memset(bwd[:, 1, T - 1:T], 0.0).then_inc(edge, 1)
                for v in range(VC):
                    if v < HD:
                        for c in range(CHUNKS):
                            t = slice(c * CHUNK, (c + 1) * CHUNK)
                            dve.wait_ge(v_ready, v * CHUNKS + c + 1)
                            nc.vector.scalar_tensor_tensor(out=kv[:, v % 2, t], in0=m.ps[:, 4 + c, :], scalar=m.v1_bias[:, v:v + 1],
                                                           in1=phi[:, 1, t], op0=ALU.add, op1=ALU.mult).then_inc(kv_ready, 1)
                        dve.wait_ge(kv_ready, (v + 1) * CHUNKS)
                        src = kv[:, v % 2, :]
                    else:
                        src = phi[:, 1, :]
                    if v >= 2:
                        dve.wait_ge(qs_ready, v - 1)
                    nc.vector.tensor_tensor_scan(fwd[:, v % 2, :], lam[:, :], src, 0.0, ALU.mult, ALU.add).then_inc(fwd_ready, 1)
                    nc.vector.tensor_tensor_scan(bwd[:, v % 2, 0:T - 1][:, ::-1], src[:, 1:T][:, ::-1], lam[:, 1:T][:, ::-1],
                                                 0.0, ALU.add, ALU.mult).then_inc(bwd_ready, 1)
                    if v >= 1:
                        weigh(dve, v - 1)
                weigh(dve, VC - 1)
                for c in range(CHUNKS):
                    t = slice(c * CHUNK, (c + 1) * CHUNK)
                    dve.wait_ge(summed, VC)
                    step(nc.vector.tensor_scalar(den[:, 0, :], m.ps[:, 4 + c, :], DEN_EPS, None, ALU.max))
                    step(nc.vector.reciprocal(den[:, 1, :], den[:, 0, :]))
                    nc.vector.tensor_tensor(attT[:, t], m.ps[:, c, :], den[:, 1, :], ALU.mult).then_inc(attT_ready, 1)
                    dve.wait_ge(attT_ready, c + 1)
                for c in range(CHUNKS):
                    dve.wait_ge(o_ready, c + 1)
                    if c >= 2:
                        dve.wait_ge(x_ready, c - 1)
                    nc.vector.tensor_tensor(ob[:, c % 2, :, :], m.ps[:, c, :].rearrange("p (t d) -> p t d", d=D),
                                            m.o_bias[:, :].unsqueeze(1).to_broadcast([P, TPC, D]), ALU.add).then_inc(ob_ready, 1)
                    dve.wait_ge(ob_ready, c + 1)
                    x_t = m.xn[:, c * TPC:(c + 1) * TPC, :]
                    nc.vector.tensor_tensor(x_t, x_t, ob[:, c % 2, :, :], ALU.add).then_inc(x_ready, 1)

            @block.gpsimd
            def _(pool):
                pool.wait_ge(edge, 2)
                for v in range(VC):
                    pool.wait_ge(fwd_ready, v + 1)
                    pool.wait_ge(bwd_ready, v + 1)
                    nc.gpsimd.tensor_tensor(both[:, v % 2, :], fwd[:, v % 2, :], bwd[:, v % 2, :], ALU.add).then_inc(both_ready, 1)


def gelu_ffn(m):
    nc = m.nc
    tag = m.stage()
    a_ready, hid_ready, y_ready, res_ready, yb_ready, x_ready = (m.sem("a_ready"), m.sem("hid_ready"), m.sem("y_ready"),
                                                                 m.sem("res_ready"), m.sem("yb_ready"), m.sem("x_ready"))
    with ExitStack() as stack:
        hid = m.sb("fhid" + tag, [P, 2, FFN, CHUNK], stack=stack)
        res = m.sb("fres" + tag, [P, 2, TPC, D], stack=stack)
        yb = m.sb("fyb" + tag, [P, 2, TPC, D], stack=stack)
        block = stack.enter_context(nc.Block())

        @block.tensor
        def _(pe):
            def up(c):
                for i in range(FFN):
                    if c >= 1:
                        pe.wait_ge(hid_ready, (c - 1) * FFN + i + 1)
                    nc.tensor.matmul(m.ps[:, i, :], m.f1_w[:, i * P:(i + 1) * P], m.xT[:, c * CHUNK:(c + 1) * CHUNK],
                                     start=True, stop=True).then_inc(a_ready, 1)

            up(0)
            for c in range(CHUNKS):
                if c + 1 < CHUNKS:
                    up(c + 1)
                pe.wait_ge(hid_ready, (c + 1) * FFN)
                if c >= 2:
                    pe.wait_ge(yb_ready, c - 1)
                for j in range(TPC):
                    for i in range(FFN):
                        last = nc.tensor.matmul(m.ps[:, 4 + c % 2, j * P:(j + 1) * P], hid[:, c % 2, i, j * P:(j + 1) * P],
                                                m.f2_w[:, i, :], start=(i == 0), stop=(i == FFN - 1))
                last.then_inc(y_ready, 1)

        @block.scalar
        def _(act):
            for c in range(CHUNKS):
                for i in range(FFN):
                    act.wait_ge(a_ready, c * FFN + i + 1)
                    if c >= 2:
                        act.wait_ge(y_ready, c - 1)
                    nc.scalar.activation(hid[:, c % 2, i, :], m.ps[:, i, :], ACT.Gelu, bias=m.f1_b[:, i:i + 1]).then_inc(hid_ready, 1)

        @block.vector
        def _(dve):
            for c in range(CHUNKS):
                t = slice(c * TPC, (c + 1) * TPC)
                if c >= 2:
                    dve.wait_ge(x_ready, c - 1)
                nc.vector.tensor_tensor(res[:, c % 2, :, :], m.X[:, t, :], m.xn[:, t, :], ALU.add).then_inc(res_ready, 1)
                dve.wait_ge(y_ready, c + 1)
                nc.vector.tensor_tensor(yb[:, c % 2, :, :], m.ps[:, 4 + c % 2, :].rearrange("p (t d) -> p t d", d=D),
                                        m.f2_bias[:, :].unsqueeze(1).to_broadcast([P, TPC, D]), ALU.add).then_inc(yb_ready, 1)
                dve.wait_ge(yb_ready, c + 1)
                dve.wait_ge(res_ready, c + 1)
                nc.vector.tensor_tensor(m.X[:, t, :], res[:, c % 2, :, :], yb[:, c % 2, :, :], ALU.add).then_inc(x_ready, 1)


def store(m, out):
    nc = m.nc
    m.stage()
    stored = m.sem("stored")
    with nc.Block() as block:

        @block.sync
        def _(sp):
            sp.dma_start(out[0].rearrange("(t p) d -> p t d", p=P), m.X[:, :, :]).then_inc(stored, 16)
            sp.wait_ge(stored, 16)


def macaron(nc: bass.Bass, w, out):
    with ExitStack() as stack:
        m = Machine(nc, stack)
        m.ps = stack.enter_context(nc.psum_tensor("ps", [P, 8, CHUNK], F32))
        m.X = m.sb("X", [P, TILES, D])
        m.xn = m.sb("xn", [P, TILES, D])
        m.xT = m.sb("xT", [P, T])
        m.ident = m.sb("ident", [P, P])
        m.identb = m.sb("identb", [P, P], BF16)
        m.neg_half = m.sb("neg_half", [P, TPC])
        m.euler = m.sb("euler", [P, TPC * E])
        m.below = m.sb("below", [P, E, E])
        m.sel_gate = m.sb("sel_gate", [P, E, P], BF16)
        m.sel_mask = m.sb("sel_mask", [P, E, P], BF16)
        m.gT = m.sb("gT", [P, T], BF16)
        m.pick = m.sb("pick", [P, HD, P])
        m.same_head = m.sb("same_head", [P, P])
        m.cw = m.sb("cw", [P, TILES, E + 1])
        counts = [E, E, E, SH0, SH0, SH0, 3, 1]
        m.wT = m.sb("wT", [P, sum(counts), D])
        at = [sum(counts[:i]) for i in range(len(counts) + 1)]
        m.w1T, m.w3T, m.w2T, m.sw1T, m.sw2T, m.sw3T, m.qkvT, m.projT = (
            m.wT[:, at[i]:at[i + 1], :] for i in range(len(counts)))
        m.gateT = m.sb("gateT", [P, E])
        m.biases = [(w["L0_ffn_b1"], E), (w["L0_ffn_b2"], E), (w["L0_ffn_b3"], E),
                    (w["L0_attn_qkv_b"][0:2 * D].rearrange("(s p) -> s p", p=P), 2),
                    (w["L1_attn_f1_b"].rearrange("(i p) -> i p", p=P), FFN)]
        m.biases += [(w[n].unsqueeze(0), 1) for n in ("L1_attn_q_b", "L1_attn_k_b", "L1_attn_ln1_w", "L1_attn_ln1_b",
                                                      "L1_attn_ln2_w", "L1_attn_ln2_b")]
        m.bias_rows = sum(n for _, n in m.biases)
        m.biasT = m.sb("biasT", [P, m.bias_rows])
        ends = [sum(n for _, n in m.biases[:i + 1]) for i in range(len(m.biases))]
        m.b1, m.b2, m.b3, m.qk_bias_raw, m.f1_b = (m.biasT[:, e - n:e] for e, (_, n) in zip(ends, m.biases[:5]))
        m.qk1_bias = m.biasT[:, ends[4]:ends[4] + 2]
        m.ln = m.biasT[:, ends[4] + 2:ends[4] + 6]
        m.qk_bias = m.sb("qk_bias", [P, 2])
        m.v_bias = m.sb("v_bias", [P, D])
        m.proj_bias = m.sb("proj_bias", [P, D])
        m.router = m.sb("router", [P, E])
        m.ew1 = m.sb("ew1", [P, E + 1, HID1 * P])
        m.ew3 = m.sb("ew3", [P, E + 1, HID1 * P])
        m.ew2 = m.sb("ew2", [P, E + 1, HID1, D])
        m.q_w, m.k_w, m.v_w, m.o_w = (m.sb(n, [P, D]) for n in ("q_w", "k_w", "v_w", "o_w"))
        m.dec_w = m.sb("dec_w", [P, H])
        m.dec_rep = m.sb("dec_rep", [P, D])
        m.v_rep = m.sb("v_rep", [P, HD, D])
        m.f1_w = m.sb("f1_w", [P, FFN * P])
        m.f2_w = m.sb("f2_w", [P, FFN, D])
        m.dec_b_all = m.sb("dec_b_all", [P, H])
        m.v_b_all = m.sb("v_b_all", [P, D])
        m.neg_dec_b = m.sb("neg_dec_b", [P, 1])
        m.v1_bias = m.sb("v1_bias", [P, HD])
        m.o_bias, m.f2_bias = m.sb("o_bias", [P, D]), m.sb("f2_bias", [P, D])

        def on_all(v):
            return v.unsqueeze(0).to_broadcast([P, v.shape[0]])

        m.loads = [
            (m.v_bias[:, :], on_all(w["L0_attn_qkv_b"][2 * D:3 * D])),
            (m.proj_bias[:, :], on_all(w["L0_attn_proj_b"])),
            (m.router[:, :], w["L1_ffn_w_router"]),
            (m.ew1[:, 0:E, :], w["L1_ffn_w1"].rearrange("e d h -> d e h")),
            (m.ew1[:, E, :], w["L1_ffn_sw1"]),
            (m.ew3[:, 0:E, :], w["L1_ffn_w3"].rearrange("e d h -> d e h")),
            (m.ew3[:, E, :], w["L1_ffn_sw3"]),
            (m.ew2[:, 0:E, :, :].rearrange("p e i d -> p (e i) d"), w["L1_ffn_w2"].rearrange("e (i p) d -> p (e i) d", p=P)),
            (m.ew2[:, E, :, :], w["L1_ffn_sw2"].rearrange("(i p) d -> p i d", p=P)),
            (m.q_w[:, :], w["L1_attn_q_w"]), (m.k_w[:, :], w["L1_attn_k_w"]),
            (m.v_w[:, :], w["L1_attn_v_w"]), (m.o_w[:, :], w["L1_attn_o_w"]),
            (m.dec_w[:, :], w["L1_attn_dec_w"]),
            (m.f1_w[:, :], w["L1_attn_f1_w"]),
            (m.f2_w[:, :, :], w["L1_attn_f2_w"].rearrange("(i p) d -> p i d", p=P)),
            (m.o_bias[:, :], on_all(w["L1_attn_o_b"])), (m.f2_bias[:, :], on_all(w["L1_attn_f2_b"])),
            (m.dec_b_all[:, :], on_all(w["L1_attn_dec_b"])), (m.v_b_all[:, :], on_all(w["L1_attn_v_b"])),
        ]

        setup(m, w)
        derive_biases(m)
        moe0(m)
        layer_norm(m, m.X, m.xn)
        softmax_attention(m, w)
        moe0(m)
        moe1(m)
        layer_norm(m, m.X, m.xn)
        layer_norm(m, m.xn, None, m.ln[:, 0:1], m.ln[:, 1:2])
        decay_attention(m)
        layer_norm(m, m.xn, None, m.ln[:, 2:3], m.ln[:, 3:4])
        gelu_ffn(m)
        moe1(m)
        store(m, out)


def derive_biases(m):
    nc = m.nc
    tag = m.stage()
    steps = m.sem("bias_steps")
    with ExitStack() as stack:
        own = m.sb("own" + tag, [P, D], stack=stack)
        own_dec = m.sb("own_dec" + tag, [P, H], stack=stack)
        block = stack.enter_context(nc.Block())

        @block.vector
        def _(dve):
            step = Chain(dve, steps)
            nc.vector.tensor_scalar(m.qk_bias[:, 0:1], m.qk_bias_raw[:, 0:1], float(HD) ** -0.5, None, ALU.mult)
            nc.vector.tensor_copy(m.qk_bias[:, 1:2], m.qk_bias_raw[:, 1:2])
            step(nc.vector.tensor_tensor(own[:, :], m.v_b_all[:, :], m.same_head[:, :], ALU.mult))
            step(nc.vector.reduce_sum(m.v1_bias[:, :], own[:, :].rearrange("p (h v) -> p v h", v=HD), AX.X))
            head = m.same_head[:, :].rearrange("p (h v) -> p h v", v=HD)[:, :, 0]
            step(nc.vector.tensor_tensor(own_dec[:, :], m.dec_b_all[:, :], head, ALU.mult))
            step(nc.vector.tensor_reduce(m.neg_dec_b[:, :], own_dec[:, :], axis=AX.X, op=ALU.add, negate=True))


_INS = ['L0_attn_x', 'L0_attn_qkv_w', 'L0_attn_qkv_b', 'L0_attn_proj_w', 'L0_attn_proj_b', 'L0_ffn_gate_w', 'L0_ffn_w1',
        'L0_ffn_b1', 'L0_ffn_w2', 'L0_ffn_b2', 'L0_ffn_w3', 'L0_ffn_b3', 'L0_ffn_sw1', 'L0_ffn_sw2', 'L0_ffn_sw3',
        'L1_attn_q_w', 'L1_attn_q_b', 'L1_attn_k_w', 'L1_attn_k_b', 'L1_attn_v_w', 'L1_attn_v_b', 'L1_attn_o_w',
        'L1_attn_o_b', 'L1_attn_ln1_w', 'L1_attn_ln1_b', 'L1_attn_ln2_w', 'L1_attn_ln2_b', 'L1_attn_dec_w',
        'L1_attn_dec_b', 'L1_attn_f1_w', 'L1_attn_f1_b', 'L1_attn_f2_w', 'L1_attn_f2_b', 'L1_ffn_w_router', 'L1_ffn_w1',
        'L1_ffn_w3', 'L1_ffn_w2', 'L1_ffn_sw1', 'L1_ffn_sw3', 'L1_ffn_sw2']
_OUTS = [((1, T, D), 'float32')]


def kernel(**inputs):
    import numpy as _np
    import concourse.bacc as _bacc
    from concourse import mybir as _mybir
    from concourse.bass_utils import run_bass_kernel_spmd as _run

    nc = _bacc.Bacc("TRN2", target_bir_lowering=False, num_devices=1)
    arrays, args = {}, {}
    for name in _INS:
        a = _np.ascontiguousarray(inputs[name])
        arrays[f"in_{name}_dram"] = a
        args[name] = nc.dram_tensor(f"in_{name}_dram", a.shape, _mybir.dt.from_np(a.dtype), kind="ExternalInput").ap()
    shape, dtype = _OUTS[0]
    out = nc.dram_tensor("out_0_dram", shape, _mybir.dt.from_np(_np.dtype(dtype)), kind="ExternalOutput").ap()
    macaron(nc, args, out)
    r = _run(nc, [arrays], core_ids=[0])
    return r.results[0]["out_0_dram"]
```

```python
import concourse.bass as bass
from concourse import mybir
from contextlib import ExitStack

F32 = mybir.dt.float32
BF16 = mybir.dt.bfloat16
ALU = mybir.AluOpType
ACT = mybir.ActivationFunctionType
AX = mybir.AxisListType

P = 128
D = 128
T = 2048
TILES = T // P
CHUNK = 512
CHUNKS = T // CHUNK
TPC = CHUNK // P
E = 8
TOPK = 2
HID0 = 128
SH0 = 256 // P
HID1 = 256 // P
H = 16
HD = D // H
FFN = 512 // P
LN_EPS = 1e-5
DEN_EPS = 1e-6
LAM_MIN = 1e-8

GH = 4
GROUPS = H // GH
PARTS = 3
ROWS = PARTS * PARTS * HD
ROWS_M = ROWS + PARTS * GH
VC = HD + 1
LEAD = 12
HOLE = 3
PART_RING = 4
P_RING = 2


class Chain:

    def __init__(self, engine, sem, before=0):
        self.engine, self.sem, self.before, self.count = engine, sem, before, 0

    def __call__(self, instruction):
        self.count += 1
        instruction.then_inc(self.sem, 1)
        self.engine.wait_ge(self.sem, self.before + self.count)


class Machine:

    def __init__(self, nc, stack):
        self.nc, self.stack, self.calls = nc, stack, 0
        self.in_use, self.cleared, self.free = [], [], []

    def sb(self, name, shape, dt=F32, stack=None):
        return (stack or self.stack).enter_context(self.nc.sbuf_tensor(name, shape, dt))

    def sem(self, name):
        handle = self.free.pop() if self.free else self.stack.enter_context(self.nc.semaphore(f"{name}_{self.calls}_{len(self.in_use)}"))
        self.in_use.append(handle)
        return handle

    def stage(self):
        self.calls += 1
        self.free += self.cleared
        for handle in self.in_use:
            self.nc.sync.sem_clear(handle)
        self.cleared, self.in_use = self.in_use, []
        return f"_{self.calls}"


def setup(m, w):
    nc = m.nc
    m.stage()
    loaded_x, loaded_small, steps = m.sem("loaded_x"), m.sem("loaded_small"), m.sem("steps")
    pool_steps, ident_ready = m.sem("pool_steps"), m.sem("ident_ready")
    loaded_gate, gate_turned, gate_stored = m.sem("loaded_gate"), m.sem("gate_turned"), m.sem("gate_stored")
    turned, stored, consts_ready = m.sem("turned"), m.sem("stored"), m.sem("consts_ready")
    raw = [(w["L0_ffn_w1"].rearrange("e h d -> h e d"), E),
           (w["L0_ffn_w3"].rearrange("e h d -> h e d"), E),
           (w["L0_ffn_w2"].rearrange("e h d -> h e d"), E),
           (w["L0_ffn_sw1"].rearrange("(a p) d -> p a d", p=P), SH0),
           (w["L0_ffn_sw2"].rearrange("(a p) d -> p a d", p=P), SH0),
           (w["L0_ffn_sw3"].rearrange("d (a p) -> d a p", p=P), SH0),
           (w["L0_attn_qkv_w"].rearrange("(a p) d -> p a d", p=P), 3),
           (w["L0_attn_proj_w"].rearrange("(a p) d -> p a d", p=P), 1)]
    ends = [sum(n for _, n in raw[:i + 1]) for i in range(len(raw))]
    n_raw = ends[-1]
    loaded = [m.sem(f"loaded{i}") for i in range(len(raw))]
    with ExitStack() as stack:
        wraw = m.sb("wraw", [P, n_raw, D], stack=stack)
        graw = m.sb("graw", [E, D], stack=stack)
        braw = m.sb("braw", [m.bias_rows, D], stack=stack)
        ahead = Prepare(m, stack, m.gateT, True, 6, 7)
        block = stack.enter_context(nc.Block())

        @block.sync
        def _(sp):
            sp.dma_start(m.X[:, :, :], w["L0_attn_x"][0].rearrange("(t p) d -> p t d", p=P)).then_inc(loaded_x, 16)
            sp.dma_start(graw[:, :], w["L0_ffn_gate_w"]).then_inc(loaded_gate, 16)
            for i, (src, n) in enumerate(raw):
                sp.dma_start(wraw[:, ends[i] - n:ends[i], :], src).then_inc(loaded[i], 16)
            at = 0
            for src, n in m.biases:
                sp.dma_start(braw[at:at + n, :], src).then_inc(loaded_small, 16)
                at += n

        @block.gpsimd
        def _(pool):
            step = Chain(pool, pool_steps)
            step(nc.gpsimd.memset(m.ident[:, :], 0.0))
            step(nc.gpsimd.affine_select(out=m.ident[:, :], in_=m.ident[:, :], compare_op=ALU.not_equal, fill=1.0,
                                         base=0, pattern=[[-1, P]], channel_multiplier=1))
            nc.gpsimd.tensor_copy(m.identb[:, :], m.ident[:, :]).then_inc(ident_ready, 1)
            step(nc.gpsimd.memset(m.neg_half[:, :], -0.5))
            ahead.rstds(pool, 0)
            nc.gpsimd.memset(m.euler[:, :], 2.718281828459045)
            nc.gpsimd.memset(m.cw[:, :, E:E + 1], 0.5)
            nc.gpsimd.memset(m.gT[:, :], 0.0)
            step(nc.gpsimd.memset(m.below[:, :, :], 1.0))
            step(nc.gpsimd.affine_select(out=m.below[:, :, :], in_=m.below[:, :, :], compare_op=ALU.is_gt, fill=0.0,
                                         base=0, pattern=[[1, E], [-1, E]], channel_multiplier=0))
            rows = PARTS + 1
            step(nc.gpsimd.memset(m.sel_gate[:, :, :], 1.0))
            step(nc.gpsimd.memset(m.sel_mask[:, :, :], 1.0))
            step(nc.gpsimd.affine_select(out=m.sel_gate[:, :, :], in_=m.sel_gate[:, :, :], compare_op=ALU.is_ge,
                                         fill=0.0, base=0, pattern=[[-rows, E], [0, P]], channel_multiplier=1))
            step(nc.gpsimd.affine_select(out=m.sel_gate[:, :, :], in_=m.sel_gate[:, :, :], compare_op=ALU.is_ge,
                                         fill=0.0, base=PARTS - 1, pattern=[[rows, E], [0, P]], channel_multiplier=-1))
            step(nc.gpsimd.affine_select(out=m.sel_mask[:, :, :], in_=m.sel_mask[:, :, :], compare_op=ALU.is_equal,
                                         fill=0.0, base=-PARTS, pattern=[[-rows, E], [0, P]], channel_multiplier=1))
            pool.sem_inc(consts_ready, 1)

        @block.tensor
        def _(pe):
            pe.wait_ge(ident_ready, 1)
            pe.wait_ge(loaded_gate, 16)
            nc.tensor.transpose(m.ps[:, 4, 0:E], graw[:, :], m.ident[0:E, 0:E]).then_inc(gate_turned, 1)
            for i in range(0, n_raw, 4):
                if i // 4 >= 4:
                    pe.wait_ge(stored, i // 4 - 3)
                for j in range(i, min(i + 4, n_raw)):
                    for k, (_, n) in enumerate(raw):
                        if j == ends[k] - n:
                            pe.wait_ge(loaded[k], 16)
                    last = nc.tensor.transpose(m.ps[:, i // 4 % 4, (j - i) * P:(j - i + 1) * P], wraw[:, j, :], m.ident[:, :])
                last.then_inc(turned, 1)
                if i == 12:
                    ahead.transpose(pe, 0)
                if i == 16:
                    pe.wait_ge(gate_stored, 1)
                    ahead.logits(pe, 0)
            pe.wait_ge(loaded_small, 16 * len(m.biases))
            nb = m.bias_rows
            nc.tensor.transpose(m.ps[:, 5, 0:nb], braw[:, :], m.ident[0:nb, 0:nb]).then_inc(turned, 1)
            pe.wait_ge(consts_ready, 1)
            ahead.transpose_gates(pe, 0)

        @block.scalar
        def _(act):
            ahead.squares(act, 0)
            ahead.store_xT(act, 0)
            ahead.exps(act, 0)

        @block.vector
        def _(dve):
            dve.wait_ge(loaded_x, 16)
            ahead.sums(dve, 0)
            ahead.variances(dve, 0)
            ahead.normalise(dve, 0)
            dve.wait_ge(gate_turned, 1)
            nc.vector.tensor_copy(m.gateT[:, :], m.ps[:, 4, 0:E]).then_inc(gate_stored, 1)
            for i in range(0, n_raw, 4):
                n = min(4, n_raw - i)
                dve.wait_ge(turned, i // 4 + 1)
                nc.vector.tensor_copy(m.wT[:, i:i + n, :], m.ps[:, i // 4 % 4, 0:n * P]).then_inc(stored, 1)
                if i == 20:
                    ahead.shift(dve, 0)
                if i == 28:
                    ahead.compare(dve, 0)
            dve.wait_ge(turned, (n_raw + 3) // 4 + 1)
            step = Chain(dve, steps)
            step(nc.vector.tensor_copy(m.biasT[:, :], m.ps[:, 5, 0:m.bias_rows]))
            nc.vector.tensor_scalar(m.qk_bias[:, 0:1], m.qk_bias_raw[:, 0:1], float(HD) ** -0.5, None, ALU.mult)
            nc.vector.tensor_copy(m.qk_bias[:, 1:2], m.qk_bias_raw[:, 1:2])
            dve.wait_ge(consts_ready, 1)
            ahead.rank_gates(dve, 0)
            ahead.pack(dve, 0)
            ahead.store_gates(dve, 0)


class Norm:

    def __init__(self, m, stack, name, src, dst=None, banks=None, scale=None, bias=None, first=0):
        self.m, self.src, self.banks, self.scale, self.bias = m, src, banks, scale, bias
        self.first = first
        tag = f"_{name}_{m.calls}"
        self.s_centred, self.s_squared, self.s_var_ready = m.sem("centred"), m.sem("squared"), m.sem("var_ready")
        self.s_rstd_ready, self.s_normed, self.s_turned = m.sem("rstd_ready"), m.sem("normed"), m.sem("turned")
        self.s_xT_ready = m.sem("xT_ready")
        self.centred = m.sb("centred" + tag, [P, TILES, D], stack=stack)
        self.square = m.sb("square" + tag, [P, TPC, D], stack=stack)
        self.dst = self.centred if dst is None else dst
        self.total, self.mean, self.total2, self.var, self.rstd = (
            m.sb(n + tag, [P, TILES], stack=stack) for n in ("total", "mean", "total2", "var", "rstd"))

    def tiles(self, c):
        return bass.ts(c, TPC)

    def count(self, c):
        return c + (1 - self.first)


    def sums(self, step, c):
        nc, t = self.m.nc, self.tiles(c)
        step(nc.vector.reduce_sum(self.total[:, t], self.src[:, t, :], AX.X))
        step(nc.vector.tensor_scalar(self.mean[:, t], self.total[:, t], 1.0 / D, None, ALU.mult))
        nc.vector.tensor_tensor(self.centred[:, t, :], self.src[:, t, :], self.mean[:, t].unsqueeze(2).to_broadcast([P, TPC, D]),
                                ALU.subtract).then_inc(self.s_centred, 1)

    def variances(self, step, c):
        nc, t = self.m.nc, self.tiles(c)
        step.engine.wait_ge(self.s_squared, self.count(c))
        step(nc.vector.reduce_sum(self.total2[:, t], self.square[:, :, :], AX.X))
        nc.vector.tensor_scalar(self.var[:, t], self.total2[:, t], 1.0 / D, LN_EPS, ALU.mult, ALU.add)\
            .then_inc(self.s_var_ready, 1)

    def normalise(self, dve, c):
        nc, t = self.m.nc, self.tiles(c)
        dve.wait_ge(self.s_rstd_ready, self.count(c))
        nc.vector.tensor_tensor(self.dst[:, t, :], self.centred[:, t, :], self.rstd[:, t].unsqueeze(2).to_broadcast([P, TPC, D]),
                                ALU.mult).then_inc(self.s_normed, 1)

    def all_chunks(self, step):
        self.sums(step, 0)
        for c in range(CHUNKS):
            self.variances(step, c)
            if c + 1 < CHUNKS:
                self.sums(step, c + 1)
            self.normalise(step.engine, c)


    def squares(self, act, c):
        act.wait_ge(self.s_centred, self.count(c))
        self.m.nc.scalar.activation(self.square[:, :, :], self.centred[:, self.tiles(c), :], ACT.Square)\
            .then_inc(self.s_squared, 1)

    def store_xT(self, act, c):
        nc, m = self.m.nc, self.m
        act.wait_ge(self.s_turned, self.count(c))
        out, bank = m.xT[:, c * CHUNK:(c + 1) * CHUNK], m.ps[:, self.banks[c % 2], :]
        if self.scale is None:
            nc.scalar.activation(out, bank, ACT.Copy).then_inc(self.s_xT_ready, 1)
        else:
            nc.scalar.activation(out, bank, ACT.Identity, bias=self.bias, scale=self.scale).then_inc(self.s_xT_ready, 1)


    def rstds(self, pool, c):
        t = self.tiles(c)
        pool.wait_ge(self.s_var_ready, self.count(c))
        self.m.nc.gpsimd.tensor_tensor(self.rstd[:, t], self.var[:, t], self.m.neg_half[:, 0:TPC], ALU.pow)\
            .then_inc(self.s_rstd_ready, 1)


    def transpose(self, pe, c):
        nc, m = self.m.nc, self.m
        pe.wait_ge(self.s_normed, self.count(c))
        if c >= 2:
            pe.wait_ge(self.s_xT_ready, c - 1)
        for j in range(TPC):
            last = nc.tensor.transpose(m.ps[:, self.banks[c % 2], j * P:(j + 1) * P], self.dst[:, c * TPC + j, :],
                                       m.ident[:, :])
        last.then_inc(self.s_turned, 1)


class Prepare:

    STEPS_NORM = 3
    STEPS_ROUTE = (11, 5, 5)

    def __init__(self, m, stack, gate, pair, bank_turn, bank_route):
        self.m, self.gate, self.pair = m, gate, pair
        self.turn, self.route = bank_turn, bank_route
        tag = f"_{m.calls}_{len(m.in_use)}"
        self.s_centred = m.sem("centred")
        self.s_squared = m.sem("squared")
        self.s_var_ready = m.sem("var_ready")
        self.s_rstd_ready = m.sem("rstd_ready")
        self.s_normed = m.sem("normed")
        self.s_turned = m.sem("turned")
        self.s_xT_ready = m.sem("xT_ready")
        self.s_logits_ready = m.sem("logits_ready")
        self.s_shifted = m.sem("shifted")
        self.s_exped = m.sem("exped")
        self.s_packed_ready = m.sem("packed_ready")
        self.s_gates_turned = m.sem("gates_turned")
        self.s_gates_ready = m.sem("gates_ready")
        self.s_norm_steps = m.sem("norm_steps")
        self.s_route_steps = m.sem("route_steps")
        self.total = m.sb("total" + tag, [P, TPC], stack=stack)
        self.mean = m.sb("mean" + tag, [P, TPC], stack=stack)
        self.centred = m.sb("centred" + tag, [P, TPC, D], stack=stack)
        self.square = m.sb("square" + tag, [P, TPC, D], stack=stack)
        self.total2 = m.sb("total2" + tag, [P, TPC], stack=stack)
        self.var = m.sb("var" + tag, [P, TPC], stack=stack)
        self.rstd = m.sb("rstd" + tag, [P, TPC], stack=stack)
        self.norm = m.sb("norm" + tag, [P, TPC, D], stack=stack)
        self.xs = m.sb("xs" + tag, [P, CHUNK], stack=stack)
        self.top = m.sb("top" + tag, [P, TPC], stack=stack)
        self.z = m.sb("z" + tag, [P, TPC * E], stack=stack)
        self.ez = m.sb("ez" + tag, [P, TPC * E], stack=stack)
        self.sum = m.sb("sum" + tag, [P, TPC], stack=stack)
        self.inv = m.sb("inv" + tag, [P, TPC], stack=stack)
        self.inv2 = m.sb("inv2" + tag, [P, TPC], stack=stack)
        self.score = m.sb("score" + tag, [P, TPC, E], stack=stack)
        self.higher = m.sb("higher" + tag, [P, TPC, E, E], stack=stack)
        self.equal = m.sb("equal" + tag, [P, TPC, E, E], stack=stack)
        self.tied = m.sb("tied" + tag, [P, TPC, E, E], stack=stack)
        self.outranked = m.sb("outranked" + tag, [P, TPC, E, E], stack=stack)
        self.rank = m.sb("rank" + tag, [P, TPC, E], stack=stack)
        self.mask = m.sb("mask" + tag, [P, TPC, E], stack=stack)
        self.gates = m.sb("gates" + tag, [P, TPC, E], stack=stack)
        self.rest = m.sb("rest" + tag, [P, TPC, E], stack=stack)
        self.rest2 = m.sb("rest2" + tag, [P, TPC, E], stack=stack)
        self.packed = m.sb("packed" + tag, [P, TPC, E, PARTS + 1], BF16, stack=stack)

    def counted(self, pool):
        pool.sem_inc(self.s_xT_ready, 2)
        pool.sem_inc(self.s_gates_ready, 1)
        pool.sem_inc(self.s_norm_steps, self.STEPS_NORM)
        for sem in (self.s_centred, self.s_squared, self.s_var_ready, self.s_rstd_ready, self.s_normed, self.s_turned,
                    self.s_logits_ready, self.s_shifted, self.s_exped, self.s_packed_ready, self.s_gates_turned):
            pool.sem_inc(sem, 1)
        pool.sem_inc(self.s_route_steps, self.route_steps())


    def sums(self, dve, c):
        nc, m = self.m.nc, self.m
        step = Chain(dve, self.s_norm_steps, c * self.STEPS_NORM)
        x = m.X[:, bass.ts(c, TPC), :]
        step(nc.vector.reduce_sum(self.total[:, :], x, AX.X))
        step(nc.vector.tensor_scalar(self.mean[:, :], self.total[:, :], 1.0 / D, None, ALU.mult))
        nc.vector.tensor_tensor(self.centred[:, :, :], x, self.mean[:, :].unsqueeze(2).to_broadcast([P, TPC, D]),
                                ALU.subtract).then_inc(self.s_centred, 1)

    def variances(self, dve, c):
        nc = self.m.nc
        step = Chain(dve, self.s_norm_steps, c * self.STEPS_NORM + 2)
        dve.wait_ge(self.s_squared, c + 1)
        step(nc.vector.reduce_sum(self.total2[:, :], self.square[:, :, :], AX.X))
        nc.vector.tensor_scalar(self.var[:, :], self.total2[:, :], 1.0 / D, LN_EPS, ALU.mult, ALU.add)\
            .then_inc(self.s_var_ready, 1)

    def normalise(self, dve, c):
        nc = self.m.nc
        dve.wait_ge(self.s_rstd_ready, c + 1)
        nc.vector.tensor_tensor(self.norm[:, :, :], self.centred[:, :, :],
                                self.rstd[:, :].unsqueeze(2).to_broadcast([P, TPC, D]), ALU.mult).then_inc(self.s_normed, 1)

    def over_e(self, a):
        return a[:, :].unsqueeze(2).to_broadcast([P, TPC, E])

    def shift(self, dve, c):
        nc, m = self.m.nc, self.m
        step = Chain(dve, self.s_route_steps, c * self.route_steps())
        logits = m.ps[:, self.route, 0:TPC * E].rearrange("p (t e) -> p t e", e=E)
        dve.wait_ge(self.s_logits_ready, c + 1)
        step(nc.vector.reduce_max(self.top[:, :], logits, AX.X))
        nc.vector.tensor_tensor(self.z[:, :].rearrange("p (t e) -> p t e", e=E), logits, self.over_e(self.top),
                                ALU.subtract).then_inc(self.s_shifted, 1)

    def route_steps(self):
        return self.STEPS_ROUTE[0] + self.STEPS_ROUTE[1 if self.pair else 2]

    def compare(self, dve, c):
        nc, m = self.m.nc, self.m
        step = Chain(dve, self.s_route_steps, c * self.route_steps() + 1)
        dve.wait_ge(self.s_exped, c + 1)
        ez = self.ez[:, :].rearrange("p (t e) -> p t e", e=E)
        step(nc.vector.reduce_sum(self.sum[:, :], ez, AX.X))
        step(nc.vector.reciprocal(self.inv[:, :], self.sum[:, :]))
        step(nc.vector.tensor_tensor(self.score[:, :, :], ez, self.over_e(self.inv), ALU.mult))
        f_side = self.score[:, :, :].unsqueeze(2).to_broadcast([P, TPC, E, E])
        e_side = self.score[:, :, :].unsqueeze(3).to_broadcast([P, TPC, E, E])
        step(nc.vector.tensor_tensor(self.higher[:, :, :, :], f_side, e_side, ALU.is_gt))
        step(nc.vector.tensor_tensor(self.equal[:, :, :, :], f_side, e_side, ALU.is_equal))

    def rank_gates(self, dve, c):
        nc, m = self.m.nc, self.m
        step = Chain(dve, self.s_route_steps, c * self.route_steps() + 6)
        below = m.below[:, :, :].rearrange("p e f -> p (e f)").unsqueeze(1).to_broadcast([P, TPC, E * E])
        flat = "p t e f -> p t (e f)"
        step(nc.vector.tensor_tensor(self.tied[:, :, :, :].rearrange(flat), self.equal[:, :, :, :].rearrange(flat), below,
                                     ALU.mult))
        step(nc.vector.tensor_tensor(self.outranked[:, :, :, :], self.higher[:, :, :, :], self.tied[:, :, :, :], ALU.add))
        step(nc.vector.reduce_sum(self.rank[:, :, :], self.outranked[:, :, :, :], AX.X))
        step(nc.vector.tensor_scalar(self.mask[:, :, :], self.rank[:, :, :], TOPK - 0.5, None, ALU.is_lt))
        step(nc.vector.tensor_tensor(self.gates[:, :, :], self.score[:, :, :], self.mask[:, :, :], ALU.mult))

    def pack(self, dve, c):
        nc, m = self.m.nc, self.m
        step = Chain(dve, self.s_route_steps, c * self.route_steps() + 11)
        if self.pair:
            if not isinstance(c, int):
                dve.wait_ge(self.s_gates_turned, c)
            step(nc.vector.tensor_copy(self.packed[:, :, :, 0], self.gates[:, :, :]))
            step(nc.vector.tensor_tensor(self.rest[:, :, :], self.gates[:, :, :], self.packed[:, :, :, 0], ALU.subtract))
            step(nc.vector.tensor_copy(self.packed[:, :, :, 1], self.rest[:, :, :]))
            step(nc.vector.tensor_tensor(self.rest2[:, :, :], self.rest[:, :, :], self.packed[:, :, :, 1], ALU.subtract))
            step(nc.vector.tensor_copy(self.packed[:, :, :, 2], self.rest2[:, :, :]))
            nc.vector.tensor_copy(self.packed[:, :, :, 3], self.mask[:, :, :]).then_inc(self.s_packed_ready, 1)
        else:
            step(nc.vector.reduce_sum(self.sum[:, :], self.gates[:, :, :], AX.X))
            step(nc.vector.reciprocal(self.inv[:, :], self.sum[:, :]))
            step(nc.vector.tensor_scalar(self.inv2[:, :], self.inv[:, :], 0.5, None, ALU.mult))
            step(nc.vector.tensor_tensor(self.rest[:, :, :], self.gates[:, :, :], self.over_e(self.inv2), ALU.mult))
            step(nc.vector.tensor_copy(m.cw[:, bass.ts(c, TPC), 0:E], self.rest[:, :, :]))

    def store_gates(self, dve, c):
        nc, m = self.m.nc, self.m
        rows = E * (PARTS + 1)
        dve.wait_ge(self.s_gates_turned, c + 1)
        nc.vector.tensor_copy(m.gT[0:rows, bass.ts(c, CHUNK)], m.ps[0:rows, self.route, :].bitcast(BF16)[:, 0:CHUNK])\
            .then_inc(self.s_gates_ready, 1)


    def squares(self, act, c):
        act.wait_ge(self.s_centred, c + 1)
        self.m.nc.scalar.activation(self.square[:, :, :], self.centred[:, :, :], ACT.Square).then_inc(self.s_squared, 1)

    def store_xT(self, act, c):
        nc, m = self.m.nc, self.m
        act.wait_ge(self.s_turned, c + 1)
        if not isinstance(c, int):
            act.wait_ge(self.s_logits_ready, c)
        nc.scalar.activation(self.xs[:, :], m.ps[:, self.turn, :], ACT.Copy).then_inc(self.s_xT_ready, 1)
        nc.scalar.activation(m.xT[:, bass.ts(c, CHUNK)], m.ps[:, self.turn, :], ACT.Copy).then_inc(self.s_xT_ready, 1)

    def exps(self, act, c):
        act.wait_ge(self.s_shifted, c + 1)
        self.m.nc.scalar.activation(self.ez[:, :], self.z[:, :], ACT.Exp).then_inc(self.s_exped, 1)


    def rstds(self, pool, c):
        pool.wait_ge(self.s_var_ready, c + 1)
        self.m.nc.gpsimd.tensor_tensor(self.rstd[:, :], self.var[:, :], self.m.neg_half[:, 0:TPC], ALU.pow)\
            .then_inc(self.s_rstd_ready, 1)

    def exps_as_powers(self, pool, c):
        pool.wait_ge(self.s_shifted, c + 1)
        self.m.nc.gpsimd.tensor_tensor(self.ez[:, :], self.m.euler[:, :], self.z[:, :], ALU.pow).then_inc(self.s_exped, 1)


    def transpose(self, pe, c):
        nc, m = self.m.nc, self.m
        pe.wait_ge(self.s_normed, c + 1)
        if not isinstance(c, int):
            pe.wait_ge(self.s_xT_ready, c * 2)
        for j in range(TPC):
            last = nc.tensor.transpose(m.ps[:, self.turn, j * P:(j + 1) * P], self.norm[:, j, :], m.ident[:, :])
        last.then_inc(self.s_turned, 1)

    def logits(self, pe, c):
        nc, m = self.m.nc, self.m
        pe.wait_ge(self.s_xT_ready, c * 2 + 1)
        for j in range(TPC):
            last = nc.tensor.matmul(m.ps[:, self.route, j * E:(j + 1) * E], self.xs[:, j * P:(j + 1) * P], self.gate[:, :],
                                    start=True, stop=True)
        last.then_inc(self.s_logits_ready, 1)

    def transpose_gates(self, pe, c):
        nc, m = self.m.nc, self.m
        rows = E * (PARTS + 1)
        pe.wait_ge(self.s_packed_ready, c + 1)
        for j in range(TPC):
            last = nc.tensor.transpose(m.ps[0:rows, self.route, :].bitcast(BF16)[:, j * P:(j + 1) * P],
                                       self.packed[:, j, :, :].rearrange("p e r -> p (e r)"), m.identb[:, :])
        last.then_inc(self.s_gates_turned, 1)


def moe0(m, loads=(), then_moe1=False):
    nc = m.nc
    tag = m.stage()
    bc_ready, xg_ready, up_ready, x3_ready = m.sem("bc_ready"), m.sem("xg_ready"), m.sem("up_ready"), m.sem("x3_ready")
    mask_bc = m.sem("mask_bc")
    hid_ready, x3b_ready, x3m_ready, y_ready = m.sem("hid_ready"), m.sem("x3b_ready"), m.sem("x3m_ready"), m.sem("y_ready")
    prod_ready, summed, sh_silu, sh_hid = m.sem("prod_ready"), m.sem("summed"), m.sem("sh_silu"), m.sem("sh_hid")
    sh_a, sh_b, sh_out, first_sum = m.sem("sh_a"), m.sem("sh_b"), m.sem("sh_out"), m.sem("first_sum")
    y_turned = m.sem("y_turned")
    GB, MB, HB, TB, YB, ZB, NB = [0, 1], 2, 3, 4, 5, 6, 7
    with ExitStack() as stack:
        xg = m.sb("xg" + tag, [P, 2, CHUNK], stack=stack)
        hid = m.sb("hid" + tag, [P, 2, CHUNK], stack=stack)
        x3b = m.sb("x3b" + tag, [P, 2, CHUNK], stack=stack)
        x3m = m.sb("x3m" + tag, [P, 2, CHUNK], stack=stack)
        prod = m.sb("prod" + tag, [P, 2, CHUNK], stack=stack)
        acc = m.sb("acc" + tag, [P, 2, CHUNK], stack=stack)
        shs = m.sb("shs" + tag, [P, SH0, CHUNK], stack=stack)
        shh = m.sb("shh" + tag, [P, SH0, CHUNK], stack=stack)
        prep = Prepare(m, stack, m.gateT, True, NB, ZB)
        ahead = Prepare(m, stack, m.router, False, NB, ZB) if then_moe1 else None
        loaded = m.sem("loaded")
        block = stack.enter_context(nc.Block())

        @block.sync
        def _(sp):
            for dst, src in loads:
                sp.dma_start(dst, src).then_inc(loaded, 16)
            if loads:
                sp.wait_ge(loaded, 16 * len(loads))

        @block.tensor
        def _(pe):
            def broadcast_gate(c, e):
                if e >= 2:
                    pe.wait_ge(xg_ready, c * E + (e - 1))
                nc.tensor.matmul(m.ps[:, GB[e % 2], :], m.sel_gate[:, e, :], m.gT[:, bass.ts(c, CHUNK)],
                                 start=True, stop=True).then_inc(bc_ready, 1)

            def broadcast_mask(c, e):
                if e >= 1:
                    pe.wait_ge(x3m_ready, c * E + e)
                nc.tensor.matmul(m.ps[:, MB, :], m.sel_mask[:, e, :], m.gT[:, bass.ts(c, CHUNK)],
                                 start=True, stop=True).then_inc(mask_bc, 1)

            def down(c, e):
                pe.wait_ge(hid_ready, c * E + (e + 1))
                if e >= 1:
                    pe.wait_ge(prod_ready, c * E + e)
                nc.tensor.matmul(m.ps[:, YB, :], m.w2T[:, e, :], hid[:, e % 2, :], start=True, stop=True)\
                    .then_inc(y_ready, 1)

            def turn_back(c):
                pe.wait_ge(summed, c * (E - 1) + (E - 1))
                for j in range(TPC):
                    last = nc.tensor.transpose(m.ps[:, NB, j * P:(j + 1) * P], acc[:, (E - 1) % 2, j * P:(j + 1) * P],
                                               m.ident[:, :])
                last.then_inc(y_turned, 1)

            def head(c, first=False):
                x_c = m.xT[:, bass.ts(c, CHUNK)]
                pe.wait_ge(prep.s_xT_ready, c * 2 + 2)
                for i in range(SH0):
                    if i >= 1:
                        pe.wait_ge(sh_silu, c * SH0 + i)
                    elif not first:
                        pe.wait_ge(hid_ready, c * E)
                    nc.tensor.matmul(m.ps[:, HB, :], m.sw1T[:, i, :], x_c, start=True, stop=True).then_inc(sh_a, 1)
                    if i == SH0 - 1:
                        if not first:
                            pe.wait_ge(xg_ready, c * E)
                            pe.wait_ge(x3m_ready, c * E)
                        pe.wait_ge(prep.s_gates_ready, c + 1)
                        broadcast_gate(c, 0)
                        if not first:
                            turn_back(c - 1)
                    if i >= 1:
                        pe.wait_ge(sh_hid, c * SH0 + i)
                    elif not first:
                        pe.wait_ge(x3b_ready, c * E)
                    nc.tensor.matmul(m.ps[:, TB, :], m.sw2T[:, i, :], x_c, start=True, stop=True).then_inc(sh_b, 1)

            def chunk(c, more, route, n):
                for e in range(E):
                    if e + 1 < E:
                        broadcast_gate(c, e + 1)
                    if e == 0:
                        pe.wait_ge(sh_silu, c * SH0 + SH0)
                    else:
                        pe.wait_ge(hid_ready, c * E + e)
                    pe.wait_ge(xg_ready, c * E + (e + 1))
                    nc.tensor.matmul(m.ps[:, HB, :], m.w1T[:, e, :], xg[:, e % 2, :], start=True, stop=True)\
                        .then_inc(up_ready, 1)
                    if route and e == 4:
                        route.logits(pe, n)
                    if e == 0:
                        pe.wait_ge(sh_hid, c * SH0 + SH0)
                    else:
                        pe.wait_ge(x3b_ready, c * E + e)
                    nc.tensor.matmul(m.ps[:, TB, :], m.w3T[:, e, :], xg[:, e % 2, :], start=True, stop=True)\
                        .then_inc(x3_ready, 1)
                    broadcast_mask(c, e)
                    if e == 0:
                        for i in range(SH0):
                            last = nc.tensor.matmul(m.ps[:, ZB, :], m.sw3T[:, i, :], shh[:, i, :],
                                                    start=(i == 0), stop=(i == SH0 - 1))
                        last.then_inc(sh_out, 1)
                    else:
                        down(c, e - 1)
                    if route and e == 3:
                        pe.wait_ge(first_sum, c + 1)
                        route.transpose(pe, n)
                if more:
                    prep.transpose_gates(pe, c + 1)
                down(c, E - 1)
                if more:
                    head(c + 1)
                else:
                    turn_back(c)

            head(0, True)
            with pe.Fori(0, CHUNKS - 1) as c:
                chunk(c, True, prep, c + 1)
            chunk(CHUNKS - 1, False, ahead, 0)

        @block.scalar
        def _(act):
            def head(c):
                for i in range(SH0):
                    act.wait_ge(sh_a, c * SH0 + (i + 1))
                    nc.scalar.activation(shs[:, i, :], m.ps[:, HB, :], ACT.Silu).then_inc(sh_silu, 1)

            def chunk(c, more, route, n):
                for e in range(E):
                    act.wait_ge(up_ready, c * E + (e + 1))
                    if e >= 2:
                        act.wait_ge(y_ready, c * E + (e - 1))
                    nc.scalar.activation(hid[:, e % 2, :], m.ps[:, HB, :], ACT.Silu, bias=m.b1[:, e:e + 1])\
                        .then_inc(hid_ready, 1)
                    act.wait_ge(x3_ready, c * E + (e + 1))
                    if e >= 2:
                        act.wait_ge(x3m_ready, c * E + (e - 1))
                    nc.scalar.activation(x3b[:, e % 2, :], m.ps[:, TB, :], ACT.Identity, bias=m.b3[:, e:e + 1])\
                        .then_inc(x3b_ready, 1)
                    if route and e == 0:
                        route.squares(act, n)
                    if route and e == 3:
                        route.store_xT(act, n)
                    if route and e == 4:
                        route.exps(act, n)
                if more:
                    head(c + 1)

            head(0)
            with act.Fori(0, CHUNKS - 1) as c:
                chunk(c, True, prep, c + 1)
            chunk(CHUNKS - 1, False, ahead, 0)

        @block.vector
        def _(dve):
            def gate_x(c, e):
                dve.wait_ge(bc_ready, c * E + (e + 1))
                if e >= 2:
                    dve.wait_ge(x3_ready, c * E + (e - 1))
                nc.vector.tensor_tensor(xg[:, e % 2, :], m.ps[:, GB[e % 2], :], m.xT[:, bass.ts(c, CHUNK)], ALU.mult)\
                    .then_inc(xg_ready, 1)

            def mask_x3(c, e):
                dve.wait_ge(x3b_ready, c * E + (e + 1))
                dve.wait_ge(mask_bc, c * E + (e + 1))
                if e >= 2:
                    dve.wait_ge(prod_ready, c * E + (e - 1))
                nc.vector.tensor_tensor(x3m[:, e % 2, :], m.ps[:, MB, :], x3b[:, e % 2, :], ALU.mult)\
                    .then_inc(x3m_ready, 1)

            def product(c, e):
                dve.wait_ge(y_ready, c * E + (e + 1))
                dve.wait_ge(x3m_ready, c * E + (e + 1))
                if e >= 2:
                    dve.wait_ge(summed, c * (E - 1) + max(1, e - 2))
                nc.vector.scalar_tensor_tensor(out=prod[:, e % 2, :], in0=m.ps[:, YB, :], scalar=m.b2[:, e:e + 1],
                                               in1=x3m[:, e % 2, :], op0=ALU.add, op1=ALU.mult).then_inc(prod_ready, 1)

            def head(c):
                for i in range(SH0):
                    dve.wait_ge(sh_b, c * SH0 + (i + 1))
                    dve.wait_ge(sh_silu, c * SH0 + (i + 1))
                    nc.vector.tensor_tensor(shh[:, i, :], m.ps[:, TB, :], shs[:, i, :], ALU.mult).then_inc(sh_hid, 1)
                    if i == 0:
                        gate_x(c, 0)

            def update(c):
                dve.wait_ge(y_turned, c + 1)
                x_t = m.X[:, bass.ts(c, TPC), :].rearrange("p t d -> p (t d)")
                nc.vector.scalar_tensor_tensor(out=x_t, in0=m.ps[:, NB, :], scalar=0.5, in1=x_t,
                                               op0=ALU.mult, op1=ALU.add)

            def chunk(c, more, route, n):
                for e in range(E):
                    if e + 1 < E:
                        gate_x(c, e + 1)
                    if route:
                        piece = (route.sums, route.variances, route.normalise, None, route.shift, route.compare,
                                 route.rank_gates, route.pack)[e]
                        if piece is not None:
                            piece(dve, n)
                    mask_x3(c, e)
                    if e >= 1:
                        product(c, e - 1)
                    if e == 1:
                        dve.wait_ge(prod_ready, c * E + 1)
                        dve.wait_ge(sh_out, c + 1)
                        nc.vector.tensor_tensor(acc[:, 0, :], m.ps[:, ZB, :], prod[:, 0, :], ALU.add).then_inc(first_sum, 1)
                if more:
                    prep.store_gates(dve, c + 1)
                product(c, E - 1)
                if more:
                    head(c + 1)
                update(c)

            head(0)
            with dve.Fori(0, CHUNKS - 1) as c:
                chunk(c, True, prep, c + 1)
            chunk(CHUNKS - 1, False, ahead, 0)

        @block.gpsimd
        def _(pool):
            def chunk(c, more, route, n):
                for e in range(1, E):
                    if route and e == 1:
                        route.rstds(pool, n)
                    pool.wait_ge(prod_ready, c * E + (e + 1))
                    if e == 1:
                        pool.wait_ge(first_sum, c + 1)
                    else:
                        pool.wait_ge(summed, c * (E - 1) + (e - 1))
                    nc.gpsimd.tensor_tensor(acc[:, e % 2, :], acc[:, (e - 1) % 2, :], prod[:, e % 2, :], ALU.add)\
                        .then_inc(summed, 1)

            prep.counted(pool)
            with pool.Fori(0, CHUNKS - 1) as c:
                chunk(c, True, prep, c + 1)
            chunk(CHUNKS - 1, False, ahead, 0)


def moe1(m, out=None, then_norm=False):
    nc = m.nc
    tag = m.stage()
    NE = E + 1
    a_ready, b_ready, silu_done, hid_ready = m.sem("a_ready"), m.sem("b_ready"), m.sem("silu_done"), m.sem("hid_ready")
    y_ready, y_used = m.sem("y_ready"), m.sem("y_used")
    AB, BB, YB, NB, RB = [0, 1], [2, 3], [4, 5], 6, 7
    with ExitStack() as stack:
        silu = m.sb("silu" + tag, [P, HID1, CHUNK], stack=stack)
        hid = m.sb("hid1" + tag, [P, 2, HID1, CHUNK], stack=stack)
        prep = Prepare(m, stack, m.router, False, NB, RB)
        stored, after_steps = m.sem("stored"), m.sem("after_steps")
        after = Norm(m, stack, "after", m.X, m.xn) if then_norm else None
        block = stack.enter_context(nc.Block())

        @block.sync
        def _(sp):
            if out is not None:
                for c in range(CHUNKS):
                    sp.wait_ge(y_used, (c + 1) * NE)
                    sp.dma_start(out[0, c * CHUNK:(c + 1) * CHUNK, :].rearrange("(t p) d -> p t d", p=P),
                                 m.X[:, c * TPC:(c + 1) * TPC, :]).then_inc(stored, 16)
                sp.wait_ge(stored, 16 * CHUNKS)

        @block.tensor
        def _(pe):
            def chunk(c, more, norm=None):
                x_c = m.xT[:, bass.ts(c, CHUNK)]

                def down(e):
                    pe.wait_ge(hid_ready, c * (NE * HID1) + HID1 * (e + 1))
                    if e >= 2:
                        pe.wait_ge(y_used, c * NE + (e - 1))
                    for j in range(TPC):
                        for i in range(HID1):
                            last = nc.tensor.matmul(m.ps[:, YB[e % 2], j * P:(j + 1) * P],
                                                    hid[:, e % 2, i, j * P:(j + 1) * P], m.ew2[:, e, i, :],
                                                    start=(i == 0), stop=(i == HID1 - 1))
                    last.then_inc(y_ready, 1)

                pe.wait_ge(prep.s_xT_ready, c * 2 + 2)
                for e in range(NE):
                    for i in range(HID1):
                        if e >= 1:
                            pe.wait_ge(silu_done, c * (NE * HID1) + ((e - 1) * HID1 + i + 1))
                        nc.tensor.matmul(m.ps[:, AB[i], :], m.ew1[:, e, i * P:(i + 1) * P], x_c, start=True, stop=True)\
                            .then_inc(a_ready, 1)
                        if e >= 1:
                            pe.wait_ge(hid_ready, c * (NE * HID1) + ((e - 1) * HID1 + i + 1))
                        nc.tensor.matmul(m.ps[:, BB[i], :], m.ew3[:, e, i * P:(i + 1) * P], x_c, start=True, stop=True)\
                            .then_inc(b_ready, 1)
                    if e >= 1:
                        down(e - 1)
                    if more and e == 3:
                        prep.transpose(pe, c + 1)
                    if more and e == 4:
                        prep.logits(pe, c + 1)
                down(NE - 1)
                pe.wait_ge(y_used, c * NE + (NE - 1))

            with pe.Fori(0, CHUNKS - 1) as c:
                chunk(c, True)
            chunk(CHUNKS - 1, False)

        @block.scalar
        def _(act):
            def chunk(c, more, norm=None):
                for e in range(NE):
                    for i in range(HID1):
                        act.wait_ge(a_ready, c * (NE * HID1) + (e * HID1 + i + 1))
                        if e >= 1:
                            act.wait_ge(hid_ready, c * (NE * HID1) + ((e - 1) * HID1 + i + 1))
                        nc.scalar.activation(silu[:, i, :], m.ps[:, AB[i], :], ACT.Silu).then_inc(silu_done, 1)
                    if more and e == 0:
                        prep.squares(act, c + 1)
                    if norm and e == 4:
                        after.squares(act, c - 1)
                    if more and e == 3:
                        prep.store_xT(act, c + 1)

            chunk(0, True)
            with act.Fori(1, CHUNKS - 1) as c:
                chunk(c, True, after)
            chunk(CHUNKS - 1, False, after)

        @block.vector
        def _(dve):
            def chunk(c, more, norm=None):
                x_t = m.X[:, bass.ts(c, TPC), :]
                cw = m.cw[:, bass.ts(c, TPC), :]

                def add(e):
                    dve.wait_ge(y_ready, c * NE + (e + 1))
                    if e >= 1:
                        dve.wait_ge(y_used, c * NE + e)
                    for j in range(TPC):
                        last = nc.vector.scalar_tensor_tensor(out=x_t[:, j, :], in0=m.ps[:, YB[e % 2], j * P:(j + 1) * P],
                                                              scalar=cw[:, j, e:e + 1], in1=x_t[:, j, :],
                                                              op0=ALU.mult, op1=ALU.add)
                    last.then_inc(y_used, 1)

                for e in range(NE):
                    for i in range(HID1):
                        dve.wait_ge(b_ready, c * (NE * HID1) + (e * HID1 + i + 1))
                        dve.wait_ge(silu_done, c * (NE * HID1) + (e * HID1 + i + 1))
                        if e >= 2:
                            dve.wait_ge(y_ready, c * NE + (e - 1))
                        nc.vector.tensor_tensor(hid[:, e % 2, i, :], m.ps[:, BB[i], :], silu[:, i, :], ALU.mult)\
                            .then_inc(hid_ready, 1)
                    if e >= 1:
                        add(e - 1)
                    if more:
                        if e == 0:
                            prep.sums(dve, c + 1)
                        if e == 1:
                            prep.variances(dve, c + 1)
                        if e == 2:
                            prep.normalise(dve, c + 1)
                        if e == 5:
                            prep.shift(dve, c + 1)
                        if e == 6:
                            prep.compare(dve, c + 1)
                        if e == 7:
                            prep.rank_gates(dve, c + 1)
                        if e == 8:
                            prep.pack(dve, c + 1)
                    if norm:
                        if e == 3:
                            after.sums(Chain(dve, after_steps, (c - 1) * 3), c - 1)
                        if e == 4:
                            after.variances(Chain(dve, after_steps, (c - 1) * 3 + 2), c - 1)
                        if e == 6:
                            after.normalise(dve, c - 1)
                add(NE - 1)

            chunk(0, True)
            with dve.Fori(1, CHUNKS - 1) as c:
                chunk(c, True, after)
            chunk(CHUNKS - 1, False, after)

        @block.gpsimd
        def _(pool):
            prep.counted(pool)
            for c in range(1, CHUNKS):
                prep.rstds(pool, c)
                if after and c >= 2:
                    after.rstds(pool, c - 2)
                prep.exps_as_powers(pool, c)
            if after:
                after.rstds(pool, CHUNKS - 2)


def softmax_attention(m):
    nc = m.nc
    tag = m.stage()
    scale = float(HD) ** -0.5
    dram_q = nc.dram_tensor("q_parts", [PARTS, D, T], BF16, kind="Internal").ap()
    dram_k = nc.dram_tensor("k_parts", [PARTS, D, T], BF16, kind="Internal").ap()
    kv_stack = ExitStack()
    key_rows = dram_k.rearrange("j (h e) t -> j e h t", e=HD)
    query_rows = dram_q.rearrange("i (h e) t -> i e h t", e=HD)
    values = m.sb("values", [P, GROUPS, TILES, GH, VC], stack=kv_stack)
    q = m.sb("q", [ROWS_M, CHUNKS, GH, CHUNK], BF16, stack=kv_stack)
    k1 = m.sb("k1", [ROWS, GH, T], BF16, stack=kv_stack)
    neg_part = m.sb("neg_part", [P, TPC, 32], BF16, stack=kv_stack)
    zeros = m.sb("zeros", [P, CHUNK], BF16, stack=kv_stack)
    own_row = m.sb("own_row", [P, GH], BF16, stack=kv_stack)

    proj, f32_ready, hi_ready, steps = m.sem("proj"), m.sem("f32_ready"), m.sem("hi_ready"), m.sem("part_steps")
    parts_ready, parts_out, v_ready = m.sem("parts_ready"), [m.sem(f"parts_out{i}") for i in range(PART_RING)], m.sem("v_ready")
    preloaded, pool_steps = m.sem("preloaded"), m.sem("pool_steps")
    sides = [(0, scale, dram_q), (1, 1.0, dram_k)]
    jobs = [(0, 0)] + [(1, c) for c in range(CHUNKS)] + [(0, c) for c in range(1, CHUNKS)]
    with ExitStack() as stack:
        full = m.sb("full" + tag, [P, 2, CHUNK], stack=stack)
        rest = m.sb("rest" + tag, [P, CHUNK], stack=stack)
        part = m.sb("part" + tag, [P, PART_RING, PARTS, CHUNK], BF16, stack=stack)
        norm = Norm(m, stack, "norm", m.X, None, [6, 7])
        block = stack.enter_context(nc.Block())

        @block.gpsimd
        def _(pool):
            for c in range(CHUNKS):
                norm.rstds(pool, c)
            step = Chain(pool, pool_steps)
            step(nc.gpsimd.memset(own_row[:, :], 0.0))
            for i in range(PARTS):
                step(nc.gpsimd.affine_select(out=own_row[:, :], in_=own_row[:, :], compare_op=ALU.not_equal, fill=1.0,
                                             base=-(ROWS + i * GH), pattern=[[-1, GH]], channel_multiplier=1))
            nc.gpsimd.memset(zeros[:, :], 0.0)
            nc.gpsimd.memset(neg_part[:, :, :], 0.0)

        @block.tensor
        def _(pe):
            norm.transpose(pe, 0)
            norm.transpose(pe, 1)
            for n, (s, c) in enumerate(jobs):
                if s == 1 or c == 0:
                    pe.wait_ge(norm.s_xT_ready, c + 1)
                if n >= 2:
                    pe.wait_ge(hi_ready, n - 1)
                nc.tensor.matmul(m.ps[:, n % 2, :], m.qkvT[:, s, :], m.xT[:, c * CHUNK:(c + 1) * CHUNK],
                                 start=True, stop=True).then_inc(proj, 1)
                if s == 1:
                    for j in range(TPC):
                        t = c * TPC + j
                        last = nc.tensor.matmul(m.ps[:, 2 + c, j * P:(j + 1) * P], m.xT[:, t * P:(t + 1) * P],
                                                m.qkvT[:, 2, :], start=True, stop=True)
                    last.then_inc(v_ready, 1)
                    if c + 2 < CHUNKS:
                        norm.transpose(pe, c + 2)

        @block.scalar
        def _(act):
            norm.squares(act, 0)
            norm.squares(act, 1)
            norm.store_xT(act, 0)
            norm.squares(act, 2)
            norm.squares(act, 3)
            for n, (s, c) in enumerate(jobs):
                if s == 1 and c >= 1:
                    norm.store_xT(act, c)
                act.wait_ge(proj, n + 1)
                if n >= 2:
                    act.wait_ge(parts_ready, n - 1)
                nc.scalar.activation(full[:, n % 2, :], m.ps[:, n % 2, :], ACT.Identity, bias=m.qk_bias[:, s:s + 1],
                                     scale=sides[s][1]).then_inc(f32_ready, 1)
                act.wait_ge(f32_ready, n + 1)
                if n >= PART_RING:
                    act.wait_ge(parts_out[n % PART_RING], 16 * (n // PART_RING))
                nc.scalar.activation(part[:, n % PART_RING, 0, :], full[:, n % 2, :], ACT.Copy).then_inc(hi_ready, 1)

        @block.vector
        def _(dve):
            step = Chain(dve, steps)
            norm.all_chunks(step)
            nc.vector.memset(values[:, :, :, :, HD:VC], 1.0)
            for n, (s, c) in enumerate(jobs):
                dve.wait_ge(hi_ready, n + 1)
                if n >= PART_RING:
                    dve.wait_ge(parts_out[n % PART_RING], 16 * (n // PART_RING))
                step(nc.vector.tensor_tensor(rest[:, :], full[:, n % 2, :], part[:, n % PART_RING, 0, :], ALU.subtract))
                step(nc.vector.tensor_copy(part[:, n % PART_RING, 1, :], rest[:, :]))
                nc.vector.tensor_tensor(part[:, n % PART_RING, 2, :], rest[:, :], part[:, n % PART_RING, 1, :], ALU.subtract)\
                    .then_inc(parts_ready, 1)
                dve.wait_ge(parts_ready, n + 1)
                if s == 1:
                    dve.wait_ge(v_ready, c + 1)
                    for j in range(TPC):
                        nc.vector.tensor_tensor(
                            values[:, :, c * TPC + j, :, 0:HD],
                            m.ps[:, 2 + c, j * P:(j + 1) * P].rearrange("p (g h e) -> p g h e", h=GH, e=HD),
                            m.v_bias[:, :].rearrange("p (g h e) -> p g h e", h=GH, e=HD), ALU.add)

        @block.sync
        def _(sp):
            def write(n):
                s, c = jobs[n]
                sp.wait_ge(parts_ready, n + 1)
                sp.dma_start(sides[s][2][:, :, c * CHUNK:(c + 1) * CHUNK].rearrange("i p t -> p i t"),
                             part[:, n % PART_RING, :, :]).then_inc(parts_out[n % PART_RING], 16)

            def written(n):
                sp.wait_ge(parts_out[n % PART_RING], 16 * (n // PART_RING + 1))

            def load_keys(half):
                t = slice(half * (T // 2), (half + 1) * (T // 2))
                for i in range(PARTS):
                    for j in range(PARTS):
                        r = (i * PARTS + j) * HD
                        sp.dma_start(k1[r:r + HD, :, t], key_rows[j, :, 0:GH, t]).then_inc(preloaded, 16)

            write(0)
            write(1)
            written(0)
            for i in range(PARTS):
                for j in range(PARTS):
                    r = (i * PARTS + j) * HD
                    sp.dma_start(q[r:r + HD, 0, :, :], query_rows[i, :, 0:GH, 0:CHUNK]).then_inc(preloaded, 16)
            write(2)
            write(3)
            written(1)
            written(2)
            load_keys(0)
            write(4)
            write(5)
            write(6)
            written(3)
            written(4)
            load_keys(1)
            write(7)
            for i in range(PART_RING):
                sp.wait_ge(parts_out[i], 16 * len(jobs) // PART_RING)
            sp.wait_ge(preloaded, 16 * PARTS * PARTS * (1 + 2))

    m.stage()
    UNITS = GROUPS * CHUNKS
    STEPS = TILES * GH
    PAIRS = STEPS // 2
    q_loaded = [m.sem(f"q_loaded{i}") for i in range(CHUNKS)]
    k1_loaded = [m.sem(f"k1_loaded{i}") for i in range(GH)]
    k2_loaded = [m.sem(f"k2_loaded{i}") for i in range(2)]
    v_loaded = [m.sem(f"v_loaded{i}") for i in range(2)]
    s1_ready, s1_used = m.sem("s1_ready"), m.sem("s1_used")
    ones_stored, pool_steps = m.sem("ones_stored"), m.sem("pool_steps")
    max_turned, max_loaded = m.sem("max_turned"), m.sem("max_loaded")
    s2_ready, exped, av_done, out_stored = m.sem("s2_ready"), m.sem("exped"), m.sem("av_done"), m.sem("out_stored")
    max_steps = m.sem("max_steps")
    att_stack = ExitStack()
    outs = m.sb("outs", [P, UNITS, CHUNK], stack=att_stack)
    with ExitStack() as stack:
        k2 = m.sb("k2", [ROWS_M, GH, T], BF16, stack=stack)
        v = m.sb("v", [P, TILES, GH, VC], stack=stack)
        ex = [m.xT[:, :].rearrange("p (h t) -> p h t", t=CHUNK),
              m.xn[:, :, :].rearrange("p (h a) d -> p h (a d)", a=TPC)]
        mx = m.sb("mx", [P, GH, TPC, CHUNKS // 2], stack=stack)
        neg = m.sb("neg", [P, GH, TPC], stack=stack)
        neg_rest = m.sb("neg_rest", [P, 2, GH, TPC], stack=stack)
        neg_turned = m.sb("neg_turned", [P, 32, TPC], BF16, stack=stack)
        S1B, S2B, AVB = [0, 1, 2, 3], [4, 5, 6], 7
        S2_BANK = [S2B[s % 3] for s in range(STEPS - 1)] + [S2B[1]]
        S2_SINCE = [next(d for d in range(1, STEPS) if S2_BANK[s - d] == S2_BANK[s]) for s in range(STEPS)]
        done = [max(0, (k + 1 - HOLE) * STEPS // (STEPS - HOLE)) for k in range(-1, STEPS)]
        S1_IN = [range(done[k], done[k + 1]) for k in range(STEPS)]
        block = stack.enter_context(nc.Block())

        DMAS_M = 16 * (P // 32)
        DMAS_Q = 16 * PARTS * PARTS
        DMAS_K = 16 * PARTS * PARTS

        def load_q(eng, g, qc):
            for i in range(PARTS):
                for j in range(PARTS):
                    r = (i * PARTS + j) * HD
                    eng.dma_start(q[r:r + HD, qc, :, :],
                                  query_rows[i, :, bass.ts(g, GH), qc * CHUNK:(qc + 1) * CHUNK]).then_inc(q_loaded[qc], 16)

        def load_k1(eng, g, h):
            for i in range(PARTS):
                for j in range(PARTS):
                    r = (i * PARTS + j) * HD
                    eng.dma_start(k1[r:r + HD, h, :], key_rows[j, :, bass.ts(g * GH + h, 1), :])\
                        .then_inc(k1_loaded[h], 16)

        def load_k2(eng, g, half):
            t = slice(half * (T // 2), (half + 1) * (T // 2))
            for i in range(PARTS):
                for j in range(PARTS):
                    r = (i * PARTS + j) * HD
                    eng.dma_start(k2[r:r + HD, :, t], key_rows[j, :, bass.ts(g, GH), t]).then_inc(k2_loaded[half], 16)

        def load_v(eng, g, half):
            t = slice(half * (TILES // 2), (half + 1) * (TILES // 2))
            eng.dma_start(v[:, t, :, :], values[:, bass.ts(g, 1), t, :, :].rearrange("p g t h e -> p (g t) h e"))\
                .then_inc(v_loaded[half], 16)

        @block.sync
        def _(sp):
            load_q(sp, 0, 1)
            sp.wait_ge(ones_stored, 1)
            for half in range(2):
                load_k2(sp, 0, half)
                load_v(sp, 0, half)
            load_q(sp, 0, 2)

            def load_maxima(u, qc):
                sp.wait_ge(max_turned, u + 1)
                for b in range(P // 32):
                    rows = neg_turned[b * 32:b * 32 + PARTS * GH, :, :].rearrange("r j t -> r (j t)").unsqueeze(1)\
                        .to_broadcast([PARTS * GH, GH, P])
                    sp.dma_start(q[ROWS:ROWS_M, qc, :, b * P:(b + 1) * P], rows).then_inc(max_loaded, 16)

            def unit(g, qc, last):
                u = g * CHUNKS + qc
                load_next_q(g, qc, last)
                if qc == CHUNKS - 2 and not last:
                    for h in range(GH):
                        if h == GH - 1:
                            load_maxima(u + 1, CHUNKS - 1)
                        sp.wait_ge(s1_ready, (u + 1) * PAIRS + (h + 1) * PAIRS // GH)
                        load_k1(sp, g + 1, h)
                elif qc == CHUNKS - 1 and not last:
                    for half in range(2):
                        if half == 1:
                            load_maxima(u + 1, 0)
                        sp.wait_ge(s2_ready, u * STEPS + (half + 1) * STEPS // 2)
                        load_k2(sp, g + 1, half)
                        sp.wait_ge(av_done, u * TILES + (half + 1) * TILES // 2)
                        load_v(sp, g + 1, half)
                elif qc < CHUNKS - 1:
                    load_maxima(u + 1, qc + 1)

            def load_next_q(g, qc, last):
                if last and qc >= 1:
                    return
                u = g * CHUNKS + qc
                if qc == 0:
                    if not isinstance(g, int) or g > 0:
                        sp.wait_ge(s2_ready, u * STEPS)
                    load_q(sp, g, 3)
                else:
                    sp.wait_ge(s2_ready, u * STEPS)
                    load_q(sp, g + 1, qc - 1)

            load_maxima(0, 0)
            for qc in range(CHUNKS):
                unit(0, qc, False)
            with sp.Fori(1, GROUPS - 1) as g:
                for qc in range(CHUNKS):
                    unit(g, qc, False)
            for qc in range(CHUNKS):
                unit(GROUPS - 1, qc, True)

        @block.gpsimd
        def _(pool):
            step = Chain(pool, pool_steps)
            step(nc.gpsimd.tensor_tensor(m.X[:, :, :], m.X[:, :, :], m.proj_bias[:, :].unsqueeze(1).to_broadcast([P, TILES, D]),
                                         ALU.add))
            step(nc.gpsimd.memset(m.pick[:, :, :], 1.0))
            pick = m.pick[:, :, :].rearrange("p c (g v) -> p c g v", v=HD)
            step(nc.gpsimd.affine_select(out=pick, in_=pick, compare_op=ALU.is_ge, fill=0.0, base=0,
                                         pattern=[[0, HD], [-HD, H], [0, HD]], channel_multiplier=1))
            step(nc.gpsimd.affine_select(out=pick, in_=pick, compare_op=ALU.is_ge, fill=0.0, base=HD - 1,
                                         pattern=[[0, HD], [HD, H], [0, HD]], channel_multiplier=-1))
            step(nc.gpsimd.tensor_copy(m.same_head[:, :], m.pick[:, 0, :]))
            step(nc.gpsimd.affine_select(out=pick, in_=pick, compare_op=ALU.is_equal, fill=0.0, base=0,
                                         pattern=[[1, HD], [0, H], [-1, HD]], channel_multiplier=0))
            step(nc.gpsimd.tensor_copy(m.dec_rep[:, :].rearrange("p (h k) -> p h k", k=HD),
                                       m.dec_w[:, :].unsqueeze(2).to_broadcast([P, H, HD])))
            for v in range(HD):
                step(nc.gpsimd.tensor_copy(
                    m.v_rep[:, v, :].rearrange("p (h k) -> p h k", k=HD),
                    m.v_w[:, :].rearrange("p (h v) -> p h v", v=HD)[:, :, v:v + 1].to_broadcast([P, H, HD])))
            step(nc.gpsimd.tensor_tensor(m.own_v[:, :], m.v_b_all[:, :], m.same_head[:, :], ALU.mult))
            head = m.same_head[:, :].rearrange("p (h v) -> p h v", v=HD)[:, :, 0]
            step(nc.gpsimd.tensor_tensor(m.own_dec[:, :], m.dec_b_all[:, :], head, ALU.mult))

        @block.tensor
        def _(pe):
            def first_pass(g, qc, i):
                h, qt, kc = i // (TPC * CHUNKS), i // CHUNKS % TPC, i % CHUNKS
                if i == 0 and qc > 0:
                    pe.wait_ge(q_loaded[qc], DMAS_Q * (g + 1))
                elif i == 0 and not (isinstance(g, int) and g == 0):
                    pe.wait_ge(q_loaded[qc], DMAS_Q * g)
                if qc == 0 and i % (TPC * CHUNKS) == 0 and not (isinstance(g, int) and g == 0):
                    pe.wait_ge(k1_loaded[h], DMAS_K * g)
                if i % 2 == 0 and not (isinstance(g, int) and g == 0 and qc == 0 and i < len(S1B)):
                    pe.wait_ge(s1_used, (g * CHUNKS + qc) * PAIRS + (i // 2 - 1))
                queries = q[0:ROWS, qc, h, :].rearrange("r (p t) -> r t p", t=TPC)[:, qt, :]
                mm = nc.tensor.matmul(m.ps[:, S1B[i % 4], :], queries,
                                      k1[:, h, kc * CHUNK:(kc + 1) * CHUNK], start=True, stop=True)
                if i % 2 == 1:
                    mm.then_inc(s1_ready, 1)

            def weigh(g, qc, kt, first=False):
                u = g * CHUNKS + qc
                if qc == 0 and kt % (TILES // 2) == 0:
                    pe.wait_ge(v_loaded[kt // (TILES // 2)], 16 * (g + 1))
                if kt == 0 and not first:
                    pe.wait_ge(out_stored, u)
                pe.wait_ge(exped, u * STEPS + (kt + 1) * GH)
                for h in range(GH):
                    last = nc.tensor.matmul(m.ps[32 * h:32 * h + VC, AVB, :], v[:, kt, h, :],
                                            ex[kt % P_RING][:, h, :], start=(kt == 0), stop=(kt == TILES - 1),
                                            skip_group_check=True)
                last.then_inc(av_done, 1)

            def unit(g, qc, last, first=False):
                u = g * CHUNKS + qc
                after = [(g, qc + 1), (g, qc + 2)]
                after = [(a, b) if b < CHUNKS else (a + 1, b - CHUNKS) for a, b in after]

                def ahead(s):
                    if last and (qc == CHUNKS - 1 or (qc == CHUNKS - 2 and s + LEAD >= STEPS)):
                        return
                    for i in S1_IN[(s + LEAD) % STEPS]:
                        first_pass(*after[(s + LEAD) // STEPS], i)

                def score(s):
                    kt, h = s // GH, s % GH
                    if not (first and s < len(S2B)):
                        pe.wait_ge(exped, u * STEPS + (s - S2_SINCE[s] + 1))
                    nc.tensor.matmul(m.ps[:, S2_BANK[s], :], k2[:, h, kt * P:(kt + 1) * P], q[:, qc, h, :],
                                     start=True, stop=True).then_inc(s2_ready, 1)

                pe.wait_ge(max_loaded, DMAS_M * (u + 1))
                for kt in range(TILES):
                    if qc == 0 and kt % (TILES // 2) == 0:
                        pe.wait_ge(k2_loaded[kt // (TILES // 2)], DMAS_K * (g + 1))
                    s = kt * GH
                    score(s)
                    score(s + 1)
                    ahead(s)
                    score(s + 2)
                    ahead(s + 1)
                    score(s + 3)
                    ahead(s + 2)
                    if kt >= 1:
                        weigh(g, qc, kt - 1, first)
                    elif qc >= 1:
                        weigh(g, qc - 1, TILES - 1)
                    elif not first:
                        weigh(g - 1, CHUNKS - 1, TILES - 1)
                    ahead(s + 3)

            nc.tensor.matmul(m.ps[:, AVB, :], zeros[:, 0:P], zeros[:, :], start=True, stop=True)
            for i in range(STEPS):
                first_pass(0, 0, i)
            for i in range(S1_IN[LEAD].start):
                first_pass(0, 1, i)
            unit(0, 0, False, True)
            for qc in range(1, CHUNKS):
                unit(0, qc, False)
            with pe.Fori(1, GROUPS - 1) as g:
                for qc in range(CHUNKS):
                    unit(g, qc, False)
            for qc in range(CHUNKS):
                unit(GROUPS - 1, qc, True)
            weigh(GROUPS - 1, CHUNKS - 1, TILES - 1)

        @block.scalar
        def _(act):
            def store_out(u):
                act.wait_ge(av_done, (u + 1) * TILES)
                nc.scalar.activation(outs[:, bass.ts(u, 1), :].rearrange("p u t -> p (u t)"), m.ps[:, AVB, :],
                                     ACT.Copy).then_inc(out_stored, 1)

            def unit(g, qc, last, first=False):
                u = g * CHUNKS + qc
                for kt in range(TILES):
                    for h in range(GH):
                        s = kt * GH + h
                        act.wait_ge(s2_ready, u * STEPS + (s + 1))
                        if h == 0 and not (first and kt < P_RING):
                            act.wait_ge(av_done, u * TILES + (kt - P_RING + 1))
                        nc.scalar.activation(ex[kt % P_RING][:, h, :], m.ps[:, S2_BANK[s], :], ACT.Exp).then_inc(exped, 1)
                    if kt == 0 and not first:
                        store_out(u - 1)

            low = 64
            nc.scalar.activation(k2[low:ROWS_M, :, :], own_row[low:ROWS_M, :].unsqueeze(2).to_broadcast([ROWS_M - low, GH, T]),
                                 ACT.Copy).then_inc(ones_stored, 1)
            unit(0, 0, False, True)
            for qc in range(1, CHUNKS):
                unit(0, qc, False)
            with act.Fori(1, GROUPS - 1) as g:
                for qc in range(CHUNKS):
                    unit(g, qc, False)
            for qc in range(CHUNKS):
                unit(GROUPS - 1, qc, True)
            store_out(UNITS - 1)

        @block.vector
        def _(dve):
            def maxima(u, first=False):
                for i in range(PAIRS):
                    dve.wait_ge(s1_ready, u * PAIRS + (i + 1))
                    h, qt, kc = 2 * i // (TPC * CHUNKS), 2 * i // CHUNKS % TPC, i % (CHUNKS // 2)
                    nc.vector.reduce_max(mx[:, h, qt, kc:kc + 1], m.ps[:, 2 * (i % 2):2 * (i % 2) + 2, :], AX.XY)\
                        .then_inc(s1_used, 1)
                dve.wait_ge(s1_used, (u + 1) * PAIRS)
                nc.vector.tensor_reduce(neg[:, :, :], mx[:, :, :, :], axis=AX.X, op=ALU.max, negate=True)\
                    .then_inc(max_steps, 1)
                dve.wait_ge(max_steps, u * 6 + 1)
                out = neg_part[:, :, 0:PARTS * GH].rearrange("p t (i h) -> p h t i", h=GH)
                nc.vector.tensor_copy(out[:, :, :, 0], neg[:, :, :]).then_inc(max_steps, 1)
                dve.wait_ge(max_steps, u * 6 + 2)
                nc.vector.tensor_tensor(neg_rest[:, 0, :, :], neg[:, :, :], out[:, :, :, 0], ALU.subtract).then_inc(max_steps, 1)
                dve.wait_ge(max_steps, u * 6 + 3)
                nc.vector.tensor_copy(out[:, :, :, 1], neg_rest[:, 0, :, :]).then_inc(max_steps, 1)
                dve.wait_ge(max_steps, u * 6 + 4)
                nc.vector.tensor_tensor(neg_rest[:, 1, :, :], neg_rest[:, 0, :, :], out[:, :, :, 1], ALU.subtract)\
                    .then_inc(max_steps, 1)
                dve.wait_ge(max_steps, u * 6 + 5)
                nc.vector.tensor_copy(out[:, :, :, 2], neg_rest[:, 1, :, :]).then_inc(max_steps, 1)
                dve.wait_ge(max_steps, u * 6 + 6)
                if not first:
                    dve.wait_ge(max_loaded, DMAS_M * u)
                nc.vector.transpose(neg_turned[:, :, :].rearrange("p j t -> p t j"), neg_part[:, :, :]).then_inc(max_turned, 1)
                dve.wait_ge(max_turned, u + 1)

            maxima(0, True)
            with dve.Fori(1, UNITS) as u:
                maxima(u)

    m.stage()
    out_turned, inv_ready, att_ready, att_turned = m.sem("out_turned"), m.sem("inv_ready"), m.sem("att_ready"), m.sem("att_turned")
    attT_ready, projected, x_updated = m.sem("attT_ready"), m.sem("projected"), m.sem("x_updated")
    with ExitStack() as stack:
        inv = m.sb("inv_den", [P, GROUPS, TPC, GH], stack=stack)
        att = m.sb("att", [P, TILES, D], stack=stack)
        attT = m.sb("attT", [P, T], stack=stack)
        ahead = Prepare(m, stack, m.gateT, True, 5, 7)
        block = stack.enter_context(nc.Block())

        @block.tensor
        def _(pe):
            def turn_out(qc):
                if qc >= 1:
                    pe.wait_ge(att_ready, qc * GROUPS)
                for g in range(GROUPS):
                    for j in range(TPC):
                        last = nc.tensor.transpose(m.ps[:, g, j * P:(j + 1) * P],
                                                   outs[:, g * CHUNKS + qc, j * P:(j + 1) * P], m.ident[:, :])
                last.then_inc(out_turned, 1)

            turn_out(0)
            for qc in range(CHUNKS):
                if qc + 1 < CHUNKS:
                    turn_out(qc + 1)
                else:
                    pe.wait_ge(att_ready, CHUNKS * GROUPS)
                if qc >= 1:
                    pe.wait_ge(attT_ready, qc)
                for j in range(TPC):
                    last = nc.tensor.transpose(m.ps[:, 4, j * P:(j + 1) * P], att[:, qc * TPC + j, :], m.ident[:, :])
                last.then_inc(att_turned, 1)
                if qc == 2:
                    ahead.transpose(pe, 0)
                if qc == 3:
                    ahead.logits(pe, 0)
                pe.wait_ge(attT_ready, qc + 1)
                if qc >= 1:
                    pe.wait_ge(x_updated, qc)
                for j in range(TPC):
                    t = qc * TPC + j
                    last = nc.tensor.matmul(m.ps[:, 6, j * P:(j + 1) * P], attT[:, t * P:(t + 1) * P],
                                            m.projT[:, 0, :], start=True, stop=True)
                last.then_inc(projected, 1)
            ahead.transpose_gates(pe, 0)

        @block.gpsimd
        def _(pool):
            ahead.rstds(pool, 0)

        @block.scalar
        def _(act):
            for qc in range(CHUNKS):
                act.wait_ge(att_turned, qc + 1)
                nc.scalar.activation(attT[:, qc * CHUNK:(qc + 1) * CHUNK], m.ps[:, 4, :], ACT.Copy).then_inc(attT_ready, 1)
                if qc == 1:
                    ahead.squares(act, 0)
                if qc == 2:
                    ahead.store_xT(act, 0)
            ahead.exps(act, 0)

        @block.vector
        def _(dve):
            def divide(qc):
                dve.wait_ge(out_turned, qc + 1)
                turned = m.ps[:, 0:GROUPS, :].rearrange("p g (t h r) -> p g t h r", h=GH, r=32)
                if qc >= 1:
                    dve.wait_ge(att_ready, qc * GROUPS)
                nc.vector.reciprocal(inv[:, :, :, :], turned[:, :, :, :, HD]).then_inc(inv_ready, 1)
                dve.wait_ge(inv_ready, qc + 1)
                for g in range(GROUPS):
                    dst = att[:, qc * TPC:(qc + 1) * TPC, g * GH * HD:(g + 1) * GH * HD]
                    nc.vector.tensor_tensor(dst.rearrange("p t (h e) -> p t h e", e=HD), turned[:, g, :, :, 0:HD],
                                            inv[:, g, :, :].unsqueeze(3).to_broadcast([P, TPC, GH, HD]), ALU.mult)\
                        .then_inc(att_ready, 1)

            divide(0)
            for qc in range(CHUNKS):
                if qc + 1 < CHUNKS:
                    divide(qc + 1)
                dve.wait_ge(projected, qc + 1)
                x_t = m.X[:, qc * TPC:(qc + 1) * TPC, :]
                nc.vector.tensor_tensor(x_t, m.ps[:, 6, :].rearrange("p (t d) -> p t d", d=D), x_t, ALU.add)\
                    .then_inc(x_updated, 1)
                if qc == 0:
                    dve.wait_ge(x_updated, 1)
                    ahead.sums(dve, 0)
                if qc == 1:
                    ahead.variances(dve, 0)
                    ahead.normalise(dve, 0)
                if qc == 2:
                    ahead.shift(dve, 0)
                    ahead.compare(dve, 0)
            ahead.rank_gates(dve, 0)
            ahead.pack(dve, 0)
            ahead.store_gates(dve, 0)
    att_stack.close()
    kv_stack.close()


def decay_attention(m):
    nc = m.nc
    tag = m.stage()
    proj, clipped, exped = m.sem("proj"), m.sem("clipped"), m.sem("exped")
    steps, feat_ready = m.sem("feat_steps"), m.sem("feat_ready")
    with ExitStack() as outer:
        phi = m.sb("phi" + tag, [P, 2, T], stack=outer)
        lam = m.sb("lam" + tag, [P, T], stack=outer)
        with ExitStack() as stack:
            z = m.sb("z" + tag, [P, 2, CHUNK], stack=stack)
            low = m.sb("low" + tag, [P, 2, CHUNK], stack=stack)
            z_ready, bias_ready = m.sem("z_ready"), m.sem("bias_ready")
            elow = m.sb("elow" + tag, [P, 2, CHUNK], stack=stack)
            one_plus = m.sb("one_plus" + tag, [P, CHUNK], stack=stack)
            sig = m.sb("sig" + tag, [P, CHUNK], stack=stack)
            jobs = [(s, c) for c in range(CHUNKS) for s in range(3)]
            weights = [m.q_w, m.k_w, m.dec_rep]
            outer_norm = Norm(m, stack, "outer", m.X, m.xn, first=CHUNKS - 1)
            inner_norm = Norm(m, stack, "inner", m.xn, None, [6, 7], m.ln[:, 0:1], m.ln[:, 1:2])
            block = stack.enter_context(nc.Block())

            @block.gpsimd
            def _(pool):
                outer_norm.rstds(pool, CHUNKS - 1)
                for c in range(CHUNKS):
                    inner_norm.rstds(pool, c)

            @block.tensor
            def _(pe):
                inner_norm.transpose(pe, 0)
                inner_norm.transpose(pe, 1)
                for n, (s, c) in enumerate(jobs):
                    if s == 0:
                        if 1 <= c < CHUNKS - 1:
                            inner_norm.transpose(pe, c + 1)
                        pe.wait_ge(inner_norm.s_xT_ready, c + 1)
                    if n >= 4:
                        pe.wait_ge(feat_ready, n - 3)
                    nc.tensor.matmul(m.ps[:, n % 4, :], weights[s][:, :], m.xT[:, c * CHUNK:(c + 1) * CHUNK],
                                     start=True, stop=True).then_inc(proj, 1)

            @block.scalar
            def _(act):
                def features(c):
                    for s in range(3):
                        n = 3 * c + s
                        act.wait_ge(proj, n + 1)
                        if n >= 2:
                            act.wait_ge(feat_ready, n - 1)
                        if s < 2:
                            nc.scalar.activation(z[:, n % 2, :], m.ps[:, n % 4, :], ACT.Identity,
                                                 bias=m.qk1_bias[:, s:s + 1]).then_inc(z_ready, 1)
                            act.wait_ge(clipped, 2 * c + s + 1)
                            nc.scalar.activation(elow[:, n % 2, :], low[:, n % 2, :], ACT.Exp).then_inc(exped, 1)
                        else:
                            nc.scalar.activation(elow[:, n % 2, :], m.ps[:, n % 4, :], ACT.Exp, bias=m.neg_dec_b[:, 0:1],
                                                 scale=-1.0).then_inc(exped, 1)

                act.wait_ge(bias_ready, 1)
                outer_norm.squares(act, CHUNKS - 1)
                for c in range(CHUNKS):
                    inner_norm.squares(act, c)
                    if c >= 2:
                        inner_norm.store_xT(act, c - 2)
                for c in range(CHUNKS):
                    if c + 2 < CHUNKS:
                        inner_norm.store_xT(act, c + 2)
                    features(c)

            @block.vector
            def _(dve):
                step = Chain(dve, steps)

                def feature(s, c):
                    n = 3 * c + s
                    t = slice(c * CHUNK, (c + 1) * CHUNK)
                    if s < 2:
                        dve.wait_ge(z_ready, 2 * c + s + 1)
                        nc.vector.tensor_scalar(low[:, n % 2, :], z[:, n % 2, :], 0.0, None, ALU.min).then_inc(clipped, 1)
                        dve.wait_ge(exped, n + 1)
                        nc.vector.scalar_tensor_tensor(out=phi[:, s, t], in0=z[:, n % 2, :], scalar=0.0,
                                                       in1=elow[:, n % 2, :], op0=ALU.max, op1=ALU.add)\
                            .then_inc(feat_ready, 1)
                    else:
                        dve.wait_ge(exped, n + 1)
                        step(nc.vector.tensor_scalar(one_plus[:, :], elow[:, n % 2, :], 1.0, None, ALU.add))
                        step(nc.vector.reciprocal(sig[:, :], one_plus[:, :]))
                        nc.vector.tensor_scalar(lam[:, t], sig[:, :], LAM_MIN, None, ALU.max).then_inc(feat_ready, 1)
                    dve.wait_ge(feat_ready, n + 1)

                nc.vector.reduce_sum(m.v1_bias[:, :], m.own_v[:, :].rearrange("p (h v) -> p v h", v=HD), AX.X)
                nc.vector.tensor_reduce(m.neg_dec_b[:, :], m.own_dec[:, :], axis=AX.X, op=ALU.add, negate=True)\
                    .then_inc(bias_ready, 1)
                outer_norm.sums(step, CHUNKS - 1)
                inner_norm.sums(step, 0)
                outer_norm.variances(step, CHUNKS - 1)
                inner_norm.variances(step, 0)
                outer_norm.normalise(dve, CHUNKS - 1)
                inner_norm.normalise(dve, 0)
                for c in range(1, CHUNKS):
                    if c == CHUNKS - 1:
                        dve.wait_ge(outer_norm.s_normed, 1)
                    inner_norm.sums(step, c)
                    if c == CHUNKS - 1:
                        feature(0, 0)
                    inner_norm.variances(step, c)
                    if c == CHUNKS - 1:
                        feature(1, 0)
                    inner_norm.normalise(dve, c)
                for s, c in [(s, c) for c in range(CHUNKS) for s in range(3)][2:]:
                    feature(s, c)

        m.stage()
        v_ready, kv_ready, fwd_ready, bwd_ready = m.sem("v_ready"), m.sem("kv_ready"), m.sem("fwd_ready"), m.sem("bwd_ready")
        both_ready, qs_ready, summed = m.sem("both_ready"), m.sem("qs_ready"), m.sem("summed")
        edge, attT_ready, o_ready, bias_added = m.sem("edge"), m.sem("attT_ready"), m.sem("o_ready"), m.sem("bias_added")
        with ExitStack() as stack:
            kv = m.sb("kv" + tag, [P, 2, T], stack=stack)
            fwd = m.sb("fwd" + tag, [P, 2, T], stack=stack)
            bwd = m.sb("bwd" + tag, [P, 2, T], stack=stack)
            both = fwd
            qs = m.sb("qs" + tag, [P, 2, T], stack=stack)
            inv = m.sb("inv" + tag, [P, T], stack=stack)
            den_read, inv_ready = m.sem("den_read"), m.sem("inv_ready")
            attT = m.sb("attT" + tag, [P, T], stack=stack)
            den = attT
            block = stack.enter_context(nc.Block())

            order = [HD] + list(range(HD))

            def weigh(dve, n):
                dve.wait_ge(both_ready, n + 1)
                if n >= 2:
                    dve.wait_ge(summed, n - 1)
                nc.vector.tensor_tensor(qs[:, n % 2, :], phi[:, 0, :], both[:, n % 2, :], ALU.mult).then_inc(qs_ready, 1)

            @block.tensor
            def _(pe):
                def values_of(v):
                    for c in range(CHUNKS):
                        if v >= 1:
                            pe.wait_ge(kv_ready, (v - 1) * CHUNKS + c + 1)
                        nc.tensor.matmul(m.ps[:, 4 + c, :], m.v_rep[:, v, :], m.xT[:, c * CHUNK:(c + 1) * CHUNK],
                                         start=True, stop=True).then_inc(v_ready, 1)

                values_of(0)
                values_of(1)
                for n, v in enumerate(order):
                    if n >= 1 and v + 2 < HD:
                        values_of(v + 2)
                    pe.wait_ge(qs_ready, n + 1)
                    if n == 1:
                        pe.wait_ge(den_read, 1)
                    for c in range(CHUNKS):
                        weighed = qs[:, n % 2, c * CHUNK:(c + 1) * CHUNK]
                        if v == HD:
                            last = nc.tensor.matmul(m.ps[:, c, :], m.same_head[:, :], weighed, start=True, stop=True)
                        else:
                            last = nc.tensor.matmul(m.ps[:, c, :], m.pick[:, v, :], weighed, start=(v == 0),
                                                    stop=(v == HD - 1))
                    last.then_inc(summed, 1)
                for c in range(CHUNKS):
                    pe.wait_ge(attT_ready, c + 1)
                    for j in range(TPC):
                        t = c * TPC + j
                        last = nc.tensor.matmul(m.ps[:, c, j * P:(j + 1) * P], attT[:, t * P:(t + 1) * P], m.o_w[:, :],
                                                start=True, stop=True)
                    last.then_inc(o_ready, 1)

            @block.vector
            def _(dve):
                nc.vector.memset(bwd[:, 0, T - 1:T], 0.0).then_inc(edge, 1)
                nc.vector.memset(bwd[:, 1, T - 1:T], 0.0).then_inc(edge, 1)
                for n, v in enumerate(order):
                    if v < HD:
                        for c in range(CHUNKS):
                            t = slice(c * CHUNK, (c + 1) * CHUNK)
                            dve.wait_ge(v_ready, v * CHUNKS + c + 1)
                            nc.vector.scalar_tensor_tensor(out=kv[:, v % 2, t], in0=m.ps[:, 4 + c, :], scalar=m.v1_bias[:, v:v + 1],
                                                           in1=phi[:, 1, t], op0=ALU.add, op1=ALU.mult).then_inc(kv_ready, 1)
                        dve.wait_ge(kv_ready, (v + 1) * CHUNKS)
                        src = kv[:, v % 2, :]
                    else:
                        src = phi[:, 1, :]
                    if n >= 2:
                        dve.wait_ge(qs_ready, n - 1)
                    nc.vector.tensor_tensor_scan(fwd[:, n % 2, :], lam[:, :], src, 0.0, ALU.mult, ALU.add).then_inc(fwd_ready, 1)
                    nc.vector.tensor_tensor_scan(bwd[:, n % 2, 0:T - 1][:, ::-1], src[:, 1:T][:, ::-1], lam[:, 1:T][:, ::-1],
                                                 0.0, ALU.add, ALU.mult).then_inc(bwd_ready, 1)
                    if n >= 1:
                        weigh(dve, n - 1)
                    if n == 2:
                        dve.wait_ge(summed, 1)
                        nc.vector.tensor_scalar(den[:, :], m.ps[:, 0:CHUNKS, :].rearrange("p c t -> p (c t)"), DEN_EPS, None,
                                                ALU.max).then_inc(den_read, 1)
                        dve.wait_ge(den_read, 1)
                        nc.vector.reciprocal(inv[:, :], den[:, :]).then_inc(inv_ready, 1)
                weigh(dve, VC - 1)
                dve.wait_ge(inv_ready, 1)
                dve.wait_ge(summed, VC)
                for c in range(CHUNKS):
                    t = slice(c * CHUNK, (c + 1) * CHUNK)
                    nc.vector.tensor_tensor(attT[:, t], m.ps[:, c, :], inv[:, t], ALU.mult).then_inc(attT_ready, 1)
                dve.wait_ge(bias_added, 1)
                for c in range(CHUNKS):
                    dve.wait_ge(o_ready, c + 1)
                    x_t = m.xn[:, c * TPC:(c + 1) * TPC, :]
                    nc.vector.tensor_tensor(x_t, m.ps[:, c, :].rearrange("p (t d) -> p t d", d=D), x_t, ALU.add)

            @block.gpsimd
            def _(pool):
                nc.gpsimd.tensor_tensor(m.xn[:, :, :], m.xn[:, :, :], m.o_bias[:, :].unsqueeze(1).to_broadcast([P, TILES, D]),
                                        ALU.add).then_inc(bias_added, 1)
                pool.wait_ge(edge, 2)
                for n in range(VC):
                    pool.wait_ge(fwd_ready, n + 1)
                    pool.wait_ge(bwd_ready, n + 1)
                    nc.gpsimd.tensor_tensor(both[:, n % 2, :], fwd[:, n % 2, :], bwd[:, n % 2, :], ALU.add).then_inc(both_ready, 1)


def gelu_ffn(m):
    nc = m.nc
    tag = m.stage()
    a_ready, hid_ready, y_ready, res_ready, yb_ready, x_ready = (m.sem("a_ready"), m.sem("hid_ready"), m.sem("y_ready"),
                                                                 m.sem("res_ready"), m.sem("yb_ready"), m.sem("x_ready"))
    with ExitStack() as stack:
        hid = m.sb("fhid" + tag, [P, 2, FFN, CHUNK], stack=stack)
        res = m.sb("fres" + tag, [P, 2, TPC, D], stack=stack)
        yb = m.sb("fyb" + tag, [P, 2, TPC, D], stack=stack)
        steps = m.sem("steps")
        norm = Norm(m, stack, "norm", m.xn, None, [6, 7], m.ln[:, 2:3], m.ln[:, 3:4])
        ahead = Prepare(m, stack, m.router, False, 6, 7)
        block = stack.enter_context(nc.Block())

        @block.gpsimd
        def _(pool):
            for c in range(CHUNKS):
                norm.rstds(pool, c)
            ahead.rstds(pool, 0)

        @block.tensor
        def _(pe):
            def up(c):
                pe.wait_ge(norm.s_xT_ready, c + 1)
                for i in range(FFN):
                    if c >= 1:
                        pe.wait_ge(hid_ready, (c - 1) * FFN + i + 1)
                    nc.tensor.matmul(m.ps[:, i, :], m.f1_w[:, i * P:(i + 1) * P], m.xT[:, c * CHUNK:(c + 1) * CHUNK],
                                     start=True, stop=True).then_inc(a_ready, 1)

            norm.transpose(pe, 0)
            norm.transpose(pe, 1)
            up(0)
            norm.transpose(pe, 2)
            for c in range(CHUNKS):
                if c + 1 < CHUNKS:
                    up(c + 1)
                if c + 3 < CHUNKS:
                    norm.transpose(pe, c + 3)
                if c == CHUNKS - 2:
                    ahead.transpose(pe, 0)
                pe.wait_ge(hid_ready, (c + 1) * FFN)
                if c >= 2:
                    pe.wait_ge(yb_ready, c - 1)
                for j in range(TPC):
                    for i in range(FFN):
                        last = nc.tensor.matmul(m.ps[:, 4 + c % 2, j * P:(j + 1) * P], hid[:, c % 2, i, j * P:(j + 1) * P],
                                                m.f2_w[:, i, :], start=(i == 0), stop=(i == FFN - 1))
                last.then_inc(y_ready, 1)
                if c == CHUNKS - 2:
                    ahead.logits(pe, 0)

        @block.scalar
        def _(act):
            norm.squares(act, 0)
            norm.squares(act, 1)
            norm.store_xT(act, 0)
            norm.squares(act, 2)
            norm.squares(act, 3)
            norm.store_xT(act, 1)
            for c in range(CHUNKS):
                if 1 <= c < CHUNKS - 1:
                    norm.store_xT(act, c + 1)
                for i in range(FFN):
                    act.wait_ge(a_ready, c * FFN + i + 1)
                    if c >= 2:
                        act.wait_ge(y_ready, c - 1)
                    nc.scalar.activation(hid[:, c % 2, i, :], m.ps[:, i, :], ACT.Gelu, bias=m.f1_b[:, i:i + 1]).then_inc(hid_ready, 1)
                if c == 1:
                    ahead.squares(act, 0)
                if c == CHUNKS - 2:
                    ahead.store_xT(act, 0)
            ahead.exps(act, 0)

        @block.vector
        def _(dve):
            step = Chain(dve, steps)
            norm.all_chunks(step)
            for c in range(CHUNKS):
                t = slice(c * TPC, (c + 1) * TPC)
                if c >= 2:
                    dve.wait_ge(x_ready, c - 1)
                nc.vector.tensor_tensor(res[:, c % 2, :, :], m.X[:, t, :], m.xn[:, t, :], ALU.add).then_inc(res_ready, 1)
                dve.wait_ge(y_ready, c + 1)
                nc.vector.tensor_tensor(yb[:, c % 2, :, :], m.ps[:, 4 + c % 2, :].rearrange("p (t d) -> p t d", d=D),
                                        m.f2_bias[:, :].unsqueeze(1).to_broadcast([P, TPC, D]), ALU.add).then_inc(yb_ready, 1)
                dve.wait_ge(yb_ready, c + 1)
                dve.wait_ge(res_ready, c + 1)
                nc.vector.tensor_tensor(m.X[:, t, :], res[:, c % 2, :, :], yb[:, c % 2, :, :], ALU.add).then_inc(x_ready, 1)
                if c == 0:
                    dve.wait_ge(x_ready, 1)
                    ahead.sums(dve, 0)
                if c == 1:
                    ahead.variances(dve, 0)
                    ahead.normalise(dve, 0)
                if c == CHUNKS - 2:
                    ahead.shift(dve, 0)
                    ahead.compare(dve, 0)
                    ahead.rank_gates(dve, 0)
                    ahead.pack(dve, 0)


def macaron(nc: bass.Bass, w, out):
    with ExitStack() as stack:
        m = Machine(nc, stack)
        m.ps = stack.enter_context(nc.psum_tensor("ps", [P, 8, CHUNK], F32))
        m.X = m.sb("X", [P, TILES, D])
        m.xn = m.sb("xn", [P, TILES, D])
        m.xT = m.sb("xT", [P, T])
        m.ident = m.sb("ident", [P, P])
        m.identb = m.sb("identb", [P, P], BF16)
        m.neg_half = m.sb("neg_half", [P, TPC])
        m.euler = m.sb("euler", [P, TPC * E])
        m.below = m.sb("below", [P, E, E])
        m.sel_gate = m.sb("sel_gate", [P, E, P], BF16)
        m.sel_mask = m.sb("sel_mask", [P, E, P], BF16)
        m.gT = m.sb("gT", [P, T], BF16)
        m.pick = m.sb("pick", [P, HD, P])
        m.same_head = m.sb("same_head", [P, P])
        m.cw = m.sb("cw", [P, TILES, E + 1])
        counts = [E, E, E, SH0, SH0, SH0, 3, 1]
        m.wT = m.sb("wT", [P, sum(counts), D])
        at = [sum(counts[:i]) for i in range(len(counts) + 1)]
        m.w1T, m.w3T, m.w2T, m.sw1T, m.sw2T, m.sw3T, m.qkvT, m.projT = (
            m.wT[:, at[i]:at[i + 1], :] for i in range(len(counts)))
        m.gateT = m.sb("gateT", [P, E])
        m.biases = [(w["L0_ffn_b1"], E), (w["L0_ffn_b2"], E), (w["L0_ffn_b3"], E),
                    (w["L0_attn_qkv_b"][0:2 * D].rearrange("(s p) -> s p", p=P), 2),
                    (w["L1_attn_f1_b"].rearrange("(i p) -> i p", p=P), FFN)]
        m.biases += [(w[n].unsqueeze(0), 1) for n in ("L1_attn_q_b", "L1_attn_k_b", "L1_attn_ln1_w", "L1_attn_ln1_b",
                                                      "L1_attn_ln2_w", "L1_attn_ln2_b")]
        m.bias_rows = sum(n for _, n in m.biases)
        m.biasT = m.sb("biasT", [P, m.bias_rows])
        ends = [sum(n for _, n in m.biases[:i + 1]) for i in range(len(m.biases))]
        m.b1, m.b2, m.b3, m.qk_bias_raw, m.f1_b = (m.biasT[:, e - n:e] for e, (_, n) in zip(ends, m.biases[:5]))
        m.qk1_bias = m.biasT[:, ends[4]:ends[4] + 2]
        m.ln = m.biasT[:, ends[4] + 2:ends[4] + 6]
        m.qk_bias = m.sb("qk_bias", [P, 2])
        m.v_bias = m.sb("v_bias", [P, D])
        m.proj_bias = m.sb("proj_bias", [P, D])
        m.router = m.sb("router", [P, E])
        m.ew1 = m.sb("ew1", [P, E + 1, HID1 * P])
        m.ew3 = m.sb("ew3", [P, E + 1, HID1 * P])
        m.ew2 = m.sb("ew2", [P, E + 1, HID1, D])
        m.q_w, m.k_w, m.v_w, m.o_w = (m.sb(n, [P, D]) for n in ("q_w", "k_w", "v_w", "o_w"))
        m.dec_w = m.sb("dec_w", [P, H])
        m.dec_rep = m.sb("dec_rep", [P, D])
        m.v_rep = m.sb("v_rep", [P, HD, D])
        m.f1_w = m.sb("f1_w", [P, FFN * P])
        m.f2_w = m.sb("f2_w", [P, FFN, D])
        m.dec_b_all = m.sb("dec_b_all", [P, H])
        m.v_b_all = m.sb("v_b_all", [P, D])
        m.own_v, m.own_dec = m.sb("own_v", [P, D]), m.sb("own_dec", [P, H])
        m.neg_dec_b = m.sb("neg_dec_b", [P, 1])
        m.v1_bias = m.sb("v1_bias", [P, HD])
        m.o_bias, m.f2_bias = m.sb("o_bias", [P, D]), m.sb("f2_bias", [P, D])

        def on_all(v):
            return v.unsqueeze(0).to_broadcast([P, v.shape[0]])

        m.loads = [
            (m.v_bias[:, :], on_all(w["L0_attn_qkv_b"][2 * D:3 * D])),
            (m.proj_bias[:, :], on_all(w["L0_attn_proj_b"])),
            (m.router[:, :], w["L1_ffn_w_router"]),
            (m.ew1[:, 0:E, :], w["L1_ffn_w1"].rearrange("e d h -> d e h")),
            (m.ew1[:, E, :], w["L1_ffn_sw1"]),
            (m.ew3[:, 0:E, :], w["L1_ffn_w3"].rearrange("e d h -> d e h")),
            (m.ew3[:, E, :], w["L1_ffn_sw3"]),
            (m.ew2[:, 0:E, :, :].rearrange("p e i d -> p (e i) d"), w["L1_ffn_w2"].rearrange("e (i p) d -> p (e i) d", p=P)),
            (m.ew2[:, E, :, :], w["L1_ffn_sw2"].rearrange("(i p) d -> p i d", p=P)),
            (m.q_w[:, :], w["L1_attn_q_w"]), (m.k_w[:, :], w["L1_attn_k_w"]),
            (m.v_w[:, :], w["L1_attn_v_w"]), (m.o_w[:, :], w["L1_attn_o_w"]),
            (m.dec_w[:, :], w["L1_attn_dec_w"]),
            (m.f1_w[:, :], w["L1_attn_f1_w"]),
            (m.f2_w[:, :, :], w["L1_attn_f2_w"].rearrange("(i p) d -> p i d", p=P)),
            (m.o_bias[:, :], on_all(w["L1_attn_o_b"])), (m.f2_bias[:, :], on_all(w["L1_attn_f2_b"])),
            (m.dec_b_all[:, :], on_all(w["L1_attn_dec_b"])), (m.v_b_all[:, :], on_all(w["L1_attn_v_b"])),
        ]

        setup(m, w)
        moe0(m, m.loads)
        softmax_attention(m)
        moe0(m, then_moe1=True)
        moe1(m, then_norm=True)
        decay_attention(m)
        gelu_ffn(m)
        moe1(m, out)


_INS = ['L0_attn_x', 'L0_attn_qkv_w', 'L0_attn_qkv_b', 'L0_attn_proj_w', 'L0_attn_proj_b', 'L0_ffn_gate_w', 'L0_ffn_w1',
        'L0_ffn_b1', 'L0_ffn_w2', 'L0_ffn_b2', 'L0_ffn_w3', 'L0_ffn_b3', 'L0_ffn_sw1', 'L0_ffn_sw2', 'L0_ffn_sw3',
        'L1_attn_q_w', 'L1_attn_q_b', 'L1_attn_k_w', 'L1_attn_k_b', 'L1_attn_v_w', 'L1_attn_v_b', 'L1_attn_o_w',
        'L1_attn_o_b', 'L1_attn_ln1_w', 'L1_attn_ln1_b', 'L1_attn_ln2_w', 'L1_attn_ln2_b', 'L1_attn_dec_w',
        'L1_attn_dec_b', 'L1_attn_f1_w', 'L1_attn_f1_b', 'L1_attn_f2_w', 'L1_attn_f2_b', 'L1_ffn_w_router', 'L1_ffn_w1',
        'L1_ffn_w3', 'L1_ffn_w2', 'L1_ffn_sw1', 'L1_ffn_sw3', 'L1_ffn_sw2']
_OUTS = [((1, T, D), 'float32')]


def kernel(**inputs):
    import numpy as _np
    import concourse.bacc as _bacc
    from concourse import mybir as _mybir
    from concourse.bass_utils import run_bass_kernel_spmd as _run

    nc = _bacc.Bacc("TRN2", target_bir_lowering=False, num_devices=1)
    arrays, args = {}, {}
    for name in _INS:
        a = _np.ascontiguousarray(inputs[name])
        arrays[f"in_{name}_dram"] = a
        args[name] = nc.dram_tensor(f"in_{name}_dram", a.shape, _mybir.dt.from_np(a.dtype), kind="ExternalInput").ap()
    shape, dtype = _OUTS[0]
    out = nc.dram_tensor("out_0_dram", shape, _mybir.dt.from_np(_np.dtype(dtype)), kind="ExternalOutput").ap()
    macaron(nc, args, out)
    r = _run(nc, [arrays], core_ids=[0])
    return r.results[0]["out_0_dram"]
```
